# Optimizing a Trainium2 kernel written in Bass

```python
import numpy as np
import jax
import jax.numpy as jnp

def _softmax(x, axis=-1):
    return jax.nn.softmax(x, axis=axis)

def _gelu(x):
    return jax.nn.gelu(x, approximate=True)

def _silu(x):
    return jax.nn.silu(x)

def _sigmoid(x):
    return jax.nn.sigmoid(x)

def _layernorm(x, axis=-1, eps=1e-05):
    m = jnp.mean(x, axis=axis, keepdims=True)
    v = jnp.var(x, axis=axis, keepdims=True)
    return (x - m) / jnp.sqrt(v + eps)

def _scatter_add(tgt, idx, src, axis=0):
    return tgt.at[idx].add(src)

def _segment_sum(src, seg, n):
    return jax.ops.segment_sum(src, seg, n)
kernel_name = 'mk_perceiver_d1_seqx_r2_e47ec9'

def setup_inputs(seed: int=0):
    np.random.seed(seed)
    _w = jnp.asarray

    def _rec_inputs():
        import jax
        import jax.numpy as jnp
        _rk = jax.random.key(seed)
        x = -0.0003929 + 0.9999 * jax.random.normal(jax.random.fold_in(_rk, 1), (128, 32, 512), jnp.float32)
        _lenS = 32 - jax.random.randint(jax.random.fold_in(_rk, 7), (128,), 0, max(1, 32 // 4) + 1, jnp.int32)
        _lenS2 = 257 - jax.random.randint(jax.random.fold_in(_rk, 8), (128,), 0, max(1, 257 // 4) + 1, jnp.int32)
        _ctx_512P = jax.random.normal(jax.random.fold_in(_rk, 11), (128, 16, 256), jnp.float32)
        _ctx_512c = jax.random.dirichlet(jax.random.fold_in(_rk, 511), 0.3 * jnp.ones((16,), jnp.float32), (128, 257))
        _ctx_512t = jnp.einsum('bsk,bkd->bsd', _ctx_512c, _ctx_512P)
        _ctx_512t = _ctx_512t * jax.lax.rsqrt(jnp.mean(jnp.square(_ctx_512t)) + 1e-12) * 0.953939
        ctx_512 = -1.39393e-06 + 0.999914 * (_ctx_512t + 0.3 * jax.random.normal(jax.random.fold_in(_rk, 611), (128, 257, 256), jnp.float32))
        return (x, ctx_512)
    x, ctx_512 = _rec_inputs()

    def _L0_xattn_setup():
        import jax, jax.numpy as jnp
        import numpy as np
        HEADS = 16
        D_MODEL = 512
        IMG_MODEL = 256
        D_K = D_MODEL // HEADS
        key = jax.random.key(seed)
        ks = jax.random.split(key, 12)
        B, LQ, LKV = (8, 1024, 512)
        s_dm = 1.0 / np.sqrt(D_MODEL)
        s_im = 1.0 / np.sqrt(IMG_MODEL)
        return {'q': jax.random.normal(ks[0], (B, LQ, D_MODEL), jnp.float32), 'k': jax.random.normal(ks[1], (B, LKV, IMG_MODEL), jnp.float32), 'v': jax.random.normal(ks[2], (B, LKV, IMG_MODEL), jnp.float32), 'Wq': jax.random.normal(ks[3], (D_MODEL, D_MODEL), jnp.float32) * s_dm, 'bq': jnp.zeros((D_MODEL,), jnp.float32), 'Wk': jax.random.normal(ks[4], (IMG_MODEL, D_MODEL), jnp.float32) * s_im, 'bk': jnp.zeros((D_MODEL,), jnp.float32), 'Wv': jax.random.normal(ks[5], (IMG_MODEL, D_MODEL), jnp.float32) * s_im, 'bv': jnp.zeros((D_MODEL,), jnp.float32), 'Wo': jax.random.normal(ks[6], (D_MODEL, D_MODEL), jnp.float32) * s_dm, 'bo': jnp.zeros((D_MODEL,), jnp.float32)}
    _L0_xattn_all = _L0_xattn_setup()
    _L0_xattn_in = {k: v for k, v in _L0_xattn_all.items() if k in ('Wq', 'bq', 'Wk', 'bk', 'Wv', 'bv', 'Wo', 'bo')}
    del _L0_xattn_all

    def _L0_attn_setup():
        import jax, jax.numpy as jnp
        import numpy as np
        DIM = 512
        NUM_HEADS = 16
        HEAD_DIM = DIM // NUM_HEADS
        SCALE = HEAD_DIM ** (-0.5)
        key = jax.random.key(seed)
        ks = jax.random.split(key, 5)
        x = jax.random.normal(ks[0], (4, 1024, DIM), dtype=jnp.float32)
        w_qkv = jax.random.normal(ks[1], (DIM, 3 * DIM), dtype=jnp.float32) * DIM ** (-0.5)
        b_qkv = jax.random.normal(ks[2], (3 * DIM,), dtype=jnp.float32) * 0.02
        w_proj = jax.random.normal(ks[3], (DIM, DIM), dtype=jnp.float32) * DIM ** (-0.5)
        b_proj = jax.random.normal(ks[4], (DIM,), dtype=jnp.float32) * 0.02
        return {'x': x, 'w_qkv': w_qkv, 'b_qkv': b_qkv, 'w_proj': w_proj, 'b_proj': b_proj}
    _L0_attn_all = _L0_attn_setup()
    _L0_attn_in = {k: v for k, v in _L0_attn_all.items() if k in ('w_qkv', 'b_qkv', 'w_proj', 'b_proj')}
    del _L0_attn_all

    def _L0_ffn_setup():
        import jax, jax.numpy as jnp
        import numpy as np
        B, S, D, H, E = (4, 1024, 512, 16, 4)
        key = jax.random.key(seed)
        ks = jax.random.split(key, 8)
        w = lambda k, shape: jax.random.normal(k, shape, jnp.float32) * 0.02
        return {'x': jax.random.normal(ks[0], (B, S, D), jnp.float32), 'router_w': w(ks[1], (D, E)), 'router_b': jnp.zeros((E,), jnp.float32), 'wq': w(ks[2], (E, D, D)), 'bq': jnp.zeros((E, D), jnp.float32), 'wk': w(ks[3], (E, D, D)), 'bk': jnp.zeros((E, D), jnp.float32), 'wv': w(ks[4], (E, D, D)), 'bv': jnp.zeros((E, D), jnp.float32), 'wo': w(ks[5], (E, D, D)), 'bo': jnp.zeros((E, D), jnp.float32)}
    _L0_ffn_all = _L0_ffn_setup()
    _L0_ffn_in = {k: v for k, v in _L0_ffn_all.items() if k in ('router_w', 'router_b', 'wq', 'bq', 'wk', 'bk', 'wv', 'bv', 'wo', 'bo')}
    del _L0_ffn_all
    return {'x': x, 'ctx_512': ctx_512, 'L0_xattn_Wq': _L0_xattn_in['Wq'], 'L0_xattn_bq': _L0_xattn_in['bq'], 'L0_xattn_Wk': _L0_xattn_in['Wk'], 'L0_xattn_bk': _L0_xattn_in['bk'], 'L0_xattn_Wv': _L0_xattn_in['Wv'], 'L0_xattn_bv': _L0_xattn_in['bv'], 'L0_xattn_Wo': _L0_xattn_in['Wo'], 'L0_xattn_bo': _L0_xattn_in['bo'], 'L0_attn_w_qkv': _L0_attn_in['w_qkv'], 'L0_attn_b_qkv': _L0_attn_in['b_qkv'], 'L0_attn_w_proj': _L0_attn_in['w_proj'], 'L0_attn_b_proj': _L0_attn_in['b_proj'], 'L0_ffn_router_w': _L0_ffn_in['router_w'], 'L0_ffn_router_b': _L0_ffn_in['router_b'], 'L0_ffn_wq': _L0_ffn_in['wq'], 'L0_ffn_bq': _L0_ffn_in['bq'], 'L0_ffn_wk': _L0_ffn_in['wk'], 'L0_ffn_bk': _L0_ffn_in['bk'], 'L0_ffn_wv': _L0_ffn_in['wv'], 'L0_ffn_bv': _L0_ffn_in['bv'], 'L0_ffn_wo': _L0_ffn_in['wo'], 'L0_ffn_bo': _L0_ffn_in['bo']}

def reference(x, ctx_512, L0_xattn_Wq, L0_xattn_bq, L0_xattn_Wk, L0_xattn_bk, L0_xattn_Wv, L0_xattn_bv, L0_xattn_Wo, L0_xattn_bo, L0_attn_w_qkv, L0_attn_b_qkv, L0_attn_w_proj, L0_attn_b_proj, L0_ffn_router_w, L0_ffn_router_b, L0_ffn_wq, L0_ffn_bq, L0_ffn_wk, L0_ffn_bk, L0_ffn_wv, L0_ffn_bv, L0_ffn_wo, L0_ffn_bo):
    import jax
    import jax.numpy as jnp

    def _L0_xattn_ref(q, k, v, Wq, bq, Wk, bk, Wv, bv, Wo, bo):
        import jax, jax.numpy as jnp
        import numpy as np
        HEADS = 16
        D_MODEL = 512
        IMG_MODEL = 256
        D_K = D_MODEL // HEADS
        B, LQ, _ = q.shape
        LKV = k.shape[1]
        qh = (q @ Wq + bq).reshape(B, LQ, HEADS, D_K).transpose(0, 2, 1, 3)
        kh = (k @ Wk + bk).reshape(B, LKV, HEADS, D_K).transpose(0, 2, 1, 3)
        vh = (v @ Wv + bv).reshape(B, LKV, HEADS, D_K).transpose(0, 2, 1, 3)
        scale = 1.0 / np.sqrt(D_K)
        scores = jnp.einsum('bhqd,bhkd->bhqk', qh, kh) * scale
        attn = jax.nn.softmax(scores, axis=-1)
        out = jnp.einsum('bhqk,bhkd->bhqd', attn, vh)
        concat = out.transpose(0, 2, 1, 3).reshape(B, LQ, D_MODEL)
        return concat @ Wo + bo

    def _L0_attn_ref(x, w_qkv, b_qkv, w_proj, b_proj):
        import jax, jax.numpy as jnp
        import numpy as np
        DIM = 512
        NUM_HEADS = 16
        HEAD_DIM = DIM // NUM_HEADS
        SCALE = HEAD_DIM ** (-0.5)
        b, n, c = x.shape
        qkv = x @ w_qkv + b_qkv
        qkv = qkv.reshape(b, n, 3, NUM_HEADS, HEAD_DIM)
        qkv = jnp.transpose(qkv, (2, 0, 3, 1, 4))
        q, k, v = (qkv[0], qkv[1], qkv[2])
        attn = jnp.einsum('bhnd,bhmd->bhnm', q, k) * SCALE
        attn = jax.nn.softmax(attn, axis=-1)
        out = jnp.einsum('bhnm,bhmd->bhnd', attn, v)
        out = jnp.transpose(out, (0, 2, 1, 3)).reshape(b, n, c)
        out = out @ w_proj + b_proj
        return out

    def _L0_ffn_ref(x, router_w, router_b, wq, bq, wk, bk, wv, bv, wo, bo):
        import jax, jax.numpy as jnp
        import numpy as np
        B, S, D, H, E = (4, 1024, 512, 16, 4)
        b, s, d = x.shape
        e_total = router_w.shape[-1]
        h = H
        hd = d // h
        sm_scale = 0.5
        logits = x @ router_w + router_b
        probs = jax.nn.softmax(logits, axis=-1)
        _, top2 = jax.lax.top_k(probs, 2)
        out = jnp.zeros_like(x)
        bidx = jnp.arange(b)[:, None]
        for e in range(e_total):
            member = (top2 == e).any(-1)
            w_tok = jnp.where(member, probs[..., e], 0.0)
            order = jnp.argsort((~member).astype(jnp.int32), axis=-1, stable=True)
            xg = jnp.take_along_axis(x, order[..., None], axis=1)
            validg = jnp.take_along_axis(member, order, axis=1)
            wg = jnp.take_along_axis(w_tok, order, axis=1)
            q = (xg @ wq[e] + bq[e]).reshape(b, s, h, hd)
            k = (xg @ wk[e] + bk[e]).reshape(b, s, h, hd)
            v = (xg @ wv[e] + bv[e]).reshape(b, s, h, hd)
            att = jnp.einsum('bqhd,bkhd->bhqk', q, k) * sm_scale
            att = jnp.where(validg[:, None, None, :], att, -1000000000.0)
            att = jax.nn.softmax(att, axis=-1)
            y = jnp.einsum('bhqk,bkhd->bqhd', att, v).reshape(b, s, d)
            y = y @ wo[e] + bo[e]
            out = out.at[bidx, order].add(wg[..., None] * y)
        return out
    x = x + _L0_xattn_ref(_layernorm(x, axis=-1), ctx_512, ctx_512, L0_xattn_Wq, L0_xattn_bq, L0_xattn_Wk, L0_xattn_bk, L0_xattn_Wv, L0_xattn_bv, L0_xattn_Wo, L0_xattn_bo)
    x = x + _L0_attn_ref(_layernorm(x, axis=-1), L0_attn_w_qkv, L0_attn_b_qkv, L0_attn_w_proj, L0_attn_b_proj)
    x = x + _L0_ffn_ref(_layernorm(x, axis=-1), L0_ffn_router_w, L0_ffn_router_b, L0_ffn_wq, L0_ffn_bq, L0_ffn_wk, L0_ffn_bk, L0_ffn_wv, L0_ffn_bv, L0_ffn_wo, L0_ffn_bo)
    return x

_drawn_inputs = setup_inputs


def setup_inputs(seed=0):
    import zlib

    import numpy as np

    out = dict(_drawn_inputs(seed))
    spreads = {'L0_xattn_bq': (0.0, 0.341),
     'L0_xattn_bk': (0.0, 0.8),
     'L0_xattn_bv': (0.0, 0.1),
     'L0_xattn_bo': (0.0, 0.1),
     'L0_ffn_router_b': (0.0, 0.646),
     'L0_ffn_bq': (0.0, 0.8),
     'L0_ffn_bk': (0.0, 0.8),
     'L0_ffn_bv': (0.0, 0.483),
     'L0_ffn_bo': (0.0, 0.1)}
    factors = {'L0_attn_b_qkv': 3.229, 'L0_attn_b_proj': 3.438, 'L0_ffn_wq': 7.764, 'L0_ffn_wk': 7.587}
    for name, (base, spread) in spreads.items():
        noise = np.random.default_rng([zlib.crc32(name.encode()), seed]).standard_normal(out[name].shape)
        drawn = base * np.exp(spread * noise) if base else spread * noise
        out[name] = jnp.asarray(drawn.astype(out[name].dtype))
    for name, factor in factors.items():
        out[name] = (out[name] * factor).astype(out[name].dtype)
    return out
```

```python
from contextlib import ExitStack

import concourse.bass as bass
from concourse import mybir

F32 = mybir.dt.float32
F32R = mybir.dt.float32r
ALU = mybir.AluOpType
ACT = mybir.ActivationFunctionType
X = mybir.AxisListType.X

P = 128
BATCH = 128
LQ = 32
D = 512
H = 16
DH = D // H
C = D // P
HG = P // DH
LK = 257
LKE = LK + 1
DC = 256
CC = DC // P
TOK = BATCH * LQ
TILE_SEQ = P // LQ
TILES = TOK // P
SUP = 4
N = SUP * P
SUPERS = TOK // N
EXPERTS = 4
LAYERS = 1 + EXPERTS
EPS = 1e-5
CROSS_SCALE = float(DH) ** -0.5
SELF_SCALE = float(DH) ** -0.5
EXPERT_SCALE = 0.5
MASKED = 1.0e9
PASSES = ((0, 0), (0, 1), (1, 0))


def alloc(nc, ctx):
    sems = []

    def clear():
        nc.clear_and_free_semaphores(sems)
        nc.all_engine_barrier()

    ctx.callback(clear)

    def sb(name, shape, dt=F32):
        return ctx.enter_context(nc.sbuf_tensor(name, shape, dt))

    def ps(name):
        return ctx.enter_context(nc.psum_tensor(name, [P, 512], F32))

    def sem(name):
        sems.append(nc.alloc_semaphore(name=name))
        return sems[-1]

    return sb, ps, sem


def wait(eng, seen, *waits):
    for s, value in waits:
        eng.wait_ge(s, value)
        eng.sem_inc(seen, 1)


def bc_mid(ap, n):
    return ap.unsqueeze(1).broadcast_to([ap.shape[0], n, ap.shape[1]])


def bc_last(ap, n):
    return ap.unsqueeze(2).broadcast_to([ap.shape[0], ap.shape[1], n])


def norm_phase(nc, tag, x_d, xn_d, q=None, router=None):
    with ExitStack() as ctx:
        sb, ps, sem = alloc(nc, ctx)
        x = sb(f"{tag}_x", [P, SUP, D])
        xn = sb(f"{tag}_xn", [P, SUP, D])
        xt = [sb(f"{tag}_xt{k}", [P, C, N], F32R) for k in range(2)]
        stats = sb(f"{tag}_stats", [P, SUP, 6])
        mv = sb(f"{tag}_mv", [P, SUP, 2])
        var_eps = sb(f"{tag}_vareps", [P, SUP])
        rstd = sb(f"{tag}_rstd", [P, SUP])
        power = sb(f"{tag}_power", [P, SUP])
        ident = sb(f"{tag}_ident", [P, P])
        turned = [ps(f"{tag}_turned{k}") for k in range(2)]
        prod = [ps(f"{tag}_prod{k}") for k in range(C)]
        if q:
            w_d, b_d, q_d = q
            w32 = sb(f"{tag}_w32", [P, C, D])
            w = [sb(f"{tag}_w{k}", [P, C, D], F32R) for k in range(2)]
            bias = sb(f"{tag}_bias", [P, C])
            bias_s = sb(f"{tag}_bias_s", [P, C])
            qt = sb(f"{tag}_qt", [P, C, N])
        if router:
            rw_d, rb_d, logit_d = router
            rw32 = sb(f"{tag}_rw32", [P, C, EXPERTS])
            rw = [sb(f"{tag}_rw{k}", [P, C, EXPERTS], F32R) for k in range(2)]
            rb = sb(f"{tag}_rb", [P, EXPERTS])
            logit = sb(f"{tag}_logit", [P, SUP, EXPERTS])

        s_seen = sem(f"{tag}_s_seen")
        s_ident = sem(f"{tag}_s_ident")
        s_w_in = sem(f"{tag}_s_w_in")
        s_w_hi = sem(f"{tag}_s_w_hi")
        s_w_split = sem(f"{tag}_s_w_split")
        s_x_in = sem(f"{tag}_s_x_in")
        s_stats = sem(f"{tag}_s_stats")
        s_mv = sem(f"{tag}_s_mv")
        s_eps = sem(f"{tag}_s_eps")
        s_rstd = sem(f"{tag}_s_rstd")
        s_xn = sem(f"{tag}_s_xn")
        s_turned = [sem(f"{tag}_s_turned{k}") for k in range(2)]
        s_hi = sem(f"{tag}_s_hi")
        s_split = [sem(f"{tag}_s_split{k}") for k in range(2)]
        s_prod = sem(f"{tag}_s_prod")
        s_taken = sem(f"{tag}_s_taken")
        s_out = sem(f"{tag}_s_out")
        outs = 1 if q else 2 + bool(router)
        prods = C if q else SUP if router else 0

        block = ctx.enter_context(nc.Block())

        @block.sync
        def _(sp):
            if q:
                sp.dma_start(w32[:], w_d).then_inc(s_w_in, 16)
                sp.dma_start(bias[:], b_d).then_inc(s_w_in, 16)
            if router:
                sp.dma_start(rw32[:], rw_d).then_inc(s_w_in, 16)
                sp.dma_start(rb[:], rb_d).then_inc(s_w_in, 16)
            sp.sem_inc(s_xn, 1)
            with sp.Fori(0, SUPERS) as s:
                wait(sp, s_seen, (s_xn, s * SUP + 1))
                sp.dma_start(x[:], x_d[bass.ds(s * SUP, SUP)].rearrange("t p d -> p t d")).then_inc(s_x_in, 16)

        @block.gpsimd
        def _(pool):
            nc.gpsimd.memset(ident[:], 0.0).then_inc(s_ident, 1)
            nc.gpsimd.memset(power[:], -0.5).then_inc(s_ident, 1)
            pool.wait_ge(s_ident, 2)
            nc.gpsimd.affine_select(out=ident[:], in_=ident[:], compare_op=ALU.not_equal, fill=1.0, base=0,
                                    pattern=[[-1, P]], channel_multiplier=1).then_inc(s_ident, 1)
            with pool.Fori(0, SUPERS) as s:
                wait(pool, s_seen, (s_mv, s * SUP + SUP))
                nc.gpsimd.tensor_scalar(var_eps[:], mv[:, :, 1], EPS, 1.0, ALU.add, ALU.mult).then_inc(s_eps, 1)
                pool.wait_ge(s_eps, s + 1)
                nc.gpsimd.tensor_tensor(rstd[:], var_eps[:], power[:], ALU.pow).then_inc(s_rstd, 1)

        @block.vector
        def _(dve):
            if q:
                dve.wait_ge(s_w_hi, 1)
                nc.vector.tensor_tensor(w[1][:], w32[:], w[0][:].bitcast(F32), ALU.subtract).then_inc(s_w_split, 1)
                nc.vector.tensor_scalar(bias_s[:], bias[:], CROSS_SCALE, None, ALU.mult).then_inc(s_w_split, 1)
            if router:
                dve.wait_ge(s_w_hi, 1)
                nc.vector.tensor_tensor(rw[1][:], rw32[:], rw[0][:].bitcast(F32), ALU.subtract).then_inc(s_w_split, 1)
            dve.sem_inc(s_split[0], 1)
            dve.sem_inc(s_split[1], 1)
            with dve.Fori(0, SUPERS) as s:
                dve.wait_ge(s_x_in, s * 16 + 16)
                for t in range(SUP):
                    nc.vector.bn_stats(stats[:, t, :], x[:, t, :]).then_inc(s_stats, 1)
                for t in range(SUP):
                    wait(dve, s_seen, (s_stats, s * SUP + t + 1))
                    nc.vector.bn_aggr(mv[:, t, :], stats[:, t, :]).then_inc(s_mv, 1)
                dve.wait_ge(s_rstd, s + 1)
                for t in range(SUP):
                    nc.vector.tensor_scalar(xn[:, t, :], x[:, t, :], mv[:, t, 0:1], rstd[:, t:t + 1],
                                            ALU.subtract, ALU.mult).then_inc(s_xn, 1)
                for t in range(SUP):
                    dve.wait_ge(s_hi, s * SUP + t + 1)
                    nc.vector.tensor_tensor(xt[1][:, :, t * P:(t + 1) * P],
                                            turned[t % 2][:].rearrange("p (c n) -> p c n", c=C),
                                            xt[0][:, :, t * P:(t + 1) * P].bitcast(F32),
                                            ALU.subtract).then_inc(s_split[t % 2], 1)
                if router:
                    for t in range(SUP):
                        dve.wait_ge(s_prod, s * prods + t + 1)
                        if t == 0:
                            dve.wait_ge(s_out, s * (16 * outs) + 16)
                        nc.vector.tensor_tensor(logit[:, t, :], prod[t][:, 0:EXPERTS], rb[:], ALU.add)\
                            .then_inc(s_taken, 1)

        @block.tensor
        def _(pe):
            pe.wait_ge(s_ident, 3)
            with pe.Fori(0, SUPERS) as s:
                for t in range(SUP):
                    pe.wait_ge(s_xn, s * SUP + t + 2)
                    pe.wait_ge(s_split[t % 2], s * (SUP // 2) + t // 2 + 1)
                    for c in range(C):
                        last = nc.tensor.transpose(turned[t % 2][:, c * P:(c + 1) * P], xn[:, t, c * P:(c + 1) * P],
                                                   ident[:])
                    last.then_inc(s_turned[t % 2], 1)
                if q or router:
                    for k in range(2):
                        pe.wait_ge(s_split[k], s * (SUP // 2) + SUP // 2 + 1)
                if q:
                    pe.wait_ge(s_w_split, 1)
                    for g in range(C):
                        pe.wait_ge(s_taken, s * C + 1)
                        for c in range(C):
                            for n, (a, b) in enumerate(PASSES):
                                last = nc.tensor.matmul(prod[g][:], w[a][:, c, g * P:(g + 1) * P], xt[b][:, c, :],
                                                        start=(c == 0 and n == 0), stop=(c == C - 1 and n == 2))
                        last.then_inc(s_prod, 1)
                if router:
                    pe.wait_ge(s_w_split, 1)
                    pe.wait_ge(s_taken, s * SUP + 1)
                    for t in range(SUP):
                        for c in range(C):
                            for n, (a, b) in enumerate(PASSES):
                                last = nc.tensor.matmul(prod[t][:, 0:EXPERTS], xt[a][:, c, t * P:(t + 1) * P],
                                                        rw[b][:, c, :], start=(c == 0 and n == 0),
                                                        stop=(c == C - 1 and n == 2))
                        last.then_inc(s_prod, 1)

        @block.scalar
        def _(act):
            if q or router:
                act.wait_ge(s_w_in, 32)
                src, dst = (w32, w[0]) if q else (rw32, rw[0])
                nc.scalar.activation(dst[:], src[:], ACT.Copy).then_inc(s_w_hi, 1)
            act.sem_inc(s_taken, 1)
            act.sem_inc(s_out, 16)
            with act.Fori(0, SUPERS) as s:
                for t in range(SUP):
                    act.wait_ge(s_turned[t % 2], s * (SUP // 2) + t // 2 + 1)
                    if t == 0 and q:
                        act.wait_ge(s_taken, s * C + 1)
                    elif t == 0:
                        act.wait_ge(s_out, s * (16 * outs) + 16)
                    nc.scalar.activation(xt[0][:, :, t * P:(t + 1) * P],
                                         turned[t % 2][:].rearrange("p (c n) -> p c n", c=C),
                                         ACT.Copy).then_inc(s_hi, 1)
                if q:
                    act.wait_ge(s_w_split, 2)
                    act.wait_ge(s_out, s * 16 + 16)
                    for g in range(C):
                        act.wait_ge(s_prod, s * C + g + 1)
                        nc.scalar.activation(qt[:, g, :], prod[g][:], ACT.Identity, bias=bias_s[:, g:g + 1],
                                             scale=CROSS_SCALE).then_inc(s_taken, 1)
                    act.wait_ge(s_taken, s * C + C + 1)
                    act.dma_start(q_d[:, :, bass.ds(s * N, N)], qt[:]).then_inc(s_out, 16)
                else:
                    for k in range(2):
                        act.wait_ge(s_split[k], s * (SUP // 2) + SUP // 2 + 1)
                    for k in range(2):
                        act.dma_start(xn_d[s, k], xt[k][:].bitcast(F32)).then_inc(s_out, 16)
                    if router:
                        act.wait_ge(s_taken, s * SUP + SUP + 1)
                        act.dma_start(logit_d[:, bass.ds(s * SUP, SUP), :], logit[:]).then_inc(s_out, 16)
            act.wait_ge(s_out, SUPERS * 16 * outs + 16)


def cross_phase(nc, x_d, q_d, ctx_d, ctx_t_d, wk_d, wv_d, wo_d, bias_d, bo_d, x1_d):
    B = TILE_SEQ
    with ExitStack() as ctx:
        sb, ps, sem = alloc(nc, ctx)
        wk32 = sb("c_wk32", [P, CC, D])
        wk = [sb(f"c_wk{k}", [P, CC, D], F32R) for k in range(2)]
        wv = sb("c_wv", [P, CC, D])
        wo32 = sb("c_wo32", [P, C, D])
        wo = [sb(f"c_wo{k}", [P, C, D], F32R) for k in range(2)]
        bias = sb("c_bias", [P, 3, C])
        bo = sb("c_bo", [P, D])
        ident = sb("c_ident", [P, P])
        ct = [sb(f"c_ct{b}", [P, CC, LK]) for b in range(2)]
        cn = [sb(f"c_cn{b}", [P, 2, DC]) for b in range(2)]
        c1 = [sb(f"c_cl{b}", [96, DC]) for b in range(2)]
        cth = [[sb(f"c_cth{b}_{k}", [P, CC, LKE], F32R) for k in range(2)] for b in range(2)]
        cnh = [[sb(f"c_cnh{b}_{k}", [P, 2, DC], F32R) for k in range(2)] for b in range(2)]
        c1h = [sb(f"c_clh{b}", [96, DC], F32R) for b in range(2)]
        qt = sb("c_qt", [P, C, P])
        qs = [sb(f"c_qs{k}", [P, C, P], F32R) for k in range(2)]
        own = sb("c_own", [P, HG])
        qh = [[sb(f"c_qh{b}_{k}", [P, C, HG, LQ], F32R) for k in range(2)] for b in range(2)]
        kt = [sb(f"c_kt{k}", [P, C, LKE], F32R) for k in range(2)]
        negmax = sb("c_negmax", [P, C])
        total = sb("c_total", [P, C])
        inv = sb("c_inv", [P, C])
        probs = sb("c_probs", [P, C, LK])
        last_p = sb("c_last_p", [P, C, 96], F32R)
        pt = [sb(f"c_pt{k}", [P, 2, C * P], F32R) for k in range(2)]
        p1 = sb("c_p1", [96, C * P], F32R)
        mix = sb("c_mix", [P, CC, H, B, LQ])
        ot = sb("c_ot", [P, C, P])
        oth = [sb(f"c_oth{k}", [P, C, P], F32R) for k in range(2)]
        xt = [sb(f"c_xt{b}", [P, D]) for b in range(2)]
        xb = sb("c_xb", [P, D])
        x1 = sb("c_x1", [P, D])

        bank_k = [ps(f"c_bank_k{b}") for b in range(2)]
        bank_s = [ps(f"c_bank_s{b}") for b in range(2)]
        bank_t = [ps(f"c_bank_t{b}") for b in range(2)]
        bank_v = [ps(f"c_bank_v{b}") for b in range(2)]

        s_seen = sem("c_s_seen")
        s_w_in = sem("c_s_w_in")
        s_w_hi = sem("c_s_w_hi")
        s_w_split = sem("c_s_w_split")
        s_const = sem("c_s_const")
        s_zero = sem("c_s_zero")
        s_ctx_in = [sem(f"c_s_ctx_in{b}") for b in range(2)]
        s_q_in = sem("c_s_q_in")
        s_x_in = sem("c_s_x_in")
        s_ctx_hi = sem("c_s_ctx_hi")
        s_c1_hi = sem("c_s_c1_hi")
        s_c1_split = sem("c_s_c1_split")
        s_ctx_split = sem("c_s_ctx_split")
        s_q_hi = sem("c_s_q_hi")
        s_q_split = sem("c_s_q_split")
        s_k = [sem(f"c_s_k{b}") for b in range(2)]
        s_k_hi = sem("c_s_k_hi")
        s_k_split = [sem(f"c_s_k_split{b}") for b in range(2)]
        s_s = [sem(f"c_s_s{b}") for b in range(2)]
        s_max = sem("c_s_max")
        s_exp = [sem(f"c_s_exp{b}") for b in range(2)]
        s_inv = sem("c_s_inv")
        s_norm = sem("c_s_norm")
        s_last = sem("c_s_last")
        s_probs = sem("c_s_probs")
        s_t = [sem(f"c_s_t{b}") for b in range(2)]
        s_t_hi = sem("c_s_t_hi")
        s_t_split = [sem(f"c_s_t_split{b}") for b in range(2)]
        s_v = [sem(f"c_s_v{b}") for b in range(2)]
        s_v_taken = [sem(f"c_s_v_taken{b}") for b in range(2)]
        s_o_hi = sem("c_s_o_hi")
        s_o_split = sem("c_s_o_split")
        s_xb = sem("c_s_xb")
        s_x1 = sem("c_s_x1")
        s_out = sem("c_s_out")

        def v0_output(i):
            return i * (B + 1) - 1

        def v1_project(i):
            if isinstance(i, int) and i == TILES:
                return i * (B + 1) - 1
            return i * (B + 1)

        def v_before(i, j, bank):
            ahead = 1 if bank == 0 or j >= 1 else 0
            if isinstance(i, int) and i == 0:
                return j
            return i * (B + 1) - 1 + j + ahead

        block = ctx.enter_context(nc.Block())

        @block.sync
        def _(sp):
            sp.dma_start(wk32[:], wk_d).then_inc(s_w_in, 16)
            sp.dma_start(bias[:], bias_d).then_inc(s_w_in, 16)
            sp.dma_start(wo32[:], wo_d).then_inc(s_w_in, 16)
            sp.dma_start(wv[:], wv_d).then_inc(s_w_in, 16)
            sp.dma_start(bo[:], bo_d.broadcast_to([P, D])).then_inc(s_w_in, 16)
            sp.sem_inc(s_out, 16)
            sp.wait_ge(s_zero, 2)

            def load(i, j, first=False):
                b = j % 2
                m = i * B + j
                if not first:
                    wait(sp, s_seen, (s_ctx_hi, (m - 1) * 2), (s_ctx_split, (m - 1) * 2), (s_c1_split, m - 1))
                sp.dma_start(ct[b][:], ctx_t_d[m]).then_inc(s_ctx_in[b], 16)
                sp.dma_start(cn[b][:], ctx_d[m, 0:LK - 1].rearrange("(c p) d -> p c d", p=P)).then_inc(s_ctx_in[b], 16)
                for r in (0, 32, 64):
                    sp.dma_start(c1[b][r:r + 1, :], ctx_d[m, LK - 1:LK]).then_inc(s_ctx_in[b], 16)

            def load_queries(i):
                sp.dma_start(qt[:], q_d[:, :, bass.ds(i * P, P)]).then_inc(s_q_in, 16)

            def load_x(i):
                sp.dma_start(xt[0][:], x_d[i]).then_inc(s_x_in, 16)

            def store(i):
                wait(sp, s_seen, (s_x1, i + 1))
                sp.dma_start(x1_d[i], x1[:]).then_inc(s_out, 16)

            def tile(i, first=False, last=False):
                load(i, 2)
                load(i, 3)
                if not last:
                    wait(sp, s_seen, (s_q_split, (i + 1) * 2 * B))
                    load_queries(i + 1)
                    load(i + 1, 0)
                    load(i + 1, 1)
                if not first:
                    store(i - 1)
                    wait(sp, s_seen, (s_xb, i))
                load_x(i)

            load_queries(0)
            load(0, 0, first=True)
            load(0, 1, first=True)
            tile(0, first=True)
            with sp.Fori(1, TILES - 1) as i:
                tile(i)
            tile(TILES - 1, last=True)
            store(TILES - 1)
            sp.wait_ge(s_out, 16 * TILES + 16)

        @block.gpsimd
        def _(pool):
            nc.gpsimd.memset(ident[:], 0.0).then_inc(s_const, 1)
            pool.wait_ge(s_const, 1)
            nc.gpsimd.affine_select(out=ident[:], in_=ident[:], compare_op=ALU.not_equal, fill=1.0, base=0,
                                    pattern=[[-1, P]], channel_multiplier=1).then_inc(s_const, 1)
            for b in range(2):
                nc.gpsimd.memset(c1[b][:], 0.0).then_inc(s_zero, 1)
            nc.gpsimd.memset(own[:], 1.0).then_inc(s_const, 1)
            pool.wait_ge(s_const, 3)
            nc.gpsimd.affine_select(out=own[:], in_=own[:], compare_op=ALU.is_ge, fill=0.0, base=0,
                                    pattern=[[-DH, HG]], channel_multiplier=1).then_inc(s_const, 1)
            pool.wait_ge(s_const, 4)
            nc.gpsimd.affine_select(out=own[:], in_=own[:], compare_op=ALU.is_ge, fill=0.0, base=DH - 1,
                                    pattern=[[DH, HG]], channel_multiplier=-1).then_inc(s_const, 1)
            for b in range(2):
                for k in range(2):
                    nc.gpsimd.memset(cth[b][k][:, :, LK:LKE].bitcast(F32), 0.0).then_inc(s_const, 1)
            nc.gpsimd.memset(last_p[:].bitcast(F32), 0.0).then_inc(s_const, 1)

            def halves(i, j):
                b = j % 2
                m = i * B + j
                wait(pool, s_seen, (s_ctx_hi, 2 * m + 1))
                nc.gpsimd.tensor_tensor(cth[b][1][:, :, 0:LK], ct[b][:], cth[b][0][:, :, 0:LK].bitcast(F32),
                                        ALU.subtract).then_inc(s_ctx_split, 1)
                wait(pool, s_seen, (s_q_in, (i + 1) * 16))
                if j == 0:
                    nc.gpsimd.tensor_copy(qs[0][:], qt[:]).then_inc(s_q_hi, 1)
                    pool.wait_ge(s_q_hi, 2 * i + 1)
                    nc.gpsimd.tensor_tensor(qs[1][:], qt[:], qs[0][:].bitcast(F32), ALU.subtract).then_inc(s_q_hi, 1)
                    pool.wait_ge(s_q_hi, 2 * i + 2)
                for k in range(2):
                    nc.gpsimd.tensor_tensor(
                        qh[b][k][:],
                        qs[k][:, :, j * LQ:(j + 1) * LQ].bitcast(F32).unsqueeze(2).broadcast_to([P, C, HG, LQ]),
                        own[:].unsqueeze(1).unsqueeze(3).broadcast_to([P, C, HG, LQ]),
                        ALU.mult).then_inc(s_q_split, 1)

            def halves_n(i, j):
                b = j % 2
                m = i * B + j
                pool.wait_ge(s_ctx_hi, 2 * m + 2)
                nc.gpsimd.tensor_tensor(cnh[b][1][:], cn[b][:], cnh[b][0][:].bitcast(F32),
                                        ALU.subtract).then_inc(s_ctx_split, 1)

            def output(i):
                pool.wait_ge(s_x_in, (i + 1) * 16)
                pool.wait_ge(s_x1, i)
                nc.gpsimd.tensor_tensor(xb[:], xt[0][:], bo[:], ALU.add).then_inc(s_xb, 1)
                pool.wait_ge(s_o_hi, i * 2 + 2)
                nc.gpsimd.tensor_tensor(oth[1][:], ot[:], oth[0][:].bitcast(F32), ALU.subtract).then_inc(s_o_split, 1)

            pool.wait_ge(s_const, 10)
            pool.wait_ge(s_w_in, 80)
            for j in range(2):
                halves(0, j)
                halves_n(0, j)

            def tile(i, first=False, last=False):
                for j in range(B):
                    ahead = (i if j + 2 < B else i + 1, (j + 2) % B)
                    if j + 2 < B or not last:
                        halves(*ahead)
                    if j == 0 and not first:
                        output(i - 1)
                    if j + 2 < B or not last:
                        halves_n(*ahead)

            tile(0, first=True)
            with pool.Fori(1, TILES - 1) as i:
                tile(i)
            tile(TILES - 1, last=True)
            output(TILES - 1)

        @block.tensor
        def _(pe):
            pe.wait_ge(s_const, 10)
            pe.wait_ge(s_w_split, 2)

            def keys(i, j, groups):
                b = j % 2
                m = i * B + j
                pe.wait_ge(s_ctx_split, 2 * m + 1)
                for g in groups:
                    k = g % 2
                    pe.wait_ge(s_k_split[k], 2 * m + g // 2 + 1)
                    for c in range(CC):
                        for n, (a, d) in enumerate(PASSES):
                            last = nc.tensor.matmul(bank_k[k][:, 0:LKE], wk[a][:, c, g * P:(g + 1) * P],
                                                    cth[b][d][:, c, :], start=(c == 0 and n == 0),
                                                    stop=(c == CC - 1 and n == 2))
                    last.then_inc(s_k[k], 1)

            def scores(i, j, groups):
                b = j % 2
                m = i * B + j
                pe.wait_ge(s_q_split, 2 * m + 2)
                for g in groups:
                    k = g % 2
                    pe.wait_ge(s_k_split[k], 2 * m + g // 2 + 2)
                    pe.wait_ge(s_exp[k], 2 * m + g // 2 + 1)
                    for n, (a, d) in enumerate(PASSES):
                        last = nc.tensor.matmul(bank_s[k][:, 0:LKE], qh[b][a][:, g, :, :], kt[d][:, g, :],
                                                start=(n == 0), stop=(n == 2))
                    last.then_inc(s_s[k], 1)

            def turn(i, j, parts):
                m = i * B + j
                pe.wait_ge(s_probs, m + 1)
                for u in parts:
                    n = 3 * j + u
                    k = n % 2
                    pe.wait_ge(s_t_split[k], i * (3 * B // 2) + n // 2 + 1)
                    for g in range(C):
                        if u < 2:
                            last = nc.tensor.transpose(bank_t[k][:, g * P:(g + 1) * P],
                                                       probs[:, g, u * P:(u + 1) * P], ident[:])
                        else:
                            last = nc.tensor.transpose(bank_t[k][0:96, g * P:(g + 1) * P],
                                                       last_p[:, g, :].bitcast(F32), ident[:])
                    last.then_inc(s_t[k], 1)

            def sums(i, j, c):
                b = j % 2
                m = i * B + j

                def turned(u):
                    n = 3 * j + u
                    pe.wait_ge(s_t_split[n % 2], i * (3 * B // 2) + n // 2 + 2)

                pe.wait_ge(s_ctx_split, 2 * m + 2)
                pe.wait_ge(s_v_taken[c], v_before(i, j, c) + 1)
                cols = slice(c * P, (c + 1) * P)
                for u in range(2):
                    turned(u)
                    for n, (a, d) in enumerate(PASSES):
                        nc.tensor.matmul(bank_v[c][:], cnh[b][a][:, u, cols], pt[d][:, u, :],
                                         start=(u == 0 and n == 0), stop=False)
                turned(2)
                pe.wait_ge(s_c1_split, m + 1)
                nc.tensor.matmul(bank_v[c][:], c1h[b][:, cols], p1[:], start=False, stop=True).then_inc(s_v[c], 1)

            def output(i):
                for c in range(CC):
                    pe.wait_ge(s_v_taken[c], v0_output(i + 1) + 1)
                for h in range(H):
                    r = DH * (h % HG)
                    for c in range(CC):
                        last = nc.tensor.matmul(bank_v[0][r:r + DH, (h // HG) * P:(h // HG + 1) * P],
                                                wv[:, c, h * DH:(h + 1) * DH], mix[:, c, h, :, :],
                                                start=(c == 0), stop=(c == CC - 1), skip_group_check=True)
                last.then_inc(s_v[0], 1)

            def project(i):
                pe.wait_ge(s_o_split, i + 1)
                pe.wait_ge(s_v_taken[1], v1_project(i + 1) + 1)
                for c in range(C):
                    for n, (a, d) in enumerate(PASSES):
                        last = nc.tensor.matmul(bank_v[1][:], oth[a][:, c, :], wo[d][:, c, :],
                                                start=(c == 0 and n == 0), stop=(c == C - 1 and n == 2))
                last.then_inc(s_v[1], 1)

            keys(0, 0, range(C))
            scores(0, 0, range(C))

            def tile(i, first=False, last=False):
                for j in range(B):
                    more = j + 1 < B or not last
                    ni, nj = (i, j + 1) if j + 1 < B else (i + 1, 0)
                    if more:
                        keys(ni, nj, (0, 1))
                    turn(i, j, (0, 1))
                    if more:
                        keys(ni, nj, (2, 3))
                    turn(i, j, (2,))
                    if j == 0 and not first:
                        output(i - 1)
                    if more:
                        scores(ni, nj, (0, 1))
                    if j == 1 and not first:
                        project(i - 1)
                    sums(i, j, 0)
                    if more:
                        scores(ni, nj, (2, 3))
                    sums(i, j, 1)

            tile(0, first=True)
            with pe.Fori(1, TILES - 1) as i:
                tile(i)
            tile(TILES - 1, last=True)
            output(TILES - 1)
            project(TILES - 1)

        @block.scalar
        def _(act):
            act.wait_ge(s_w_in, 80)
            nc.scalar.activation(wk[0][:], wk32[:], ACT.Copy).then_inc(s_w_hi, 1)
            nc.scalar.activation(wo[0][:], wo32[:], ACT.Copy).then_inc(s_w_hi, 1)
            for k in range(2):
                act.sem_inc(s_exp[k], 1)
                act.sem_inc(s_v_taken[k], 1)

            def context_t(i, j):
                b = j % 2
                act.wait_ge(s_ctx_in[b], (i * (B // 2) + j // 2 + 1) * 80)
                nc.scalar.activation(cth[b][0][:, :, 0:LK], ct[b][:], ACT.Copy).then_inc(s_ctx_hi, 1)

            def context_n(j):
                b = j % 2
                nc.scalar.activation(cnh[b][0][:], cn[b][:], ACT.Copy).then_inc(s_ctx_hi, 1)

            def keys(i, j, groups):
                m = i * B + j
                for g in groups:
                    act.wait_ge(s_k[g % 2], 2 * m + g // 2 + 1)
                    nc.scalar.activation(kt[0][:, g, :], bank_k[g % 2][:, 0:LKE], ACT.Identity,
                                         bias=bias[:, 1, g:g + 1]).then_inc(s_k_hi, 1)

            def exps(i, j, groups):
                m = i * B + j
                for g in groups:
                    act.wait_ge(s_max, 4 * m + g + 1)
                    nc.scalar.activation(probs[:, g, :], bank_s[g % 2][:, 0:LK], ACT.Exp, bias=negmax[:, g:g + 1],
                                         accum_out=total[:, g:g + 1]).then_inc(s_exp[g % 2], 1)

            def turned(i, j):
                for u in range(2):
                    n = 3 * j + u
                    act.wait_ge(s_t[n % 2], i * (3 * B // 2) + n // 2 + 1)
                    nc.scalar.activation(pt[0][:, u, :], bank_t[n % 2][:], ACT.Copy).then_inc(s_t_hi, 1)

            def turned_last(i, j):
                n = 3 * j + 2
                act.wait_ge(s_t[n % 2], i * (3 * B // 2) + n // 2 + 1)
                nc.scalar.activation(p1[:], bank_t[n % 2][0:96, :], ACT.Copy).then_inc(s_t_split[n % 2], 1)

            def sums(i, j, c):
                act.wait_ge(s_v[c], v_before(i, j, c) + 1)
                nc.scalar.activation(mix[:, c, :, j, :], bank_v[c][:].rearrange("p (h q) -> p h q", h=H),
                                     ACT.Copy).then_inc(s_v_taken[c], 1)

            def output(i):
                act.wait_ge(s_o_hi, i * 2 + 1)
                nc.scalar.activation(oth[0][:], ot[:], ACT.Copy).then_inc(s_o_hi, 1)

            for j in range(2):
                context_t(0, j)
                context_n(j)
            keys(0, 0, range(C))
            exps(0, 0, range(C))

            def tile(i, first=False, last=False):
                for j in range(B):
                    more = j + 1 < B or not last
                    ni, nj = (i, j + 1) if j + 1 < B else (i + 1, 0)
                    ahead = (i if j + 2 < B else i + 1, (j + 2) % B)
                    if more:
                        keys(ni, nj, (0, 1))
                    turned(i, j)
                    if more:
                        keys(ni, nj, (2, 3))
                    turned_last(i, j)
                    if j == 0 and not first:
                        output(i - 1)
                    if more:
                        exps(ni, nj, (0, 1))
                    if j + 2 < B or not last:
                        context_t(*ahead)
                    sums(i, j, 0)
                    if more:
                        exps(ni, nj, (2, 3))
                    sums(i, j, 1)
                    if j + 2 < B or not last:
                        context_n((j + 2) % B)

            tile(0, first=True)
            with act.Fori(1, TILES - 1) as i:
                tile(i)
            tile(TILES - 1, last=True)
            output(TILES - 1)

        @block.vector
        def _(dve):
            for n, (w32, lo, hi) in enumerate(((wk32, wk[1], wk[0]), (wo32, wo[1], wo[0]))):
                dve.wait_ge(s_w_hi, n + 1)
                nc.vector.tensor_tensor(lo[:], w32[:], hi[:].bitcast(F32), ALU.subtract).then_inc(s_w_split, 1)
            for k in range(2):
                dve.sem_inc(s_k_split[k], 1)
                dve.sem_inc(s_t_split[k], 1)
            dve.wait_ge(s_const, 10)

            def keys(i, j, groups):
                m = i * B + j
                for g in groups:
                    dve.wait_ge(s_k_hi, 4 * m + g + 1)
                    nc.vector.scalar_tensor_tensor(out=kt[1][:, g, :], in0=bank_k[g % 2][:, 0:LKE],
                                                   scalar=bias[:, 1, g:g + 1], in1=kt[0][:, g, :].bitcast(F32),
                                                   op0=ALU.add, op1=ALU.subtract).then_inc(s_k_split[g % 2], 1)

            def maxima(i, j, groups):
                m = i * B + j
                for g in groups:
                    dve.wait_ge(s_s[g % 2], 2 * m + g // 2 + 1)
                    nc.vector.tensor_reduce(negmax[:, g:g + 1], bank_s[g % 2][:, 0:LK], X, ALU.max,
                                            negate=True).then_inc(s_max, 1)

            def normalise(i, j, pair):
                m = i * B + j
                for k in range(2):
                    dve.wait_ge(s_exp[k], 2 * m + pair + 2)
                both = slice(2 * pair, 2 * pair + 2)
                nc.vector.reciprocal(inv[:, both], total[:, both]).then_inc(s_inv, 1)
                dve.wait_ge(s_inv, 2 * m + pair + 1)
                for g in (2 * pair, 2 * pair + 1):
                    last = nc.vector.tensor_scalar(probs[:, g, :], probs[:, g, :], inv[:, g:g + 1], None, ALU.mult)
                last.then_inc(s_norm, 1)

            def last_halves(i, j):
                m = i * B + j
                dve.wait_ge(s_norm, 2 * m + 2)
                nc.vector.tensor_copy(last_p[:, :, 0:64:32],
                                      bc_last(probs[:, :, LK - 1], 2)).then_inc(s_last, 1)
                dve.wait_ge(s_last, m + 1)
                nc.vector.tensor_tensor(last_p[:, :, 64], probs[:, :, LK - 1], last_p[:, :, 0].bitcast(F32),
                                        ALU.subtract).then_inc(s_probs, 1)

            def turned(i, j):
                m = i * B + j
                for u in range(2):
                    n = 3 * j + u
                    dve.wait_ge(s_t_hi, 2 * m + u + 1)
                    nc.vector.tensor_tensor(pt[1][:, u, :], bank_t[n % 2][:], pt[0][:, u, :].bitcast(F32),
                                            ALU.subtract).then_inc(s_t_split[n % 2], 1)

            def output(i):
                dve.wait_ge(s_v[0], v0_output(i + 1) + 1)
                nc.vector.tensor_tensor(ot[:], bank_v[0][:].rearrange("p (g n) -> p g n", g=C),
                                        bc_last(bias[:, 2, :], P), ALU.add).then_inc(s_o_hi, 1)
                dve.wait_ge(s_o_hi, i * 2 + 1)
                dve.sem_inc(s_v_taken[0], 1)

            def residual(i):
                dve.wait_ge(s_v[1], v1_project(i + 1) + 1)
                dve.wait_ge(s_xb, i + 1)
                dve.wait_ge(s_out, 16 * i + 16)
                nc.vector.tensor_tensor(x1[:], bank_v[1][:], xb[:], ALU.add).then_inc(s_x1, 1)
                dve.wait_ge(s_x1, i + 1)
                dve.sem_inc(s_v_taken[1], 1)

            def last_key(i, j):
                b = j % 2
                m = i * B + j
                dve.wait_ge(s_ctx_in[b], (i * (B // 2) + j // 2 + 1) * 80)
                nc.vector.tensor_copy(c1h[b][:], c1[b][:]).then_inc(s_c1_hi, 1)
                dve.wait_ge(s_c1_hi, m + 1)
                nc.vector.tensor_tensor(c1h[b][32:64, :], c1[b][32:64, :], c1h[b][32:64, :].bitcast(F32),
                                        ALU.subtract).then_inc(s_c1_split, 1)

            last_key(0, 0)
            keys(0, 0, range(C))
            maxima(0, 0, range(C))
            normalise(0, 0, 0)
            normalise(0, 0, 1)
            last_halves(0, 0)

            def tile(i, first=False, last=False):
                for j in range(B):
                    more = j + 1 < B or not last
                    ni, nj = (i, j + 1) if j + 1 < B else (i + 1, 0)
                    if more:
                        keys(ni, nj, (0, 1))
                    turned(i, j)
                    if more:
                        keys(ni, nj, (2, 3))
                    if j == 0 and not first:
                        output(i - 1)
                    if more:
                        maxima(ni, nj, (0, 1))
                    if j == 1 and not first:
                        residual(i - 1)
                    if more:
                        last_key(ni, nj)
                        normalise(ni, nj, 0)
                        maxima(ni, nj, (2, 3))
                        normalise(ni, nj, 1)
                        last_halves(ni, nj)

            tile(0, first=True)
            with dve.Fori(1, TILES - 1) as i:
                tile(i)
            tile(TILES - 1, last=True)
            output(TILES - 1)
            residual(TILES - 1)


def attention_phase(nc, tag, layers, scale, w_d, bias_d, bo_d, xn_d, x_d, y_d, routed=None):
    with ExitStack() as ctx:
        sb, ps, sem = alloc(nc, ctx)
        w32 = [sb(f"{tag}_w32_{b}", [P, C, D]) for b in range(2)]
        w = [[sb(f"{tag}_w{m}_{k}", [P, C, D], F32R) for k in range(2)] for m in range(4)]
        bias = sb(f"{tag}_bias", [P, 3, C])
        bias_q = sb(f"{tag}_bias_q", [P, C])
        bo = sb(f"{tag}_bo", [P, D])
        xn = [sb(f"{tag}_xn{k}", [P, C, N], F32R) for k in range(2)]
        qt = sb(f"{tag}_qt", [P, C, N])
        kb = sb(f"{tag}_kb", [P, C, SUP * TILE_SEQ, HG, LQ])
        v = sb(f"{tag}_v", [P, SUP, D])
        sc = [sb(f"{tag}_sc{b}", [P, H, LQ]) for b in range(2)]
        ex = [sb(f"{tag}_ex{b}", [P, H, LQ]) for b in range(2)]
        negmax = [sb(f"{tag}_negmax{b}", [P, H]) for b in range(2)]
        total = sb(f"{tag}_total", [P, H])
        inv = [sb(f"{tag}_inv{b}", [P, H]) for b in range(2)]
        pt = [sb(f"{tag}_pt{b}", [P, H, P]) for b in range(2)]
        ot = [sb(f"{tag}_ot{b}", [P, C, P]) for b in range(2)]
        oth = [[sb(f"{tag}_oth{b}_{k}", [P, C, P], F32R) for k in range(2)] for b in range(2)]
        x = [sb(f"{tag}_x{b}", [P, D]) for b in range(2)]
        y = [sb(f"{tag}_y{b}", [P, D]) for b in range(2)]
        yb = [sb(f"{tag}_yb{b}", [P, D]) for b in range(2)]
        if routed:
            mask_d, wt_d = routed
            mask = sb(f"{tag}_mask", [P, SUP, LQ])
            wt = sb(f"{tag}_wt", [P, SUP])

        bank_p = [ps(f"{tag}_bank_p{k}") for k in range(4)]
        bank_s = [ps(f"{tag}_bank_s{k}") for k in range(2)]
        bank_o = [ps(f"{tag}_bank_o{k}") for k in range(2)]

        s_seen = sem(f"{tag}_s_seen")
        s_w_in = [sem(f"{tag}_s_w_in{b}") for b in range(2)]
        s_w_hi = sem(f"{tag}_s_w_hi")
        s_w_split = sem(f"{tag}_s_w_split")
        s_b_in = sem(f"{tag}_s_b_in")
        s_bias_q = sem(f"{tag}_s_bias_q")
        s_zero = sem(f"{tag}_s_zero")
        s_xn_in = sem(f"{tag}_s_xn_in")
        s_m_in = sem(f"{tag}_s_m_in")
        s_x_in = [sem(f"{tag}_s_x_in{b}") for b in range(2)]
        s_prod = [sem(f"{tag}_s_prod{k}") for k in range(4)]
        s_taken = [sem(f"{tag}_s_taken{k}") for k in range(4)]
        s_scores = [sem(f"{tag}_s_scores{b}") for b in range(2)]
        s_s_free = [sem(f"{tag}_s_s_free{b}") for b in range(2)]
        s_max = sem(f"{tag}_s_max")
        s_shift = sem(f"{tag}_s_shift")
        s_exp = sem(f"{tag}_s_exp")
        s_total = sem(f"{tag}_s_total")
        s_inv = sem(f"{tag}_s_inv")
        s_norm = sem(f"{tag}_s_norm")
        s_pt = sem(f"{tag}_s_pt")
        s_sums = [sem(f"{tag}_s_sums{b}") for b in range(2)]
        s_o_free = [sem(f"{tag}_s_o_free{b}") for b in range(2)]
        s_o_hi = sem(f"{tag}_s_o_hi")
        s_o_split = sem(f"{tag}_s_o_split")
        s_y = sem(f"{tag}_s_y")
        s_out = [sem(f"{tag}_s_out{b}") for b in range(2)]

        block = ctx.enter_context(nc.Block())

        def supertiles(eng, layer, body):
            if layers == 1:
                layer(0)
                with eng.Fori(0, SUPERS) as s:
                    body(0, s, s)
            else:
                with eng.Fori(0, layers) as e:
                    layer(e)
                    with eng.Fori(0, SUPERS) as s:
                        body(e, s, e * SUPERS + s)

        @block.sync
        def _(sp):
            sp.sem_inc(s_y, 2)
            for b in range(2):
                sp.sem_inc(s_out[b], 16)

            def load_w(e, m, n):
                wait(sp, s_seen, (s_w_split, n + 1))
                sp.dma_start(w32[m % 2][:], w_d[e, m]).then_inc(s_w_in[m % 2], 16)

            def layer(e):
                load_w(e, 2, e * 4 + 2)
                load_w(e, 3, e * 4 + 3)
                wait(sp, s_seen, (s_y, e * (SUPERS * SUP) + 2))
                sp.dma_start(bias[:], bias_d[e]).then_inc(s_b_in, 16)
                sp.dma_start(bo[:], bo_d[e].broadcast_to([P, D])).then_inc(s_b_in, 16)
                if layers > 1:
                    load_w((e + 1) % layers, 0, e * 4 + 4)
                    load_w((e + 1) % layers, 1, e * 4 + 5)

            def body(e, s, i):
                def store(t):
                    wait(sp, s_seen, (s_y, SUP * i + t + 3))
                    sp.dma_start(y_d[s * SUP + t], y[t % 2][:]).then_inc(s_out[t % 2], 16)

                if routed:
                    wait(sp, s_seen, (s_y, SUP * i + 2))
                    sp.dma_start(mask[:], mask_d[:, e, bass.ds(s * SUP, SUP), :]).then_inc(s_m_in, 16)
                    sp.dma_start(wt[:], wt_d[:, e, bass.ds(s * SUP, SUP)]).then_inc(s_m_in, 16)
                for t in range(SUP):
                    wait(sp, s_seen, (s_y, SUP * i + t + 1))
                    sp.dma_start(x[t % 2][:], x_d[s * SUP + t]).then_inc(s_x_in[t % 2], 16)
                    if t >= 1:
                        store(t - 1)
                store(SUP - 1)

            load_w(0, 0, 0)
            load_w(0, 1, 1)
            supertiles(sp, layer, body)
            for b in range(2):
                sp.wait_ge(s_out[b], 16 * (layers * SUPERS * SUP // 2) + 16)
            if layers > 1:
                for b in range(2):
                    sp.wait_ge(s_w_in[b], 16 * (layers * 2 + 1))

        @block.gpsimd
        def _(pool):
            nc.gpsimd.memset(kb[:], 0.0).then_inc(s_zero, 1)
            for b in range(2):
                nc.gpsimd.memset(pt[b][:], 0.0).then_inc(s_zero, 1)

            def body(e, s, i):
                def normalise(t):
                    pool.wait_ge(s_inv, SUP * i + t + 1)
                    nc.gpsimd.tensor_tensor(ex[t % 2][:], ex[t % 2][:], bc_last(inv[t % 2][:], LQ), ALU.mult)\
                        .then_inc(s_norm, 1)

                def output_lo(t):
                    pool.wait_ge(s_o_hi, SUP * i + t + 1)
                    nc.gpsimd.tensor_tensor(oth[t % 2][1][:], ot[t % 2][:], oth[t % 2][0][:].bitcast(F32),
                                            ALU.subtract).then_inc(s_o_split, 1)

                normalise(0)
                normalise(1)
                normalise(2)
                output_lo(0)
                output_lo(1)
                normalise(3)
                output_lo(2)
                output_lo(3)

            supertiles(pool, lambda e: None, body)

        @block.tensor
        def _(pe):
            pe.wait_ge(s_zero, 3)

            def layer(e):
                wait(pe, s_seen, (s_w_split, e * 4 + 4 + 2))

            def body(e, s, i):
                def product(k, n, out, pairs):
                    pe.wait_ge(s_taken[k], 4 * i + n + 2)
                    for c in range(C):
                        for u, (a, b) in enumerate(PASSES):
                            lhs, rhs = pairs(c, a, b)
                            last = nc.tensor.matmul(out, lhs, rhs, start=(c == 0 and u == 0),
                                                    stop=(c == C - 1 and u == 2))
                    last.then_inc(s_prod[k], 1)

                def scores(t):
                    if t == 0:
                        for g in range(C):
                            pe.wait_ge(s_taken[g], 4 * i + 4)
                    pe.wait_ge(s_s_free[t % 2], (SUP // 2) * i + t // 2 + 1)
                    for b in range(TILE_SEQ):
                        for g in range(C):
                            last = nc.tensor.matmul(
                                bank_s[t % 2][LQ * b:LQ * b + LQ, g * P:(g + 1) * P],
                                qt[:, g, t * P + LQ * b:t * P + LQ * b + LQ], kb[:, g, t * TILE_SEQ + b, :, :],
                                start=True, stop=True, skip_group_check=True)
                    last.then_inc(s_scores[t % 2], 1)

                def sums(t):
                    pe.wait_ge(s_pt, SUP * i + t + 1)
                    pe.wait_ge(s_taken[t], 4 * i + 5)
                    pe.wait_ge(s_o_free[t % 2], (SUP // 2) * i + t // 2 + 1)
                    for h in range(H):
                        r = DH * (h % HG)
                        last = nc.tensor.matmul(bank_o[t % 2][r:r + DH, (h // HG) * P:(h // HG + 1) * P],
                                                v[:, t, h * DH:(h + 1) * DH], pt[t % 2][:, h, :],
                                                start=True, stop=True, skip_group_check=True)
                    last.then_inc(s_sums[t % 2], 1)

                def project(t):
                    pe.wait_ge(s_o_split, SUP * i + t + 1)
                    product(t, 3, bank_p[t][:], lambda c, a, b: (oth[t % 2][a][:, c, :], w[3][b][:, c, :]))

                pe.wait_ge(s_xn_in, 32 * i + 32)
                for m in range(2):
                    for g in range(C):
                        product(g, m, bank_p[g][:],
                                lambda c, a, b: (w[m][a][:, c, g * P:(g + 1) * P], xn[b][:, c, :]))
                for t in range(SUP):
                    scores(t)
                    product(t, 2, bank_p[t][:],
                            lambda c, a, b: (xn[a][:, c, t * P:(t + 1) * P], w[2][b][:, c, :]))
                sums(0)
                sums(1)
                project(0)
                sums(2)
                project(1)
                sums(3)
                project(2)
                project(3)

            supertiles(pe, layer, body)

        @block.scalar
        def _(act):
            for k in range(4):
                act.sem_inc(s_taken[k], 2)
            if not routed:
                for b in range(2):
                    act.sem_inc(s_s_free[b], 1)
            act.wait_ge(s_zero, 3)

            def load_xn(s):
                for k in range(2):
                    act.dma_start(xn[k][:].bitcast(F32), xn_d[s, k]).then_inc(s_xn_in, 16)

            load_xn(0)

            def layer(e):
                for m in range(4):
                    act.wait_ge(s_w_in[m % 2], e * 32 + (m // 2) * 16 + 16)
                    if layers > 1:
                        act.wait_ge(s_taken[3], e * (SUPERS * 4) + 2)
                    nc.scalar.activation(w[m][0][:], w32[m % 2][:], ACT.Copy).then_inc(s_w_hi, 1)
                act.wait_ge(s_b_in, e * 32 + 32)
                nc.scalar.activation(bias_q[:], bias[:, 0, :], ACT.Copy, scale=scale).then_inc(s_bias_q, 1)
                wait(act, s_seen, (s_bias_q, e + 1))

            def body(e, s, i):
                def exp(t):
                    act.wait_ge(s_shift, SUP * i + t + 1)
                    if not routed:
                        act.sem_inc(s_s_free[t % 2], 1)
                    nc.scalar.activation(ex[t % 2][:], sc[t % 2][:], ACT.Exp).then_inc(s_exp, 1)

                def values(t):
                    act.wait_ge(s_prod[t], 4 * i + 3)
                    nc.scalar.activation(v[:, t, :], bank_p[t][:], ACT.Copy).then_inc(s_taken[t], 1)

                def output_hi(t):
                    act.wait_ge(s_o_free[t % 2], (SUP // 2) * i + t // 2 + 2)
                    nc.scalar.activation(oth[t % 2][0][:], ot[t % 2][:], ACT.Copy).then_inc(s_o_hi, 1)

                for g in range(C):
                    act.wait_ge(s_prod[g], 4 * i + 1)
                    nc.scalar.activation(qt[:, g, :], bank_p[g][:], ACT.Identity, bias=bias_q[:, g:g + 1],
                                         scale=scale).then_inc(s_taken[g], 1)
                for g in range(C):
                    act.wait_ge(s_prod[g], 4 * i + 2)
                    for h in range(HG):
                        r = slice(DH * h, DH * h + DH)
                        last = nc.scalar.activation(kb[r, g, :, h, :],
                                                    bank_p[g][r, :].rearrange("p (b k) -> p b k", k=LQ),
                                                    ACT.Identity, bias=bias[r, 1, g:g + 1])
                    last.then_inc(s_taken[g], 1)
                values(0)
                exp(0)
                values(1)
                exp(1)
                values(2)
                values(3)
                load_xn((s + 1) % SUPERS)
                exp(2)
                output_hi(0)
                output_hi(1)
                exp(3)
                output_hi(2)
                output_hi(3)

            supertiles(act, layer, body)
            act.wait_ge(s_xn_in, 32 * (layers * SUPERS) + 32)

        @block.vector
        def _(dve):
            dve.sem_inc(s_w_split, 2)
            for b in range(2):
                dve.sem_inc(s_o_free[b], 1)
                if routed:
                    dve.sem_inc(s_s_free[b], 1)
            dve.wait_ge(s_zero, 3)

            def layer(e):
                for m in range(4):
                    dve.wait_ge(s_w_hi, e * 4 + m + 1)
                    nc.vector.tensor_tensor(w[m][1][:], w32[m % 2][:], w[m][0][:].bitcast(F32),
                                            ALU.subtract).then_inc(s_w_split, 1)
                wait(dve, s_seen, (s_b_in, e * 32 + 32))

            def body(e, s, i):
                def shift(t):
                    bank = bank_s[t % 2][:].rearrange("p (h k) -> p h k", h=H)
                    dve.wait_ge(s_scores[t % 2], (SUP // 2) * i + t // 2 + 1)
                    if routed:
                        if t == 0:
                            dve.wait_ge(s_m_in, 32 * i + 32)
                        nc.vector.tensor_tensor(sc[t % 2][:], bank, bc_mid(mask[:, t, :], H), ALU.add)\
                            .then_inc(s_s_free[t % 2], 1)
                        dve.wait_ge(s_s_free[t % 2], (SUP // 2) * i + t // 2 + 2)
                        bank = sc[t % 2][:]
                    nc.vector.tensor_reduce(negmax[t % 2][:], bank, X, ALU.max, negate=True).then_inc(s_max, 1)
                    dve.wait_ge(s_max, SUP * i + t + 1)
                    nc.vector.tensor_tensor(sc[t % 2][:], bank, bc_last(negmax[t % 2][:], LQ), ALU.add).then_inc(s_shift, 1)

                def total_of(t):
                    dve.wait_ge(s_exp, SUP * i + t + 1)
                    nc.vector.tensor_reduce(total[:], ex[t % 2][:], X, ALU.add).then_inc(s_total, 1)
                    dve.wait_ge(s_total, SUP * i + t + 1)
                    nc.vector.reciprocal(inv[t % 2][:], total[:]).then_inc(s_inv, 1)

                def turn(t):
                    dve.wait_ge(s_norm, SUP * i + t + 1)
                    for b in range(TILE_SEQ):
                        r = slice(LQ * b, LQ * b + LQ)
                        last = nc.vector.transpose(pt[t % 2][r, :, r], ex[t % 2][r, :, :])
                    last.then_inc(s_pt, 1)

                def output(t):
                    dve.wait_ge(s_sums[t % 2], (SUP // 2) * i + t // 2 + 1)
                    nc.vector.tensor_tensor(ot[t % 2][:], bank_o[t % 2][:].rearrange("p (g n) -> p g n", g=C),
                                            bc_last(bias[:, 2, :], P), ALU.add).then_inc(s_o_free[t % 2], 1)

                def residual(t):
                    dve.wait_ge(s_prod[t], 4 * i + 4)
                    dve.wait_ge(s_y, SUP * i + t + 1)
                    nc.vector.tensor_tensor(yb[t % 2][:], bank_p[t][:], bo[:], ALU.add).then_inc(s_taken[t], 1)
                    dve.wait_ge(s_taken[t], 4 * i + 6)
                    dve.wait_ge(s_x_in[t % 2], 16 * ((SUP // 2) * i + t // 2) + 16)
                    dve.wait_ge(s_out[t % 2], 16 * ((SUP // 2) * i + t // 2) + 16)
                    if routed:
                        nc.vector.scalar_tensor_tensor(out=y[t % 2][:], in0=yb[t % 2][:], scalar=wt[:, t:t + 1],
                                                       in1=x[t % 2][:], op0=ALU.mult, op1=ALU.add).then_inc(s_y, 1)
                    else:
                        nc.vector.tensor_tensor(y[t % 2][:], yb[t % 2][:], x[t % 2][:], ALU.add).then_inc(s_y, 1)

                shift(0)
                shift(1)
                total_of(0)
                turn(0)
                shift(2)
                total_of(1)
                turn(1)
                shift(3)
                total_of(2)
                output(0)
                turn(2)
                output(1)
                total_of(3)
                residual(0)
                turn(3)
                output(2)
                residual(1)
                output(3)
                residual(2)
                residual(3)

            supertiles(dve, layer, body)


def router_phase(nc, logit_d, mask_d, wt_d):
    ALL = TILES * EXPERTS
    with ExitStack() as ctx:
        sb, ps, sem = alloc(nc, ctx)
        logit = sb("r_logit", [P, TILES, EXPERTS])
        top = sb("r_top", [P, TILES])
        total = sb("r_total", [P, TILES])
        inv = sb("r_inv", [P, TILES])
        prob = sb("r_prob", [P, TILES, EXPERTS])
        above = sb("r_above", [P, TILES, EXPERTS, EXPERTS])
        tied = sb("r_tied", [P, TILES, EXPERTS, EXPERTS])
        before = sb("r_before", [P, EXPERTS, EXPERTS])
        rank = sb("r_rank", [P, TILES, EXPERTS])
        member = sb("r_member", [P, TILES, EXPERTS])
        wt = sb("r_wt", [P, EXPERTS, TILES])
        mask = sb("r_mask", [P, EXPERTS, TILES, LQ])
        ident = sb("r_ident", [P, P])
        place = sb("r_place", [P, LQ])
        own = sb("r_own", [P, TILE_SEQ])
        same = sb("r_same", [P, P])
        spread = [sb(f"r_spread{b}", [P, SUP, EXPERTS, LQ]) for b in range(2)]
        bank = [ps(f"r_bank{b}") for b in range(2)]

        s_in = sem("r_s_in")
        s_const = sem("r_s_const")
        s_dve = sem("r_s_dve")
        s_exp = sem("r_s_exp")
        s_spread = sem("r_s_spread")
        s_mask = sem("r_s_mask")
        s_taken = sem("r_s_taken")
        s_out = sem("r_s_out")

        block = ctx.enter_context(nc.Block())
        steps = [0]

        @block.sync
        def _(sp):
            sp.dma_start(logit[:], logit_d).then_inc(s_in, 16)
            sp.wait_ge(s_taken, SUPERS)
            sp.dma_start(mask_d, mask[:]).then_inc(s_out, 16)
            sp.dma_start(wt_d, wt[:]).then_inc(s_out, 16)
            sp.wait_ge(s_out, 32)

        @block.gpsimd
        def _(pool):
            nc.gpsimd.memset(ident[:], 0.0).then_inc(s_const, 1)
            nc.gpsimd.memset(own[:], 1.0).then_inc(s_const, 1)
            nc.gpsimd.memset(before[:], 0.0).then_inc(s_const, 1)
            pool.wait_ge(s_const, 3)
            nc.gpsimd.affine_select(out=ident[:], in_=ident[:], compare_op=ALU.not_equal, fill=1.0, base=0,
                                    pattern=[[-1, P]], channel_multiplier=1).then_inc(s_const, 1)
            nc.gpsimd.affine_select(out=own[:], in_=own[:], compare_op=ALU.is_ge, fill=0.0, base=0,
                                    pattern=[[-LQ, TILE_SEQ]], channel_multiplier=1).then_inc(s_const, 1)
            for e in range(1, EXPERTS):
                nc.gpsimd.memset(before[:, e, 0:e], 1.0).then_inc(s_const, 1)
            pool.wait_ge(s_const, 5 + EXPERTS - 1)
            nc.gpsimd.affine_select(out=own[:], in_=own[:], compare_op=ALU.is_ge, fill=0.0, base=LQ - 1,
                                    pattern=[[LQ, TILE_SEQ]], channel_multiplier=-1).then_inc(s_const, 1)

        @block.scalar
        def _(act):
            act.wait_ge(s_dve, 2)
            nc.scalar.activation(prob[:], logit[:], ACT.Exp).then_inc(s_exp, 1)

        @block.vector
        def _(dve):
            def step(ins):
                steps[0] += 1
                ins.then_inc(s_dve, 1)
                dve.wait_ge(s_dve, steps[0])

            dve.wait_ge(s_in, 16)
            step(nc.vector.tensor_reduce(top[:], logit[:], X, ALU.max, negate=True))
            step(nc.vector.tensor_tensor(logit[:], logit[:], bc_last(top[:], EXPERTS), ALU.add))
            dve.wait_ge(s_exp, 1)
            step(nc.vector.tensor_reduce(total[:], prob[:], X, ALU.add))
            step(nc.vector.reciprocal(inv[:], total[:]))
            step(nc.vector.tensor_tensor(prob[:], prob[:], bc_last(inv[:], EXPERTS), ALU.mult))
            wide = [P, TILES, EXPERTS, EXPERTS]
            other = prob[:].unsqueeze(2).broadcast_to(wide)
            mine = prob[:].unsqueeze(3).broadcast_to(wide)
            step(nc.vector.tensor_tensor(above[:], other, mine, ALU.is_gt))
            step(nc.vector.tensor_tensor(tied[:], other, mine, ALU.is_equal))
            dve.wait_ge(s_const, 6 + EXPERTS - 1)
            step(nc.vector.tensor_tensor(tied[:], tied[:], before[:].unsqueeze(1).broadcast_to(wide), ALU.mult))
            step(nc.vector.tensor_tensor(above[:], above[:], tied[:], ALU.add))
            step(nc.vector.tensor_reduce(rank[:], above[:], X, ALU.add))
            step(nc.vector.tensor_scalar(member[:], rank[:], 1.5, None, ALU.is_lt))
            step(nc.vector.tensor_tensor(wt[:].rearrange("p e t -> p t e"), prob[:], member[:], ALU.mult))
            step(nc.vector.tensor_tensor(place[:], ident[:, 0:LQ], ident[:, LQ:2 * LQ], ALU.add))
            step(nc.vector.tensor_tensor(place[:], place[:], ident[:, 2 * LQ:3 * LQ], ALU.add))
            step(nc.vector.tensor_tensor(place[:], place[:], ident[:, 3 * LQ:4 * LQ], ALU.add))
            step(nc.vector.tensor_copy(same[:].rearrange("p (b q) -> p b q", b=TILE_SEQ), bc_last(own[:], LQ)))
            for s in range(SUPERS):
                if s >= 2:
                    dve.wait_ge(s_mask, s - 1)
                nc.vector.tensor_tensor(
                    spread[s % 2][:].rearrange("p t e q -> p (t e) q"),
                    bc_last(member[:, s * SUP:(s + 1) * SUP, :].rearrange("p t e -> p (t e)"), LQ),
                    bc_mid(place[:], SUP * EXPERTS), ALU.mult).then_inc(s_spread, 1)
                dve.wait_ge(s_mask, s + 1)
                nc.vector.tensor_scalar(mask[:, :, s * SUP:(s + 1) * SUP, :].rearrange("p e t q -> p t e q"),
                                        bank[s % 2][:].rearrange("p (t e q) -> p t e q", t=SUP, e=EXPERTS),
                                        -1.0, MASKED, ALU.add, ALU.mult).then_inc(s_taken, 1)

        @block.tensor
        def _(pe):
            for s in range(SUPERS):
                pe.wait_ge(s_spread, s + 1)
                if s >= 2:
                    pe.wait_ge(s_taken, s - 1)
                nc.tensor.matmul(bank[s % 2][:], same[:], spread[s % 2][:].rearrange("p t e q -> p (t e q)"),
                                 start=True, stop=True).then_inc(s_mask, 1)


def program(nc, x, ctx, ctx_t, w, w_k, w_v, bias_p, bias_o, r_w, r_b, out):
    x_t = x.rearrange("(t p) d -> t p d", p=P)
    out_t = out.rearrange("(t p) d -> t p d", p=P)
    q_d = nc.dram_tensor("q_scratch", (P, C, TOK), F32).ap()
    xn_d = nc.dram_tensor("xn_scratch", (SUPERS, 2, P, C, N), F32).ap()
    x1_d = nc.dram_tensor("x1_scratch", (TILES, P, D), F32).ap()
    xn2_d = nc.dram_tensor("xn2_scratch", (SUPERS, 2, P, C, N), F32).ap()
    logit_d = nc.dram_tensor("logit_scratch", (P, TILES, EXPERTS), F32).ap()
    mask_d = nc.dram_tensor("mask_scratch", (P, EXPERTS, TILES, LQ), F32).ap()
    wt_d = nc.dram_tensor("wt_scratch", (P, EXPERTS, TILES), F32).ap()
    norm_phase(nc, "n0", x_t, None, q=(w[0], bias_p[0, :, 0], q_d))
    cross_phase(nc, x_t, q_d, ctx, ctx_t, w_k, w_v, w[1], bias_p[0], bias_o[0:1], x1_d)
    norm_phase(nc, "n1", x1_d, xn_d)
    attention_phase(nc, "a", 1, SELF_SCALE, w[2:6].rearrange("(l m) p c n -> l m p c n", m=4), bias_p[1:2],
                    bias_o[1:2].unsqueeze(1), xn_d, x1_d, out_t)
    norm_phase(nc, "n2", out_t, xn2_d, router=(r_w, r_b.broadcast_to([P, EXPERTS]), logit_d))
    router_phase(nc, logit_d, mask_d, wt_d)
    attention_phase(nc, "e", EXPERTS, EXPERT_SCALE, w[6:6 + 4 * EXPERTS].rearrange("(l m) p c n -> l m p c n", m=4),
                    bias_p[2:2 + EXPERTS], bias_o[2:2 + EXPERTS].unsqueeze(1), xn2_d, out_t, out_t,
                    routed=(mask_d, wt_d))


def kernel(**inputs):
    import numpy as np
    import concourse.bacc as bacc
    from concourse.bass_utils import run_bass_kernel_spmd as run

    a = {k: np.ascontiguousarray(v) for k, v in inputs.items()}

    def rows(w):
        return np.ascontiguousarray(w.reshape(-1, P, w.shape[-1]).transpose(1, 0, 2))

    def cols(*biases):
        return np.ascontiguousarray(np.stack([b.reshape(C, P).T for b in biases], axis=1))

    qkv, bqkv = a["L0_attn_w_qkv"], a["L0_attn_b_qkv"]
    w = [a["L0_xattn_Wq"], a["L0_xattn_Wo"]]
    w += [qkv[:, k * D:(k + 1) * D] for k in range(3)] + [a["L0_attn_w_proj"]]
    bias_p = [cols(a["L0_xattn_bq"], a["L0_xattn_bk"], a["L0_xattn_bv"]),
              cols(*[bqkv[k * D:(k + 1) * D] for k in range(3)])]
    bias_o = [a["L0_xattn_bo"], a["L0_attn_b_proj"]]
    for e in range(EXPERTS):
        w += [a[f"L0_ffn_w{k}"][e] for k in "qkvo"]
        bias_p.append(cols(*[a[f"L0_ffn_b{k}"][e] for k in "qkv"]))
        bias_o.append(a["L0_ffn_bo"][e])
    arrays = {
        "x": a["x"].reshape(TOK, D),
        "ctx": a["ctx_512"],
        "ctx_t": np.ascontiguousarray(a["ctx_512"].reshape(BATCH, LK, CC, P).transpose(0, 3, 2, 1)),
        "w": np.stack([rows(m) for m in w]),
        "w_k": rows(a["L0_xattn_Wk"]),
        "w_v": rows(a["L0_xattn_Wv"]),
        "bias_p": np.stack(bias_p),
        "bias_o": np.stack(bias_o),
        "r_w": rows(a["L0_ffn_router_w"]),
        "r_b": a["L0_ffn_router_b"].reshape(1, EXPERTS),
    }
    nc = bacc.Bacc("TRN2", target_bir_lowering=False, num_devices=1)
    args = [nc.dram_tensor(k, v.shape, F32, kind="ExternalInput").ap() for k, v in arrays.items()]
    args.append(nc.dram_tensor("out", (TOK, D), F32, kind="ExternalOutput").ap())
    program(nc, *args)
    r = run(nc, [arrays], core_ids=[0])
    return r.results[0]["out"].reshape(BATCH, LQ, D)
```

```python
from contextlib import ExitStack

import concourse.bass as bass
from concourse import mybir

F32 = mybir.dt.float32
F32R = mybir.dt.float32r
ALU = mybir.AluOpType
ACT = mybir.ActivationFunctionType
X = mybir.AxisListType.X

P = 128
BATCH = 128
LQ = 32
D = 512
H = 16
DH = D // H
C = D // P
HG = P // DH
LK = 257
LKE = LK + 1
DC = 256
CC = DC // P
TOK = BATCH * LQ
TILE_SEQ = P // LQ
TILES = TOK // P
SUP = 4
N = SUP * P
SUPERS = TOK // N
EXPERTS = 4
LAYERS = 1 + EXPERTS
EPS = 1e-5
CROSS_SCALE = float(DH) ** -0.5
SELF_SCALE = float(DH) ** -0.5
EXPERT_SCALE = 0.5
MASKED = 1.0e9
PASSES = ((0, 0), (0, 1), (1, 0))


def alloc(nc, ctx):
    sems = []

    def clear():
        nc.clear_and_free_semaphores(sems)
        nc.all_engine_barrier()

    ctx.callback(clear)

    def sb(name, shape, dt=F32):
        return ctx.enter_context(nc.sbuf_tensor(name, shape, dt))

    def ps(name):
        return ctx.enter_context(nc.psum_tensor(name, [P, 512], F32))

    def sem(name):
        sems.append(nc.alloc_semaphore(name=name))
        return sems[-1]

    return sb, ps, sem


def wait(eng, seen, *waits):
    for s, value in waits:
        eng.wait_ge(s, value)
        eng.sem_inc(seen, 1)


def bc_mid(ap, n):
    return ap.unsqueeze(1).broadcast_to([ap.shape[0], n, ap.shape[1]])


def bc_last(ap, n):
    return ap.unsqueeze(2).broadcast_to([ap.shape[0], ap.shape[1], n])


def norm_phase(nc, tag, x_d, xn_d, q=None, router=None):
    with ExitStack() as ctx:
        sb, ps, sem = alloc(nc, ctx)
        x = sb(f"{tag}_x", [P, SUP, D])
        xn = sb(f"{tag}_xn", [P, SUP, D])
        xt = [sb(f"{tag}_xt{k}", [P, C, N], F32R) for k in range(2)]
        stats = sb(f"{tag}_stats", [P, SUP, 6])
        mv = sb(f"{tag}_mv", [P, SUP, 2])
        var_eps = sb(f"{tag}_vareps", [P, SUP])
        rstd = sb(f"{tag}_rstd", [P, SUP])
        power = sb(f"{tag}_power", [P, SUP])
        ident = sb(f"{tag}_ident", [P, P])
        turned = [ps(f"{tag}_turned{k}") for k in range(2)]
        prod = [ps(f"{tag}_prod{k}") for k in range(C)]
        if q:
            w_d, b_d, q_d = q
            w32 = sb(f"{tag}_w32", [P, C, D])
            w = [sb(f"{tag}_w{k}", [P, C, D], F32R) for k in range(2)]
            bias = sb(f"{tag}_bias", [P, C])
            bias_s = sb(f"{tag}_bias_s", [P, C])
            qt = sb(f"{tag}_qt", [P, C, N])
        if router:
            rw_d, rb_d, logit_d = router
            rw32 = sb(f"{tag}_rw32", [P, C, EXPERTS])
            rw = [sb(f"{tag}_rw{k}", [P, C, EXPERTS], F32R) for k in range(2)]
            rb = sb(f"{tag}_rb", [P, EXPERTS])
            logit = sb(f"{tag}_logit", [P, SUP, EXPERTS])

        s_seen = sem(f"{tag}_s_seen")
        s_ident = sem(f"{tag}_s_ident")
        s_w_in = sem(f"{tag}_s_w_in")
        s_w_hi = sem(f"{tag}_s_w_hi")
        s_w_split = sem(f"{tag}_s_w_split")
        s_x_in = sem(f"{tag}_s_x_in")
        s_stats = sem(f"{tag}_s_stats")
        s_mv = sem(f"{tag}_s_mv")
        s_eps = sem(f"{tag}_s_eps")
        s_rstd = sem(f"{tag}_s_rstd")
        s_xn = sem(f"{tag}_s_xn")
        s_turned = [sem(f"{tag}_s_turned{k}") for k in range(2)]
        s_hi = sem(f"{tag}_s_hi")
        s_split = [sem(f"{tag}_s_split{k}") for k in range(2)]
        s_prod = sem(f"{tag}_s_prod")
        s_taken = sem(f"{tag}_s_taken")
        s_out = sem(f"{tag}_s_out")
        outs = 1 if q else 2 + bool(router)
        prods = C if q else SUP if router else 0

        block = ctx.enter_context(nc.Block())

        @block.sync
        def _(sp):
            if q:
                sp.dma_start(w32[:], w_d).then_inc(s_w_in, 16)
                sp.dma_start(bias[:], b_d).then_inc(s_w_in, 16)
            if router:
                sp.dma_start(rw32[:], rw_d).then_inc(s_w_in, 16)
                sp.dma_start(rb[:], rb_d).then_inc(s_w_in, 16)
            sp.sem_inc(s_xn, 1)
            with sp.Fori(0, SUPERS) as s:
                wait(sp, s_seen, (s_xn, s * SUP + 1))
                sp.dma_start(x[:], x_d[bass.ds(s * SUP, SUP)].rearrange("t p d -> p t d")).then_inc(s_x_in, 16)

        @block.gpsimd
        def _(pool):
            nc.gpsimd.memset(ident[:], 0.0).then_inc(s_ident, 1)
            nc.gpsimd.memset(power[:], -0.5).then_inc(s_ident, 1)
            pool.wait_ge(s_ident, 2)
            nc.gpsimd.affine_select(out=ident[:], in_=ident[:], compare_op=ALU.not_equal, fill=1.0, base=0,
                                    pattern=[[-1, P]], channel_multiplier=1).then_inc(s_ident, 1)
            with pool.Fori(0, SUPERS) as s:
                wait(pool, s_seen, (s_mv, s * SUP + SUP))
                nc.gpsimd.tensor_scalar(var_eps[:], mv[:, :, 1], EPS, 1.0, ALU.add, ALU.mult).then_inc(s_eps, 1)
                pool.wait_ge(s_eps, s + 1)
                nc.gpsimd.tensor_tensor(rstd[:], var_eps[:], power[:], ALU.pow).then_inc(s_rstd, 1)

        @block.vector
        def _(dve):
            if q:
                dve.wait_ge(s_w_hi, 1)
                nc.vector.tensor_tensor(w[1][:], w32[:], w[0][:].bitcast(F32), ALU.subtract).then_inc(s_w_split, 1)
                nc.vector.tensor_scalar(bias_s[:], bias[:], CROSS_SCALE, None, ALU.mult).then_inc(s_w_split, 1)
            if router:
                dve.wait_ge(s_w_hi, 1)
                nc.vector.tensor_tensor(rw[1][:], rw32[:], rw[0][:].bitcast(F32), ALU.subtract).then_inc(s_w_split, 1)
            dve.sem_inc(s_split[0], 1)
            dve.sem_inc(s_split[1], 1)
            with dve.Fori(0, SUPERS) as s:
                dve.wait_ge(s_x_in, s * 16 + 16)
                for t in range(SUP):
                    nc.vector.bn_stats(stats[:, t, :], x[:, t, :]).then_inc(s_stats, 1)
                for t in range(SUP):
                    wait(dve, s_seen, (s_stats, s * SUP + t + 1))
                    nc.vector.bn_aggr(mv[:, t, :], stats[:, t, :]).then_inc(s_mv, 1)
                dve.wait_ge(s_rstd, s + 1)
                for t in range(SUP):
                    nc.vector.tensor_scalar(xn[:, t, :], x[:, t, :], mv[:, t, 0:1], rstd[:, t:t + 1],
                                            ALU.subtract, ALU.mult).then_inc(s_xn, 1)
                for t in range(SUP):
                    dve.wait_ge(s_hi, s * SUP + t + 1)
                    nc.vector.tensor_tensor(xt[1][:, :, t * P:(t + 1) * P],
                                            turned[t % 2][:].rearrange("p (c n) -> p c n", c=C),
                                            xt[0][:, :, t * P:(t + 1) * P].bitcast(F32),
                                            ALU.subtract).then_inc(s_split[t % 2], 1)
                if router:
                    for t in range(SUP):
                        dve.wait_ge(s_prod, s * prods + t + 1)
                        if t == 0:
                            dve.wait_ge(s_out, s * (16 * outs) + 16)
                        nc.vector.tensor_tensor(logit[:, t, :], prod[t][:, 0:EXPERTS], rb[:], ALU.add)\
                            .then_inc(s_taken, 1)

        @block.tensor
        def _(pe):
            pe.wait_ge(s_ident, 3)
            with pe.Fori(0, SUPERS) as s:
                for t in range(SUP):
                    pe.wait_ge(s_xn, s * SUP + t + 2)
                    pe.wait_ge(s_split[t % 2], s * (SUP // 2) + t // 2 + 1)
                    for c in range(C):
                        last = nc.tensor.transpose(turned[t % 2][:, c * P:(c + 1) * P], xn[:, t, c * P:(c + 1) * P],
                                                   ident[:])
                    last.then_inc(s_turned[t % 2], 1)
                if q or router:
                    for k in range(2):
                        pe.wait_ge(s_split[k], s * (SUP // 2) + SUP // 2 + 1)
                if q:
                    pe.wait_ge(s_w_split, 1)
                    for g in range(C):
                        pe.wait_ge(s_taken, s * C + 1)
                        for c in range(C):
                            for n, (a, b) in enumerate(PASSES):
                                last = nc.tensor.matmul(prod[g][:], w[a][:, c, g * P:(g + 1) * P], xt[b][:, c, :],
                                                        start=(c == 0 and n == 0), stop=(c == C - 1 and n == 2))
                        last.then_inc(s_prod, 1)
                if router:
                    pe.wait_ge(s_w_split, 1)
                    pe.wait_ge(s_taken, s * SUP + 1)
                    for t in range(SUP):
                        for c in range(C):
                            for n, (a, b) in enumerate(PASSES):
                                last = nc.tensor.matmul(prod[t][:, 0:EXPERTS], xt[a][:, c, t * P:(t + 1) * P],
                                                        rw[b][:, c, :], start=(c == 0 and n == 0),
                                                        stop=(c == C - 1 and n == 2))
                        last.then_inc(s_prod, 1)

        @block.scalar
        def _(act):
            if q or router:
                act.wait_ge(s_w_in, 32)
                src, dst = (w32, w[0]) if q else (rw32, rw[0])
                nc.scalar.activation(dst[:], src[:], ACT.Copy).then_inc(s_w_hi, 1)
            act.sem_inc(s_taken, 1)
            act.sem_inc(s_out, 16)
            with act.Fori(0, SUPERS) as s:
                for t in range(SUP):
                    act.wait_ge(s_turned[t % 2], s * (SUP // 2) + t // 2 + 1)
                    if t == 0 and q:
                        act.wait_ge(s_taken, s * C + 1)
                    elif t == 0:
                        act.wait_ge(s_out, s * (16 * outs) + 16)
                    nc.scalar.activation(xt[0][:, :, t * P:(t + 1) * P],
                                         turned[t % 2][:].rearrange("p (c n) -> p c n", c=C),
                                         ACT.Copy).then_inc(s_hi, 1)
                if q:
                    act.wait_ge(s_w_split, 2)
                    act.wait_ge(s_out, s * 16 + 16)
                    for g in range(C):
                        act.wait_ge(s_prod, s * C + g + 1)
                        nc.scalar.activation(qt[:, g, :], prod[g][:], ACT.Identity, bias=bias_s[:, g:g + 1],
                                             scale=CROSS_SCALE).then_inc(s_taken, 1)
                    act.wait_ge(s_taken, s * C + C + 1)
                    act.dma_start(q_d[:, :, bass.ds(s * N, N)], qt[:]).then_inc(s_out, 16)
                else:
                    for k in range(2):
                        act.wait_ge(s_split[k], s * (SUP // 2) + SUP // 2 + 1)
                    for k in range(2):
                        act.dma_start(xn_d[s, k], xt[k][:].bitcast(F32)).then_inc(s_out, 16)
                    if router:
                        act.wait_ge(s_taken, s * SUP + SUP + 1)
                        act.dma_start(logit_d[:, bass.ds(s * SUP, SUP), :], logit[:]).then_inc(s_out, 16)
            act.wait_ge(s_out, SUPERS * 16 * outs + 16)


def cross_phase(nc, x_d, q_d, ctx_d, ctx_t_d, wk_d, wv_d, wo_d, bias_d, bo_d, x1_d):
    B = TILE_SEQ
    with ExitStack() as ctx:
        sb, ps, sem = alloc(nc, ctx)
        wk32 = sb("c_wk32", [P, CC, D])
        wk = [sb(f"c_wk{k}", [P, CC, D], F32R) for k in range(2)]
        wv = sb("c_wv", [P, CC, D])
        wo32 = sb("c_wo32", [P, C, D])
        wo = [sb(f"c_wo{k}", [P, C, D], F32R) for k in range(2)]
        bias = sb("c_bias", [P, 3, C])
        bo = sb("c_bo", [P, D])
        ident = sb("c_ident", [P, P])
        ct = [sb(f"c_ct{b}", [P, CC, LK]) for b in range(2)]
        cn = [sb(f"c_cn{b}", [P, 2, DC]) for b in range(2)]
        c1 = [sb(f"c_cl{b}", [96, DC]) for b in range(2)]
        cth = [[sb(f"c_cth{b}_{k}", [P, CC, LKE], F32R) for k in range(2)] for b in range(2)]
        cnh = [[sb(f"c_cnh{b}_{k}", [P, 2, DC], F32R) for k in range(2)] for b in range(2)]
        c1h = [sb(f"c_clh{b}", [96, DC], F32R) for b in range(2)]
        qt = sb("c_qt", [P, C, P])
        qs = [sb(f"c_qs{k}", [P, C, P], F32R) for k in range(2)]
        own = sb("c_own", [P, HG])
        qh = [[sb(f"c_qh{b}_{k}", [P, C, HG, LQ], F32R) for k in range(2)] for b in range(2)]
        kt = [sb(f"c_kt{k}", [P, C, LKE], F32R) for k in range(2)]
        negmax = sb("c_negmax", [P, C])
        total = sb("c_total", [P, C])
        inv = sb("c_inv", [P, C])
        probs = sb("c_probs", [P, C, LK])
        last_p = sb("c_last_p", [P, C, 96], F32R)
        pt = [sb(f"c_pt{k}", [P, 2, C * P], F32R) for k in range(2)]
        p1 = sb("c_p1", [96, C * P], F32R)
        mix = sb("c_mix", [P, CC, H, B, LQ])
        ot = sb("c_ot", [P, C, P])
        oth = [sb(f"c_oth{k}", [P, C, P], F32R) for k in range(2)]
        xt = [sb(f"c_xt{b}", [P, D]) for b in range(2)]
        xb = sb("c_xb", [P, D])
        x1 = sb("c_x1", [P, D])

        bank_k = [ps(f"c_bank_k{b}") for b in range(2)]
        bank_s = [ps(f"c_bank_s{b}") for b in range(2)]
        bank_t = [ps(f"c_bank_t{b}") for b in range(2)]
        bank_v = [ps(f"c_bank_v{b}") for b in range(2)]

        s_seen = sem("c_s_seen")
        s_w_in = sem("c_s_w_in")
        s_w_hi = sem("c_s_w_hi")
        s_w_split = sem("c_s_w_split")
        s_const = sem("c_s_const")
        s_zero = sem("c_s_zero")
        s_ctx_in = [sem(f"c_s_ctx_in{b}") for b in range(2)]
        s_q_in = sem("c_s_q_in")
        s_x_in = sem("c_s_x_in")
        s_ctx_hi = sem("c_s_ctx_hi")
        s_c1_hi = sem("c_s_c1_hi")
        s_c1_split = sem("c_s_c1_split")
        s_ctx_split = sem("c_s_ctx_split")
        s_q_hi = sem("c_s_q_hi")
        s_q_split = sem("c_s_q_split")
        s_k = [sem(f"c_s_k{b}") for b in range(2)]
        s_k_hi = sem("c_s_k_hi")
        s_k_split = [sem(f"c_s_k_split{b}") for b in range(2)]
        s_s = [sem(f"c_s_s{b}") for b in range(2)]
        s_max = sem("c_s_max")
        s_exp = [sem(f"c_s_exp{b}") for b in range(2)]
        s_inv = sem("c_s_inv")
        s_norm = sem("c_s_norm")
        s_last = sem("c_s_last")
        s_probs = sem("c_s_probs")
        s_t = [sem(f"c_s_t{b}") for b in range(2)]
        s_t_hi = sem("c_s_t_hi")
        s_t_split = [sem(f"c_s_t_split{b}") for b in range(2)]
        s_v = [sem(f"c_s_v{b}") for b in range(2)]
        s_v_taken = [sem(f"c_s_v_taken{b}") for b in range(2)]
        s_o_hi = sem("c_s_o_hi")
        s_o_split = sem("c_s_o_split")
        s_xb = sem("c_s_xb")
        s_x1 = sem("c_s_x1")
        s_out = sem("c_s_out")

        def v0_output(i):
            return i * (B + 1) - 1

        def v1_project(i):
            if isinstance(i, int) and i == TILES:
                return i * (B + 1) - 1
            return i * (B + 1)

        def v_before(i, j, bank):
            ahead = 1 if bank == 0 or j >= 1 else 0
            if isinstance(i, int) and i == 0:
                return j
            return i * (B + 1) - 1 + j + ahead

        block = ctx.enter_context(nc.Block())

        @block.sync
        def _(sp):
            sp.dma_start(wk32[:], wk_d).then_inc(s_w_in, 16)
            sp.dma_start(bias[:], bias_d).then_inc(s_w_in, 16)
            sp.dma_start(wo32[:], wo_d).then_inc(s_w_in, 16)
            sp.dma_start(wv[:], wv_d).then_inc(s_w_in, 16)
            sp.dma_start(bo[:], bo_d.broadcast_to([P, D])).then_inc(s_w_in, 16)
            sp.sem_inc(s_out, 16)
            sp.wait_ge(s_zero, 2)

            def load(i, j, first=False):
                b = j % 2
                m = i * B + j
                if not first:
                    wait(sp, s_seen, (s_ctx_hi, (m - 1) * 2), (s_ctx_split, (m - 1) * 2), (s_c1_split, m - 1))
                sp.dma_start(ct[b][:], ctx_t_d[m]).then_inc(s_ctx_in[b], 16)
                sp.dma_start(cn[b][:], ctx_d[m, 0:LK - 1].rearrange("(c p) d -> p c d", p=P)).then_inc(s_ctx_in[b], 16)
                for r in (0, 32, 64):
                    sp.dma_start(c1[b][r:r + 1, :], ctx_d[m, LK - 1:LK]).then_inc(s_ctx_in[b], 16)

            def load_queries(i):
                sp.dma_start(qt[:], q_d[:, :, bass.ds(i * P, P)]).then_inc(s_q_in, 16)

            def load_x(i):
                sp.dma_start(xt[0][:], x_d[i]).then_inc(s_x_in, 16)

            def store(i):
                wait(sp, s_seen, (s_x1, i + 1))
                sp.dma_start(x1_d[i], x1[:]).then_inc(s_out, 16)

            def tile(i, first=False, last=False):
                load(i, 2)
                load(i, 3)
                if not last:
                    wait(sp, s_seen, (s_q_split, (i + 1) * 2 * B))
                    load_queries(i + 1)
                    load(i + 1, 0)
                    load(i + 1, 1)
                if not first:
                    store(i - 1)
                    wait(sp, s_seen, (s_xb, i))
                load_x(i)

            load_queries(0)
            load(0, 0, first=True)
            load(0, 1, first=True)
            tile(0, first=True)
            with sp.Fori(1, TILES - 1) as i:
                tile(i)
            tile(TILES - 1, last=True)
            store(TILES - 1)
            sp.wait_ge(s_out, 16 * TILES + 16)

        @block.gpsimd
        def _(pool):
            nc.gpsimd.memset(ident[:], 0.0).then_inc(s_const, 1)
            pool.wait_ge(s_const, 1)
            nc.gpsimd.affine_select(out=ident[:], in_=ident[:], compare_op=ALU.not_equal, fill=1.0, base=0,
                                    pattern=[[-1, P]], channel_multiplier=1).then_inc(s_const, 1)
            for b in range(2):
                nc.gpsimd.memset(c1[b][:], 0.0).then_inc(s_zero, 1)
            nc.gpsimd.memset(own[:], 1.0).then_inc(s_const, 1)
            pool.wait_ge(s_const, 3)
            nc.gpsimd.affine_select(out=own[:], in_=own[:], compare_op=ALU.is_ge, fill=0.0, base=0,
                                    pattern=[[-DH, HG]], channel_multiplier=1).then_inc(s_const, 1)
            pool.wait_ge(s_const, 4)
            nc.gpsimd.affine_select(out=own[:], in_=own[:], compare_op=ALU.is_ge, fill=0.0, base=DH - 1,
                                    pattern=[[DH, HG]], channel_multiplier=-1).then_inc(s_const, 1)
            for b in range(2):
                for k in range(2):
                    nc.gpsimd.memset(cth[b][k][:, :, LK:LKE].bitcast(F32), 0.0).then_inc(s_const, 1)
            nc.gpsimd.memset(last_p[:].bitcast(F32), 0.0).then_inc(s_const, 1)

            def halves(i, j):
                b = j % 2
                m = i * B + j
                wait(pool, s_seen, (s_ctx_hi, 2 * m + 1))
                nc.gpsimd.tensor_tensor(cth[b][1][:, :, 0:LK], ct[b][:], cth[b][0][:, :, 0:LK].bitcast(F32),
                                        ALU.subtract).then_inc(s_ctx_split, 1)
                wait(pool, s_seen, (s_q_in, (i + 1) * 16))
                if j == 0:
                    nc.gpsimd.tensor_copy(qs[0][:], qt[:]).then_inc(s_q_hi, 1)
                    pool.wait_ge(s_q_hi, 2 * i + 1)
                    nc.gpsimd.tensor_tensor(qs[1][:], qt[:], qs[0][:].bitcast(F32), ALU.subtract).then_inc(s_q_hi, 1)
                    pool.wait_ge(s_q_hi, 2 * i + 2)
                for k in range(2):
                    nc.gpsimd.tensor_tensor(
                        qh[b][k][:],
                        qs[k][:, :, j * LQ:(j + 1) * LQ].bitcast(F32).unsqueeze(2).broadcast_to([P, C, HG, LQ]),
                        own[:].unsqueeze(1).unsqueeze(3).broadcast_to([P, C, HG, LQ]),
                        ALU.mult).then_inc(s_q_split, 1)

            def halves_n(i, j):
                b = j % 2
                m = i * B + j
                pool.wait_ge(s_ctx_hi, 2 * m + 2)
                nc.gpsimd.tensor_tensor(cnh[b][1][:], cn[b][:], cnh[b][0][:].bitcast(F32),
                                        ALU.subtract).then_inc(s_ctx_split, 1)

            def output(i):
                pool.wait_ge(s_x_in, (i + 1) * 16)
                pool.wait_ge(s_x1, i)
                nc.gpsimd.tensor_tensor(xb[:], xt[0][:], bo[:], ALU.add).then_inc(s_xb, 1)
                pool.wait_ge(s_o_hi, i * 2 + 2)
                nc.gpsimd.tensor_tensor(oth[1][:], ot[:], oth[0][:].bitcast(F32), ALU.subtract).then_inc(s_o_split, 1)

            pool.wait_ge(s_const, 10)
            pool.wait_ge(s_w_in, 80)
            for j in range(2):
                halves(0, j)
                halves_n(0, j)

            def tile(i, first=False, last=False):
                for j in range(B):
                    ahead = (i if j + 2 < B else i + 1, (j + 2) % B)
                    if j + 2 < B or not last:
                        halves(*ahead)
                    if j == 0 and not first:
                        output(i - 1)
                    if j + 2 < B or not last:
                        halves_n(*ahead)

            tile(0, first=True)
            with pool.Fori(1, TILES - 1) as i:
                tile(i)
            tile(TILES - 1, last=True)
            output(TILES - 1)

        @block.tensor
        def _(pe):
            pe.wait_ge(s_const, 10)
            pe.wait_ge(s_w_split, 2)

            def keys(i, j, groups):
                b = j % 2
                m = i * B + j
                pe.wait_ge(s_ctx_split, 2 * m + 1)
                for g in groups:
                    k = g % 2
                    pe.wait_ge(s_k_split[k], 2 * m + g // 2 + 1)
                    for c in range(CC):
                        for n, (a, d) in enumerate(PASSES):
                            last = nc.tensor.matmul(bank_k[k][:, 0:LKE], wk[a][:, c, g * P:(g + 1) * P],
                                                    cth[b][d][:, c, :], start=(c == 0 and n == 0),
                                                    stop=(c == CC - 1 and n == 2))
                    last.then_inc(s_k[k], 1)

            def scores(i, j, groups):
                b = j % 2
                m = i * B + j
                pe.wait_ge(s_q_split, 2 * m + 2)
                for g in groups:
                    k = g % 2
                    pe.wait_ge(s_k_split[k], 2 * m + g // 2 + 2)
                    pe.wait_ge(s_exp[k], 2 * m + g // 2 + 1)
                    for n, (a, d) in enumerate(PASSES):
                        last = nc.tensor.matmul(bank_s[k][:, 0:LKE], qh[b][a][:, g, :, :], kt[d][:, g, :],
                                                start=(n == 0), stop=(n == 2))
                    last.then_inc(s_s[k], 1)

            def turn(i, j, parts):
                m = i * B + j
                pe.wait_ge(s_probs, m + 1)
                for u in parts:
                    n = 3 * j + u
                    k = n % 2
                    pe.wait_ge(s_t_split[k], i * (3 * B // 2) + n // 2 + 1)
                    for g in range(C):
                        if u < 2:
                            last = nc.tensor.transpose(bank_t[k][:, g * P:(g + 1) * P],
                                                       probs[:, g, u * P:(u + 1) * P], ident[:])
                        else:
                            last = nc.tensor.transpose(bank_t[k][0:96, g * P:(g + 1) * P],
                                                       last_p[:, g, :].bitcast(F32), ident[:])
                    last.then_inc(s_t[k], 1)

            def sums(i, j, c):
                b = j % 2
                m = i * B + j

                def turned(u):
                    n = 3 * j + u
                    pe.wait_ge(s_t_split[n % 2], i * (3 * B // 2) + n // 2 + 2)

                pe.wait_ge(s_ctx_split, 2 * m + 2)
                pe.wait_ge(s_v_taken[c], v_before(i, j, c) + 1)
                cols = slice(c * P, (c + 1) * P)
                for u in range(2):
                    turned(u)
                    for n, (a, d) in enumerate(PASSES):
                        nc.tensor.matmul(bank_v[c][:], cnh[b][a][:, u, cols], pt[d][:, u, :],
                                         start=(u == 0 and n == 0), stop=False)
                turned(2)
                pe.wait_ge(s_c1_split, m + 1)
                nc.tensor.matmul(bank_v[c][:], c1h[b][:, cols], p1[:], start=False, stop=True).then_inc(s_v[c], 1)

            def output(i):
                for c in range(CC):
                    pe.wait_ge(s_v_taken[c], v0_output(i + 1) + 1)
                for h in range(H):
                    r = DH * (h % HG)
                    for c in range(CC):
                        last = nc.tensor.matmul(bank_v[0][r:r + DH, (h // HG) * P:(h // HG + 1) * P],
                                                wv[:, c, h * DH:(h + 1) * DH], mix[:, c, h, :, :],
                                                start=(c == 0), stop=(c == CC - 1), skip_group_check=True)
                last.then_inc(s_v[0], 1)

            def project(i):
                pe.wait_ge(s_o_split, i + 1)
                pe.wait_ge(s_v_taken[1], v1_project(i + 1) + 1)
                for c in range(C):
                    for n, (a, d) in enumerate(PASSES):
                        last = nc.tensor.matmul(bank_v[1][:], oth[a][:, c, :], wo[d][:, c, :],
                                                start=(c == 0 and n == 0), stop=(c == C - 1 and n == 2))
                last.then_inc(s_v[1], 1)

            keys(0, 0, range(C))
            scores(0, 0, range(C))

            def tile(i, first=False, last=False):
                for j in range(B):
                    more = j + 1 < B or not last
                    ni, nj = (i, j + 1) if j + 1 < B else (i + 1, 0)
                    if more:
                        keys(ni, nj, (0, 1))
                    turn(i, j, (0, 1))
                    if more:
                        keys(ni, nj, (2, 3))
                    turn(i, j, (2,))
                    if j == 0 and not first:
                        output(i - 1)
                    if more:
                        scores(ni, nj, (0, 1))
                    if j == 1 and not first:
                        project(i - 1)
                    sums(i, j, 0)
                    if more:
                        scores(ni, nj, (2, 3))
                    sums(i, j, 1)

            tile(0, first=True)
            with pe.Fori(1, TILES - 1) as i:
                tile(i)
            tile(TILES - 1, last=True)
            output(TILES - 1)
            project(TILES - 1)

        @block.scalar
        def _(act):
            act.wait_ge(s_w_in, 80)
            nc.scalar.activation(wk[0][:], wk32[:], ACT.Copy).then_inc(s_w_hi, 1)
            nc.scalar.activation(wo[0][:], wo32[:], ACT.Copy).then_inc(s_w_hi, 1)
            for k in range(2):
                act.sem_inc(s_exp[k], 1)
                act.sem_inc(s_v_taken[k], 1)

            def context_t(i, j):
                b = j % 2
                act.wait_ge(s_ctx_in[b], (i * (B // 2) + j // 2 + 1) * 80)
                nc.scalar.activation(cth[b][0][:, :, 0:LK], ct[b][:], ACT.Copy).then_inc(s_ctx_hi, 1)

            def context_n(j):
                b = j % 2
                nc.scalar.activation(cnh[b][0][:], cn[b][:], ACT.Copy).then_inc(s_ctx_hi, 1)

            def keys(i, j, groups):
                m = i * B + j
                for g in groups:
                    act.wait_ge(s_k[g % 2], 2 * m + g // 2 + 1)
                    nc.scalar.activation(kt[0][:, g, :], bank_k[g % 2][:, 0:LKE], ACT.Identity,
                                         bias=bias[:, 1, g:g + 1]).then_inc(s_k_hi, 1)

            def exps(i, j, groups):
                m = i * B + j
                for g in groups:
                    act.wait_ge(s_max, 4 * m + g + 1)
                    nc.scalar.activation(probs[:, g, :], bank_s[g % 2][:, 0:LK], ACT.Exp, bias=negmax[:, g:g + 1],
                                         accum_out=total[:, g:g + 1]).then_inc(s_exp[g % 2], 1)

            def turned(i, j):
                for u in range(2):
                    n = 3 * j + u
                    act.wait_ge(s_t[n % 2], i * (3 * B // 2) + n // 2 + 1)
                    nc.scalar.activation(pt[0][:, u, :], bank_t[n % 2][:], ACT.Copy).then_inc(s_t_hi, 1)

            def turned_last(i, j):
                n = 3 * j + 2
                act.wait_ge(s_t[n % 2], i * (3 * B // 2) + n // 2 + 1)
                nc.scalar.activation(p1[:], bank_t[n % 2][0:96, :], ACT.Copy).then_inc(s_t_split[n % 2], 1)

            def sums(i, j, c):
                act.wait_ge(s_v[c], v_before(i, j, c) + 1)
                nc.scalar.activation(mix[:, c, :, j, :], bank_v[c][:].rearrange("p (h q) -> p h q", h=H),
                                     ACT.Copy).then_inc(s_v_taken[c], 1)

            def output(i):
                act.wait_ge(s_o_hi, i * 2 + 1)
                nc.scalar.activation(oth[0][:], ot[:], ACT.Copy).then_inc(s_o_hi, 1)

            for j in range(2):
                context_t(0, j)
                context_n(j)
            keys(0, 0, range(C))
            exps(0, 0, range(C))

            def tile(i, first=False, last=False):
                for j in range(B):
                    more = j + 1 < B or not last
                    ni, nj = (i, j + 1) if j + 1 < B else (i + 1, 0)
                    ahead = (i if j + 2 < B else i + 1, (j + 2) % B)
                    if more:
                        keys(ni, nj, (0, 1))
                    turned(i, j)
                    if more:
                        keys(ni, nj, (2, 3))
                    turned_last(i, j)
                    if j == 0 and not first:
                        output(i - 1)
                    if more:
                        exps(ni, nj, (0, 1))
                    if j + 2 < B or not last:
                        context_t(*ahead)
                    sums(i, j, 0)
                    if more:
                        exps(ni, nj, (2, 3))
                    sums(i, j, 1)
                    if j + 2 < B or not last:
                        context_n((j + 2) % B)

            tile(0, first=True)
            with act.Fori(1, TILES - 1) as i:
                tile(i)
            tile(TILES - 1, last=True)
            output(TILES - 1)

        @block.vector
        def _(dve):
            for n, (w32, lo, hi) in enumerate(((wk32, wk[1], wk[0]), (wo32, wo[1], wo[0]))):
                dve.wait_ge(s_w_hi, n + 1)
                nc.vector.tensor_tensor(lo[:], w32[:], hi[:].bitcast(F32), ALU.subtract).then_inc(s_w_split, 1)
            for k in range(2):
                dve.sem_inc(s_k_split[k], 1)
                dve.sem_inc(s_t_split[k], 1)
            dve.wait_ge(s_const, 10)

            def keys(i, j, groups):
                m = i * B + j
                for g in groups:
                    dve.wait_ge(s_k_hi, 4 * m + g + 1)
                    nc.vector.scalar_tensor_tensor(out=kt[1][:, g, :], in0=bank_k[g % 2][:, 0:LKE],
                                                   scalar=bias[:, 1, g:g + 1], in1=kt[0][:, g, :].bitcast(F32),
                                                   op0=ALU.add, op1=ALU.subtract).then_inc(s_k_split[g % 2], 1)

            def maxima(i, j, groups):
                m = i * B + j
                for g in groups:
                    dve.wait_ge(s_s[g % 2], 2 * m + g // 2 + 1)
                    nc.vector.tensor_reduce(negmax[:, g:g + 1], bank_s[g % 2][:, 0:LK], X, ALU.max,
                                            negate=True).then_inc(s_max, 1)

            def normalise(i, j, pair):
                m = i * B + j
                for k in range(2):
                    dve.wait_ge(s_exp[k], 2 * m + pair + 2)
                both = slice(2 * pair, 2 * pair + 2)
                nc.vector.reciprocal(inv[:, both], total[:, both]).then_inc(s_inv, 1)
                dve.wait_ge(s_inv, 2 * m + pair + 1)
                for g in (2 * pair, 2 * pair + 1):
                    last = nc.vector.tensor_scalar(probs[:, g, :], probs[:, g, :], inv[:, g:g + 1], None, ALU.mult)
                last.then_inc(s_norm, 1)

            def last_halves(i, j):
                m = i * B + j
                dve.wait_ge(s_norm, 2 * m + 2)
                nc.vector.tensor_copy(last_p[:, :, 0:64:32],
                                      bc_last(probs[:, :, LK - 1], 2)).then_inc(s_last, 1)
                dve.wait_ge(s_last, m + 1)
                nc.vector.tensor_tensor(last_p[:, :, 64], probs[:, :, LK - 1], last_p[:, :, 0].bitcast(F32),
                                        ALU.subtract).then_inc(s_probs, 1)

            def turned(i, j):
                m = i * B + j
                for u in range(2):
                    n = 3 * j + u
                    dve.wait_ge(s_t_hi, 2 * m + u + 1)
                    nc.vector.tensor_tensor(pt[1][:, u, :], bank_t[n % 2][:], pt[0][:, u, :].bitcast(F32),
                                            ALU.subtract).then_inc(s_t_split[n % 2], 1)

            def output(i):
                dve.wait_ge(s_v[0], v0_output(i + 1) + 1)
                nc.vector.tensor_tensor(ot[:], bank_v[0][:].rearrange("p (g n) -> p g n", g=C),
                                        bc_last(bias[:, 2, :], P), ALU.add).then_inc(s_o_hi, 1)
                dve.wait_ge(s_o_hi, i * 2 + 1)
                dve.sem_inc(s_v_taken[0], 1)

            def residual(i):
                dve.wait_ge(s_v[1], v1_project(i + 1) + 1)
                dve.wait_ge(s_xb, i + 1)
                dve.wait_ge(s_out, 16 * i + 16)
                nc.vector.tensor_tensor(x1[:], bank_v[1][:], xb[:], ALU.add).then_inc(s_x1, 1)
                dve.wait_ge(s_x1, i + 1)
                dve.sem_inc(s_v_taken[1], 1)

            def last_key(i, j):
                b = j % 2
                m = i * B + j
                dve.wait_ge(s_ctx_in[b], (i * (B // 2) + j // 2 + 1) * 80)
                nc.vector.tensor_copy(c1h[b][:], c1[b][:]).then_inc(s_c1_hi, 1)
                dve.wait_ge(s_c1_hi, m + 1)
                nc.vector.tensor_tensor(c1h[b][32:64, :], c1[b][32:64, :], c1h[b][32:64, :].bitcast(F32),
                                        ALU.subtract).then_inc(s_c1_split, 1)

            last_key(0, 0)
            keys(0, 0, range(C))
            maxima(0, 0, range(C))
            normalise(0, 0, 0)
            normalise(0, 0, 1)
            last_halves(0, 0)

            def tile(i, first=False, last=False):
                for j in range(B):
                    more = j + 1 < B or not last
                    ni, nj = (i, j + 1) if j + 1 < B else (i + 1, 0)
                    if more:
                        keys(ni, nj, (0, 1))
                    turned(i, j)
                    if more:
                        keys(ni, nj, (2, 3))
                    if j == 0 and not first:
                        output(i - 1)
                    if more:
                        maxima(ni, nj, (0, 1))
                    if j == 1 and not first:
                        residual(i - 1)
                    if more:
                        last_key(ni, nj)
                        normalise(ni, nj, 0)
                        maxima(ni, nj, (2, 3))
                        normalise(ni, nj, 1)
                        last_halves(ni, nj)

            tile(0, first=True)
            with dve.Fori(1, TILES - 1) as i:
                tile(i)
            tile(TILES - 1, last=True)
            output(TILES - 1)
            residual(TILES - 1)


def attention_phase(nc, tag, layers, scale, w_d, bias_d, bo_d, xn_d, x_d, y_d, routed=None):
    with ExitStack() as ctx:
        sb, ps, sem = alloc(nc, ctx)
        w32 = sb(f"{tag}_w32", [P, C, D])
        w = [[sb(f"{tag}_w{m}_{k}", [P, C, D], F32R) for k in range(2)] for m in range(4)]
        bias_qk = sb(f"{tag}_bias_qk", [P, 2, C])
        bias_v = sb(f"{tag}_bias_v", [P, C])
        bias_q = sb(f"{tag}_bias_q", [P, C])
        bo = sb(f"{tag}_bo", [P, D])
        xn = [[sb(f"{tag}_xn{b}_{k}", [P, C, N], F32R) for k in range(2)] for b in range(2)]
        qt = sb(f"{tag}_qt", [P, C, N])
        kb = sb(f"{tag}_kb", [P, C, SUP * TILE_SEQ, HG, LQ])
        v = sb(f"{tag}_v", [P, SUP, D])
        ex = [sb(f"{tag}_ex{b}", [P, H, LQ]) for b in range(2)]
        negmax = [sb(f"{tag}_negmax{b}", [P, H]) for b in range(2)]
        total = sb(f"{tag}_total", [P, H])
        inv = [sb(f"{tag}_inv{b}", [P, H]) for b in range(2)]
        pt = [sb(f"{tag}_pt{b}", [P, H, P]) for b in range(2)]
        ot = sb(f"{tag}_ot", [P, C, P])
        oth = [[sb(f"{tag}_oth{b}_{k}", [P, C, P], F32R) for k in range(2)] for b in range(2)]
        x = [sb(f"{tag}_x{b}", [P, D]) for b in range(2)]
        y = [sb(f"{tag}_y{b}", [P, D]) for b in range(2)]
        if routed:
            mask_d, wt_d = routed
            mask = sb(f"{tag}_mask", [P, SUP, LQ])
            wt = sb(f"{tag}_wt", [P, SUP])

        bank_p = [ps(f"{tag}_bank_p{k}") for k in range(4)]
        bank_s = [ps(f"{tag}_bank_s{k}") for k in range(2)]
        bank_o = [ps(f"{tag}_bank_o{k}") for k in range(2)]

        s_seen = sem(f"{tag}_s_seen")
        s_w_in = sem(f"{tag}_s_w_in")
        s_w_hi = sem(f"{tag}_s_w_hi")
        s_w_split = sem(f"{tag}_s_w_split")
        s_bqk_in = sem(f"{tag}_s_bqk_in")
        s_bvo_in = sem(f"{tag}_s_bvo_in")
        s_bias_q = sem(f"{tag}_s_bias_q")
        s_zero = sem(f"{tag}_s_zero")
        s_xn_in = [sem(f"{tag}_s_xn_in{b}") for b in range(2)]
        s_m_in = sem(f"{tag}_s_m_in")
        s_x_in = [sem(f"{tag}_s_x_in{b}") for b in range(2)]
        s_prod = [sem(f"{tag}_s_prod{k}") for k in range(4)]
        s_taken = [sem(f"{tag}_s_taken{k}") for k in range(4)]
        s_scores = [sem(f"{tag}_s_scores{b}") for b in range(2)]
        s_s_free = [sem(f"{tag}_s_s_free{b}") for b in range(2)]
        s_max = sem(f"{tag}_s_max")
        s_shift = sem(f"{tag}_s_shift")
        s_exp = sem(f"{tag}_s_exp")
        s_total = sem(f"{tag}_s_total")
        s_inv = sem(f"{tag}_s_inv")
        s_norm = sem(f"{tag}_s_norm")
        s_pt = sem(f"{tag}_s_pt")
        s_sums = [sem(f"{tag}_s_sums{b}") for b in range(2)]
        s_o_free = [sem(f"{tag}_s_o_free{b}") for b in range(2)]
        s_o_hi = sem(f"{tag}_s_o_hi")
        s_o_split = sem(f"{tag}_s_o_split")
        s_xb = sem(f"{tag}_s_xb")
        s_y = sem(f"{tag}_s_y")
        s_out = [sem(f"{tag}_s_out{b}") for b in range(2)]

        VALUES, QUERIES, PROJECT, KEYS = range(2, 6)

        def use(i, what, final=False):
            return 4 * i + (VALUES + 1 if final and what == PROJECT else what)

        block = ctx.enter_context(nc.Block())

        def supertiles(eng, layer, body):
            def supertile(e, r, b, role):
                body(e, 2 * r + b, e * SUPERS + 2 * r + b, b, e * (SUPERS // 2) + r, role)

            def run(e, role):
                layer(e)
                with eng.Fori(0, SUPERS // 2 - 1) as r:
                    for b in range(2):
                        supertile(e, r, b, "middle")
                supertile(e, SUPERS // 2 - 1, 0, "before_" + role)
                supertile(e, SUPERS // 2 - 1, 1, role)

            if layers > 1:
                with eng.Fori(0, layers - 1) as e:
                    run(e, "turn")
            run(layers - 1, "end")

        @block.sync
        def _(sp):
            sp.sem_inc(s_y, 2)
            for b in range(2):
                sp.sem_inc(s_out[b], 16)

            def load_w(e, m):
                if m > 0 or not isinstance(e, int) or e > 0:
                    wait(sp, s_seen, (s_w_split, 4 * e + m))
                sp.dma_start(w32[:], w_d[e, m]).then_inc(s_w_in, 16)

            def load_bias_qk(e):
                sp.dma_start(bias_qk[:], bias_d[e][:, 0:2, :]).then_inc(s_bqk_in, 16)

            def load_bias_vo(e):
                sp.dma_start(bias_v[:], bias_d[e][:, 2, :]).then_inc(s_bvo_in, 16)
                sp.dma_start(bo[:], bo_d[e].broadcast_to([P, D])).then_inc(s_bvo_in, 16)

            def body(e, s, i, b, half, role):
                def load_x(t):
                    wait(sp, s_seen, (s_y, SUP * i + t + 1))
                    sp.dma_start(x[t % 2][:], x_d[s * SUP + t]).then_inc(s_x_in[t % 2], 16)

                def store(t):
                    wait(sp, s_seen, (s_y, SUP * i + t + 3))
                    sp.dma_start(y_d[s * SUP + t], y[t % 2][:]).then_inc(s_out[t % 2], 16)

                if routed:
                    wait(sp, s_seen, (s_y, SUP * i + 2))
                    sp.dma_start(mask[:], mask_d[:, e, bass.ds(s * SUP, SUP), :]).then_inc(s_m_in, 16)
                    sp.dma_start(wt[:], wt_d[:, e, bass.ds(s * SUP, SUP)]).then_inc(s_m_in, 16)
                load_x(0)
                load_x(1)
                if role == "turn":
                    wait(sp, s_seen, (s_taken[3], use(i, VALUES) + 2))
                    load_bias_qk(e + 1)
                    load_w(e + 1, 1)
                    load_w(e + 1, 2)
                store(0)
                load_x(2)
                store(1)
                load_x(3)
                if role == "before_turn":
                    load_w(e + 1, 0)
                if role == "turn":
                    load_w(e + 1, 3)
                store(2)
                store(3)
                if role == "turn":
                    load_bias_vo(e + 1)

            load_w(0, 0)
            load_bias_qk(0)
            load_bias_vo(0)
            for m in range(1, 4):
                load_w(0, m)
            supertiles(sp, lambda e: None, body)
            for b in range(2):
                sp.wait_ge(s_out[b], 16 * (layers * SUPERS * SUP // 2) + 16)

        def w_lo(engine, m):
            return engine.tensor_tensor(w[m][1][:], w32[:], w[m][0][:].bitcast(F32), ALU.subtract)

        @block.gpsimd
        def _(pool):
            nc.gpsimd.memset(kb[:], 0.0).then_inc(s_zero, 1)
            for b in range(2):
                nc.gpsimd.memset(pt[b][:], 0.0).then_inc(s_zero, 1)
            pool.sem_inc(s_o_split, 1)

            def split_o(e):
                wait(pool, s_seen, (s_w_hi, 4 * e + 4), (s_w_split, 4 * e + 3))
                w_lo(nc.gpsimd, 3).then_inc(s_w_split, 1)

            split_o(0)

            def body(e, s, i, b, half, role):
                def normalise(t):
                    pool.wait_ge(s_inv, SUP * i + t + 1)
                    nc.gpsimd.tensor_tensor(ex[t % 2][:], ex[t % 2][:], bc_last(inv[t % 2][:], LQ), ALU.mult)\
                        .then_inc(s_norm, 1)

                def output_lo(t):
                    pool.wait_ge(s_o_hi, SUP * i + t + 1)
                    nc.gpsimd.tensor_tensor(oth[t % 2][1][:], ot[:], oth[t % 2][0][:].bitcast(F32),
                                            ALU.subtract).then_inc(s_o_split, 1)

                normalise(0)
                normalise(1)
                normalise(2)
                output_lo(0)
                normalise(3)
                output_lo(1)
                output_lo(2)
                output_lo(3)
                if role == "turn":
                    split_o(e + 1)

            supertiles(pool, lambda e: None, body)

        @block.tensor
        def _(pe):
            def product(k, u, out, pairs):
                pe.wait_ge(s_taken[k], u + 2)
                for c in range(C):
                    for n, (a, d) in enumerate(PASSES):
                        lhs, rhs = pairs(c, a, d)
                        last = nc.tensor.matmul(out, lhs, rhs, start=(c == 0 and n == 0),
                                                stop=(c == C - 1 and n == 2))
                last.then_inc(s_prod[k], 1)

            def turned_product(m, g, b, u):
                product(g, u, bank_p[g][:], lambda c, a, d: (w[m][a][:, c, g * P:(g + 1) * P], xn[b][d][:, c, :]))

            def body(e, s, i, b, half, role):
                end = role == "end"

                def values(t):
                    product(t, use(i, VALUES), bank_p[t][:],
                            lambda c, a, d: (xn[b][a][:, c, t * P:(t + 1) * P], w[2][d][:, c, :]))

                def scores(t):
                    if t == 0:
                        for g in range(C):
                            pe.wait_ge(s_taken[g], use(i, VALUES) + 2)
                    pe.wait_ge(s_s_free[t % 2], (SUP // 2) * i + t // 2 + 1)
                    for q in range(TILE_SEQ):
                        for g in range(C):
                            last = nc.tensor.matmul(
                                bank_s[t % 2][LQ * q:LQ * q + LQ, g * P:(g + 1) * P],
                                qt[:, g, t * P + LQ * q:t * P + LQ * q + LQ], kb[:, g, t * TILE_SEQ + q, :, :],
                                start=True, stop=True, skip_group_check=True)
                    last.then_inc(s_scores[t % 2], 1)

                def sums(t):
                    pe.wait_ge(s_pt, SUP * i + t + 3)
                    pe.wait_ge(s_taken[t], use(i, VALUES) + 3)
                    pe.wait_ge(s_o_free[t % 2], (SUP // 2) * i + t // 2 + 1)
                    for h in range(H):
                        r = DH * (h % HG)
                        last = nc.tensor.matmul(bank_o[t % 2][r:r + DH, (h // HG) * P:(h // HG + 1) * P],
                                                v[:, t, h * DH:(h + 1) * DH], pt[t % 2][:, h, :],
                                                start=True, stop=True, skip_group_check=True)
                    last.then_inc(s_sums[t % 2], 1)

                def project(t):
                    if t == 0:
                        pe.wait_ge(s_w_split, 4 * e + 4)
                    pe.wait_ge(s_o_split, SUP * i + t + 2)
                    product(t, use(i, PROJECT, end), bank_p[t][:],
                            lambda c, a, d: (oth[t % 2][a][:, c, :], w[3][d][:, c, :]))

                def queries(g):
                    if end:
                        return
                    if g == 0:
                        pe.wait_ge(s_xn_in[1 - b], 32 * (half + b) + 32)
                        if role == "turn":
                            pe.wait_ge(s_w_split, 4 * e + 5)
                    turned_product(0, g, 1 - b, use(i, QUERIES))

                def keys(g):
                    if end:
                        return
                    if g == 0 and role == "turn":
                        pe.wait_ge(s_w_split, 4 * e + 6)
                    turned_product(1, g, 1 - b, use(i, KEYS))

                for t in range(SUP):
                    values(t)
                    scores(t)
                queries(0)
                sums(0)
                queries(1)
                sums(1)
                project(0)
                queries(2)
                sums(2)
                project(1)
                queries(3)
                sums(3)
                project(2)
                keys(0)
                project(3)
                keys(1)
                keys(2)
                keys(3)

            pe.wait_ge(s_xn_in[0], 32)
            for m in range(2):
                pe.wait_ge(s_w_split, m + 1)
                for g in range(C):
                    turned_product(m, g, 0, m)
            supertiles(pe, lambda e: wait(pe, s_seen, (s_w_split, 4 * e + 3)), body)

        @block.scalar
        def _(act):
            def load_xn(s, b):
                for k in range(2):
                    act.dma_start(xn[b][k][:].bitcast(F32), xn_d[s, k]).then_inc(s_xn_in[b], 16)

            def w_hi(e, m):
                wait(act, s_seen, (s_w_in, 64 * e + 16 * m + 16))
                nc.scalar.activation(w[m][0][:], w32[:], ACT.Copy).then_inc(s_w_hi, 1)

            def scale_bias(e):
                wait(act, s_seen, (s_bqk_in, 16 * e + 16))
                nc.scalar.activation(bias_q[:], bias_qk[:, 0, :], ACT.Copy, scale=scale).then_inc(s_bias_q, 1)
                wait(act, s_seen, (s_bias_q, e + 1))

            def queries(g, u):
                act.wait_ge(s_prod[g], u + 1)
                nc.scalar.activation(qt[:, g, :], bank_p[g][:], ACT.Identity, bias=bias_q[:, g:g + 1],
                                     scale=scale).then_inc(s_taken[g], 1)

            def keys(g, u):
                act.wait_ge(s_prod[g], u + 1)
                for h in range(HG):
                    r = slice(DH * h, DH * h + DH)
                    last = nc.scalar.activation(kb[r, g, :, h, :],
                                                bank_p[g][r, :].rearrange("p (b k) -> p b k", k=LQ),
                                                ACT.Identity, bias=bias_qk[r, 1, g:g + 1])
                last.then_inc(s_taken[g], 1)

            for k in range(4):
                act.sem_inc(s_taken[k], 2)
            if not routed:
                for b in range(2):
                    act.sem_inc(s_s_free[b], 1)
            load_xn(0, 0)
            w_hi(0, 0)
            scale_bias(0)
            load_xn(1, 1)
            w_hi(0, 1)
            for g in range(C):
                queries(g, 0)
            w_hi(0, 2)
            w_hi(0, 3)
            act.wait_ge(s_zero, 3)
            for g in range(C):
                keys(g, 1)

            def body(e, s, i, b, half, role):
                end = role == "end"

                def exp(t):
                    act.wait_ge(s_shift, SUP * i + t + 1)
                    if not routed:
                        act.sem_inc(s_s_free[t % 2], 1)
                    nc.scalar.activation(ex[t % 2][:], ex[t % 2][:], ACT.Exp).then_inc(s_exp, 1)

                def values(t):
                    act.wait_ge(s_prod[t], use(i, VALUES) + 1)
                    nc.scalar.activation(v[:, t, :], bank_p[t][:], ACT.Copy).then_inc(s_taken[t], 1)

                def output_hi(t):
                    act.wait_ge(s_o_free[t % 2], (SUP // 2) * i + t // 2 + 2)
                    nc.scalar.activation(oth[t % 2][0][:], ot[:], ACT.Copy).then_inc(s_o_hi, 1)

                def next_queries(g):
                    if not end:
                        queries(g, use(i, QUERIES))

                values(0)
                exp(0)
                if role == "turn":
                    w_hi(e + 1, 0)
                    scale_bias(e + 1)
                values(1)
                exp(1)
                values(2)
                values(3)
                if role in ("middle", "before_turn", "turn"):
                    load_xn(s + 2 if role == "middle" else b, b)
                exp(2)
                next_queries(0)
                exp(3)
                output_hi(0)
                next_queries(1)
                if role == "turn":
                    w_hi(e + 1, 1)
                output_hi(1)
                next_queries(2)
                output_hi(2)
                next_queries(3)
                output_hi(3)
                if role == "turn":
                    w_hi(e + 1, 2)
                if not end:
                    for g in range(C):
                        keys(g, use(i, KEYS))
                if role == "turn":
                    w_hi(e + 1, 3)

            supertiles(act, lambda e: None, body)

        @block.vector
        def _(dve):
            for b in range(2):
                dve.sem_inc(s_o_free[b], 1)
                if routed:
                    dve.sem_inc(s_s_free[b], 1)
            dve.sem_inc(s_pt, 2)

            def split(e, m):
                dve.wait_ge(s_w_hi, 4 * e + m + 1)
                w_lo(nc.vector, m).then_inc(s_w_split, 1)

            for m in range(3):
                split(0, m)
            dve.wait_ge(s_zero, 3)

            def layer(e):
                wait(dve, s_seen, (s_bvo_in, 32 * e + 32))

            def body(e, s, i, b, half, role):
                end = role == "end"

                def shift(t):
                    bank = bank_s[t % 2][:].rearrange("p (h k) -> p h k", h=H)
                    dve.wait_ge(s_scores[t % 2], (SUP // 2) * i + t // 2 + 1)
                    dve.wait_ge(s_pt, SUP * i + t + 1)
                    if routed:
                        if t == 0:
                            dve.wait_ge(s_m_in, 32 * i + 32)
                        nc.vector.tensor_tensor(ex[t % 2][:], bank, bc_mid(mask[:, t, :], H), ALU.add)\
                            .then_inc(s_s_free[t % 2], 1)
                        dve.wait_ge(s_s_free[t % 2], (SUP // 2) * i + t // 2 + 2)
                        bank = ex[t % 2][:]
                    nc.vector.tensor_reduce(negmax[t % 2][:], bank, X, ALU.max, negate=True).then_inc(s_max, 1)
                    dve.wait_ge(s_max, SUP * i + t + 1)
                    nc.vector.tensor_tensor(ex[t % 2][:], bank, bc_last(negmax[t % 2][:], LQ), ALU.add).then_inc(s_shift, 1)

                def total_of(t):
                    dve.wait_ge(s_exp, SUP * i + t + 1)
                    nc.vector.tensor_reduce(total[:], ex[t % 2][:], X, ALU.add).then_inc(s_total, 1)
                    dve.wait_ge(s_total, SUP * i + t + 1)
                    nc.vector.reciprocal(inv[t % 2][:], total[:]).then_inc(s_inv, 1)

                def turn(t):
                    dve.wait_ge(s_norm, SUP * i + t + 1)
                    for q in range(TILE_SEQ):
                        r = slice(LQ * q, LQ * q + LQ)
                        last = nc.vector.transpose(pt[t % 2][r, :, r], ex[t % 2][r, :, :])
                    last.then_inc(s_pt, 1)

                def output(t):
                    dve.wait_ge(s_sums[t % 2], (SUP // 2) * i + t // 2 + 1)
                    dve.wait_ge(s_o_split, SUP * i + t + 1)
                    nc.vector.tensor_tensor(ot[:], bank_o[t % 2][:].rearrange("p (g n) -> p g n", g=C),
                                            bc_last(bias_v[:], P), ALU.add).then_inc(s_o_free[t % 2], 1)

                def add_bias(t):
                    dve.wait_ge(s_x_in[t % 2], 16 * ((SUP // 2) * i + t // 2) + 16)
                    if routed:
                        nc.vector.scalar_tensor_tensor(out=x[t % 2][:], in0=bo[:], scalar=wt[:, t:t + 1],
                                                       in1=x[t % 2][:], op0=ALU.mult, op1=ALU.add).then_inc(s_xb, 1)
                    else:
                        nc.vector.tensor_tensor(x[t % 2][:], x[t % 2][:], bo[:], ALU.add).then_inc(s_xb, 1)

                def residual(t):
                    u = use(i, PROJECT, end)
                    dve.wait_ge(s_prod[t], u + 1)
                    dve.wait_ge(s_xb, SUP * i + t + 1)
                    dve.wait_ge(s_out[t % 2], 16 * ((SUP // 2) * i + t // 2) + 16)
                    if routed:
                        nc.vector.scalar_tensor_tensor(out=y[t % 2][:], in0=bank_p[t][:], scalar=wt[:, t:t + 1],
                                                       in1=x[t % 2][:], op0=ALU.mult, op1=ALU.add).then_inc(s_y, 1)
                    else:
                        nc.vector.tensor_tensor(y[t % 2][:], bank_p[t][:], x[t % 2][:], ALU.add).then_inc(s_y, 1)
                    dve.wait_ge(s_y, SUP * i + t + 3)
                    dve.sem_inc(s_taken[t], 1)

                shift(0)
                total_of(0)
                if role == "turn":
                    split(e + 1, 0)
                shift(1)
                turn(0)
                total_of(1)
                shift(2)
                turn(1)
                total_of(2)
                shift(3)
                output(0)
                turn(2)
                total_of(3)
                output(1)
                add_bias(0)
                add_bias(1)
                turn(3)
                if role == "turn":
                    split(e + 1, 1)
                residual(0)
                output(2)
                residual(1)
                output(3)
                if role == "turn":
                    split(e + 1, 2)
                add_bias(2)
                residual(2)
                add_bias(3)
                residual(3)

            supertiles(dve, layer, body)


def router_phase(nc, logit_d, mask_d, wt_d):
    ALL = TILES * EXPERTS
    with ExitStack() as ctx:
        sb, ps, sem = alloc(nc, ctx)
        logit = sb("r_logit", [P, TILES, EXPERTS])
        top = sb("r_top", [P, TILES])
        total = sb("r_total", [P, TILES])
        inv = sb("r_inv", [P, TILES])
        prob = sb("r_prob", [P, TILES, EXPERTS])
        above = sb("r_above", [P, TILES, EXPERTS, EXPERTS])
        tied = sb("r_tied", [P, TILES, EXPERTS, EXPERTS])
        before = sb("r_before", [P, EXPERTS, EXPERTS])
        rank = sb("r_rank", [P, TILES, EXPERTS])
        member = sb("r_member", [P, TILES, EXPERTS])
        wt = sb("r_wt", [P, EXPERTS, TILES])
        mask = sb("r_mask", [P, EXPERTS, TILES, LQ])
        ident = sb("r_ident", [P, P])
        place = sb("r_place", [P, LQ])
        own = sb("r_own", [P, TILE_SEQ])
        same = sb("r_same", [P, P])
        spread = [sb(f"r_spread{b}", [P, SUP, EXPERTS, LQ]) for b in range(2)]
        bank = [ps(f"r_bank{b}") for b in range(2)]

        s_in = sem("r_s_in")
        s_const = sem("r_s_const")
        s_dve = sem("r_s_dve")
        s_exp = sem("r_s_exp")
        s_spread = sem("r_s_spread")
        s_mask = sem("r_s_mask")
        s_taken = sem("r_s_taken")
        s_out = sem("r_s_out")

        block = ctx.enter_context(nc.Block())
        steps = [0]

        @block.sync
        def _(sp):
            sp.dma_start(logit[:], logit_d).then_inc(s_in, 16)
            sp.wait_ge(s_taken, SUPERS)
            sp.dma_start(mask_d, mask[:]).then_inc(s_out, 16)
            sp.dma_start(wt_d, wt[:]).then_inc(s_out, 16)
            sp.wait_ge(s_out, 32)

        @block.gpsimd
        def _(pool):
            nc.gpsimd.memset(ident[:], 0.0).then_inc(s_const, 1)
            nc.gpsimd.memset(own[:], 1.0).then_inc(s_const, 1)
            nc.gpsimd.memset(before[:], 0.0).then_inc(s_const, 1)
            pool.wait_ge(s_const, 3)
            nc.gpsimd.affine_select(out=ident[:], in_=ident[:], compare_op=ALU.not_equal, fill=1.0, base=0,
                                    pattern=[[-1, P]], channel_multiplier=1).then_inc(s_const, 1)
            nc.gpsimd.affine_select(out=own[:], in_=own[:], compare_op=ALU.is_ge, fill=0.0, base=0,
                                    pattern=[[-LQ, TILE_SEQ]], channel_multiplier=1).then_inc(s_const, 1)
            for e in range(1, EXPERTS):
                nc.gpsimd.memset(before[:, e, 0:e], 1.0).then_inc(s_const, 1)
            pool.wait_ge(s_const, 5 + EXPERTS - 1)
            nc.gpsimd.affine_select(out=own[:], in_=own[:], compare_op=ALU.is_ge, fill=0.0, base=LQ - 1,
                                    pattern=[[LQ, TILE_SEQ]], channel_multiplier=-1).then_inc(s_const, 1)

        @block.scalar
        def _(act):
            act.wait_ge(s_dve, 2)
            nc.scalar.activation(prob[:], logit[:], ACT.Exp).then_inc(s_exp, 1)

        @block.vector
        def _(dve):
            def step(ins):
                steps[0] += 1
                ins.then_inc(s_dve, 1)
                dve.wait_ge(s_dve, steps[0])

            dve.wait_ge(s_in, 16)
            step(nc.vector.tensor_reduce(top[:], logit[:], X, ALU.max, negate=True))
            step(nc.vector.tensor_tensor(logit[:], logit[:], bc_last(top[:], EXPERTS), ALU.add))
            dve.wait_ge(s_exp, 1)
            step(nc.vector.tensor_reduce(total[:], prob[:], X, ALU.add))
            step(nc.vector.reciprocal(inv[:], total[:]))
            step(nc.vector.tensor_tensor(prob[:], prob[:], bc_last(inv[:], EXPERTS), ALU.mult))
            wide = [P, TILES, EXPERTS, EXPERTS]
            other = prob[:].unsqueeze(2).broadcast_to(wide)
            mine = prob[:].unsqueeze(3).broadcast_to(wide)
            step(nc.vector.tensor_tensor(above[:], other, mine, ALU.is_gt))
            step(nc.vector.tensor_tensor(tied[:], other, mine, ALU.is_equal))
            dve.wait_ge(s_const, 6 + EXPERTS - 1)
            step(nc.vector.tensor_tensor(tied[:], tied[:], before[:].unsqueeze(1).broadcast_to(wide), ALU.mult))
            step(nc.vector.tensor_tensor(above[:], above[:], tied[:], ALU.add))
            step(nc.vector.tensor_reduce(rank[:], above[:], X, ALU.add))
            step(nc.vector.tensor_scalar(member[:], rank[:], 1.5, None, ALU.is_lt))
            step(nc.vector.tensor_tensor(wt[:].rearrange("p e t -> p t e"), prob[:], member[:], ALU.mult))
            step(nc.vector.tensor_tensor(place[:], ident[:, 0:LQ], ident[:, LQ:2 * LQ], ALU.add))
            step(nc.vector.tensor_tensor(place[:], place[:], ident[:, 2 * LQ:3 * LQ], ALU.add))
            step(nc.vector.tensor_tensor(place[:], place[:], ident[:, 3 * LQ:4 * LQ], ALU.add))
            step(nc.vector.tensor_copy(same[:].rearrange("p (b q) -> p b q", b=TILE_SEQ), bc_last(own[:], LQ)))
            for s in range(SUPERS):
                if s >= 2:
                    dve.wait_ge(s_mask, s - 1)
                nc.vector.tensor_tensor(
                    spread[s % 2][:].rearrange("p t e q -> p (t e) q"),
                    bc_last(member[:, s * SUP:(s + 1) * SUP, :].rearrange("p t e -> p (t e)"), LQ),
                    bc_mid(place[:], SUP * EXPERTS), ALU.mult).then_inc(s_spread, 1)
                dve.wait_ge(s_mask, s + 1)
                nc.vector.tensor_scalar(mask[:, :, s * SUP:(s + 1) * SUP, :].rearrange("p e t q -> p t e q"),
                                        bank[s % 2][:].rearrange("p (t e q) -> p t e q", t=SUP, e=EXPERTS),
                                        -1.0, MASKED, ALU.add, ALU.mult).then_inc(s_taken, 1)

        @block.tensor
        def _(pe):
            for s in range(SUPERS):
                pe.wait_ge(s_spread, s + 1)
                if s >= 2:
                    pe.wait_ge(s_taken, s - 1)
                nc.tensor.matmul(bank[s % 2][:], same[:], spread[s % 2][:].rearrange("p t e q -> p (t e q)"),
                                 start=True, stop=True).then_inc(s_mask, 1)


def program(nc, x, ctx, ctx_t, w, w_k, w_v, bias_p, bias_o, r_w, r_b, out):
    x_t = x.rearrange("(t p) d -> t p d", p=P)
    out_t = out.rearrange("(t p) d -> t p d", p=P)
    q_d = nc.dram_tensor("q_scratch", (P, C, TOK), F32).ap()
    xn_d = nc.dram_tensor("xn_scratch", (SUPERS, 2, P, C, N), F32).ap()
    x1_d = nc.dram_tensor("x1_scratch", (TILES, P, D), F32).ap()
    xn2_d = nc.dram_tensor("xn2_scratch", (SUPERS, 2, P, C, N), F32).ap()
    logit_d = nc.dram_tensor("logit_scratch", (P, TILES, EXPERTS), F32).ap()
    mask_d = nc.dram_tensor("mask_scratch", (P, EXPERTS, TILES, LQ), F32).ap()
    wt_d = nc.dram_tensor("wt_scratch", (P, EXPERTS, TILES), F32).ap()
    norm_phase(nc, "n0", x_t, None, q=(w[0], bias_p[0, :, 0], q_d))
    cross_phase(nc, x_t, q_d, ctx, ctx_t, w_k, w_v, w[1], bias_p[0], bias_o[0:1], x1_d)
    norm_phase(nc, "n1", x1_d, xn_d)
    attention_phase(nc, "a", 1, SELF_SCALE, w[2:6].rearrange("(l m) p c n -> l m p c n", m=4), bias_p[1:2],
                    bias_o[1:2].unsqueeze(1), xn_d, x1_d, out_t)
    norm_phase(nc, "n2", out_t, xn2_d, router=(r_w, r_b.broadcast_to([P, EXPERTS]), logit_d))
    router_phase(nc, logit_d, mask_d, wt_d)
    attention_phase(nc, "e", EXPERTS, EXPERT_SCALE, w[6:6 + 4 * EXPERTS].rearrange("(l m) p c n -> l m p c n", m=4),
                    bias_p[2:2 + EXPERTS], bias_o[2:2 + EXPERTS].unsqueeze(1), xn2_d, out_t, out_t,
                    routed=(mask_d, wt_d))


def kernel(**inputs):
    import numpy as np
    import concourse.bacc as bacc
    from concourse.bass_utils import run_bass_kernel_spmd as run

    a = {k: np.ascontiguousarray(v) for k, v in inputs.items()}

    def rows(w):
        return np.ascontiguousarray(w.reshape(-1, P, w.shape[-1]).transpose(1, 0, 2))

    def cols(*biases):
        return np.ascontiguousarray(np.stack([b.reshape(C, P).T for b in biases], axis=1))

    qkv, bqkv = a["L0_attn_w_qkv"], a["L0_attn_b_qkv"]
    w = [a["L0_xattn_Wq"], a["L0_xattn_Wo"]]
    w += [qkv[:, k * D:(k + 1) * D] for k in range(3)] + [a["L0_attn_w_proj"]]
    bias_p = [cols(a["L0_xattn_bq"], a["L0_xattn_bk"], a["L0_xattn_bv"]),
              cols(*[bqkv[k * D:(k + 1) * D] for k in range(3)])]
    bias_o = [a["L0_xattn_bo"], a["L0_attn_b_proj"]]
    for e in range(EXPERTS):
        w += [a[f"L0_ffn_w{k}"][e] for k in "qkvo"]
        bias_p.append(cols(*[a[f"L0_ffn_b{k}"][e] for k in "qkv"]))
        bias_o.append(a["L0_ffn_bo"][e])
    arrays = {
        "x": a["x"].reshape(TOK, D),
        "ctx": a["ctx_512"],
        "ctx_t": np.ascontiguousarray(a["ctx_512"].reshape(BATCH, LK, CC, P).transpose(0, 3, 2, 1)),
        "w": np.stack([rows(m) for m in w]),
        "w_k": rows(a["L0_xattn_Wk"]),
        "w_v": rows(a["L0_xattn_Wv"]),
        "bias_p": np.stack(bias_p),
        "bias_o": np.stack(bias_o),
        "r_w": rows(a["L0_ffn_router_w"]),
        "r_b": a["L0_ffn_router_b"].reshape(1, EXPERTS),
    }
    nc = bacc.Bacc("TRN2", target_bir_lowering=False, num_devices=1)
    args = [nc.dram_tensor(k, v.shape, F32, kind="ExternalInput").ap() for k, v in arrays.items()]
    args.append(nc.dram_tensor("out", (TOK, D), F32, kind="ExternalOutput").ap())
    program(nc, *args)
    r = run(nc, [arrays], core_ids=[0])
    return r.results[0]["out"].reshape(BATCH, LQ, D)
```

```python
from contextlib import ExitStack

import concourse.bass as bass
from concourse import mybir

F32 = mybir.dt.float32
F32R = mybir.dt.float32r
ALU = mybir.AluOpType
ACT = mybir.ActivationFunctionType
X = mybir.AxisListType.X

P = 128
BATCH = 128
LQ = 32
D = 512
H = 16
DH = D // H
C = D // P
HG = P // DH
LK = 257
LKE = LK + 1
DC = 256
CC = DC // P
TOK = BATCH * LQ
TILE_SEQ = P // LQ
TILES = TOK // P
SUP = 4
N = SUP * P
SUPERS = TOK // N
EXPERTS = 4
LAYERS = 1 + EXPERTS
EPS = 1e-5
CROSS_SCALE = float(DH) ** -0.5
SELF_SCALE = float(DH) ** -0.5
EXPERT_SCALE = 0.5
MASKED = 1.0e9
PASSES = ((0, 0), (0, 1), (1, 0))


def alloc(nc, ctx):
    sems = []

    def clear():
        nc.clear_and_free_semaphores(sems)
        nc.all_engine_barrier()

    ctx.callback(clear)

    def sb(name, shape, dt=F32):
        return ctx.enter_context(nc.sbuf_tensor(name, shape, dt))

    def ps(name):
        return ctx.enter_context(nc.psum_tensor(name, [P, 512], F32))

    def sem(name):
        sems.append(nc.alloc_semaphore(name=name))
        return sems[-1]

    return sb, ps, sem


def wait(eng, seen, *waits):
    for s, value in waits:
        eng.wait_ge(s, value)
        eng.sem_inc(seen, 1)


def bc_mid(ap, n):
    return ap.unsqueeze(1).broadcast_to([ap.shape[0], n, ap.shape[1]])


def bc_last(ap, n):
    return ap.unsqueeze(2).broadcast_to([ap.shape[0], ap.shape[1], n])


def norm_phase(nc, tag, x_d, xn_d, q=None, router=None):
    with ExitStack() as ctx:
        sb, ps, sem = alloc(nc, ctx)
        x = [sb(f"{tag}_x{b}", [P, SUP, D]) for b in range(2)]
        xn = [sb(f"{tag}_xn{b}", [P, SUP, D]) for b in range(2)]
        xt = [[sb(f"{tag}_xt{b}_{k}", [P, C, N], F32R) for k in range(2)] for b in range(2)]
        stats = sb(f"{tag}_stats", [P, SUP, 6])
        mv = sb(f"{tag}_mv", [P, SUP, 2])
        var_eps = sb(f"{tag}_vareps", [P, SUP])
        rstd = sb(f"{tag}_rstd", [P, SUP])
        power = sb(f"{tag}_power", [P, SUP])
        ident = sb(f"{tag}_ident", [P, P])
        turned = [ps(f"{tag}_turned{t}") for t in range(SUP)]
        prod = [ps(f"{tag}_prod{k}") for k in range(C)]
        if q:
            w_d, b_d, q_d = q
            w32 = sb(f"{tag}_w32", [P, C, D])
            w = [sb(f"{tag}_w{k}", [P, C, D], F32R) for k in range(2)]
            bias = sb(f"{tag}_bias", [P, C])
            bias_s = sb(f"{tag}_bias_s", [P, C])
            qt = sb(f"{tag}_qt", [P, C, N])
        if router:
            rw_d, logit_d = router
            rw32 = sb(f"{tag}_rw32", [P, C, EXPERTS])
            rw = [sb(f"{tag}_rw{k}", [P, C, EXPERTS], F32R) for k in range(2)]
            logit = sb(f"{tag}_logit", [EXPERTS, N])

        s_seen = sem(f"{tag}_s_seen")
        s_ident = sem(f"{tag}_s_ident")
        s_w_in = sem(f"{tag}_s_w_in")
        s_w_hi = sem(f"{tag}_s_w_hi")
        s_w_split = sem(f"{tag}_s_w_split")
        s_x_in = [sem(f"{tag}_s_x_in{b}") for b in range(2)]
        s_stats = sem(f"{tag}_s_stats")
        s_mv = sem(f"{tag}_s_mv")
        s_eps = sem(f"{tag}_s_eps")
        s_rstd = sem(f"{tag}_s_rstd")
        s_xn = sem(f"{tag}_s_xn")
        s_turned = [sem(f"{tag}_s_turned{t}") for t in range(SUP)]
        s_hi = sem(f"{tag}_s_hi")
        s_split = [sem(f"{tag}_s_split{t}") for t in range(SUP)]
        s_prod = sem(f"{tag}_s_prod")
        s_taken = sem(f"{tag}_s_taken")
        s_xt_out = [sem(f"{tag}_s_xt_out{b}") for b in range(2)]
        s_out = sem(f"{tag}_s_out")

        block = ctx.enter_context(nc.Block())

        def pipeline(eng, *stages):
            def step(s, b, half, first=False, last=False):
                for stage in stages:
                    if isinstance(stage, tuple):
                        if not first:
                            stage[0](s - 1, 1 - b, half + b - 1)
                    elif not last:
                        stage(s, b, half)

            step(0, 0, 0, first=True)
            with eng.Fori(0, SUPERS // 2 - 1) as r:
                step(2 * r + 1, 1, r)
                step(2 * r + 2, 0, r + 1)
            step(SUPERS - 1, 1, SUPERS // 2 - 1)
            step(SUPERS, 0, SUPERS // 2, last=True)

        @block.sync
        def _(sp):
            sp.sem_inc(s_xn, SUP + 1)
            sp.dma_start(x[0][:], x_d[0:SUP].rearrange("t p d -> p t d")).then_inc(s_x_in[0], 16)
            if q:
                sp.dma_start(w32[:], w_d).then_inc(s_w_in, 16)
                sp.dma_start(bias[:], b_d).then_inc(s_w_in, 16)
            if router:
                sp.dma_start(rw32[:], rw_d).then_inc(s_w_in, 16)

            def load(s, b):
                wait(sp, s_seen, (s_xn, s * SUP + 1))
                sp.dma_start(x[b][:], x_d[bass.ds(s * SUP, SUP)].rearrange("t p d -> p t d")).then_inc(s_x_in[b], 16)

            load(1, 1)
            with sp.Fori(0, SUPERS // 2 - 1) as r:
                for b in range(2):
                    load(2 * r + b + 2, b)

        @block.gpsimd
        def _(pool):
            nc.gpsimd.memset(ident[:], 0.0).then_inc(s_ident, 1)
            nc.gpsimd.memset(power[:], -0.5).then_inc(s_ident, 1)
            pool.wait_ge(s_ident, 2)
            nc.gpsimd.affine_select(out=ident[:], in_=ident[:], compare_op=ALU.not_equal, fill=1.0, base=0,
                                    pattern=[[-1, P]], channel_multiplier=1).then_inc(s_ident, 1)
            with pool.Fori(0, SUPERS) as s:
                wait(pool, s_seen, (s_mv, s * SUP + SUP))
                nc.gpsimd.tensor_scalar(var_eps[:], mv[:, :, 1], EPS, 1.0, ALU.add, ALU.mult).then_inc(s_eps, 1)
                pool.wait_ge(s_eps, s + 1)
                nc.gpsimd.tensor_tensor(rstd[:], var_eps[:], power[:], ALU.pow).then_inc(s_rstd, 1)

        @block.vector
        def _(dve):
            for t in range(SUP):
                dve.sem_inc(s_split[t], 1)
                dve.sem_inc(s_turned[t], 2)

            def statistics(s, b, half):
                dve.wait_ge(s_x_in[b], half * 16 + 16)
                for t in range(SUP):
                    nc.vector.bn_stats(stats[:, t, :], x[b][:, t, :]).then_inc(s_stats, 1)
                wait(dve, s_seen, (s_xn, s * SUP + SUP + 1))
                for t in range(SUP):
                    wait(dve, s_seen, (s_stats, s * SUP + t + 1))
                    nc.vector.bn_aggr(mv[:, t, :], stats[:, t, :]).then_inc(s_mv, 1)

            def lo(s, b, half):
                for t in range(SUP):
                    dve.wait_ge(s_hi, s * SUP + t + 1)
                    nc.vector.tensor_tensor(xt[b][1][:, :, t * P:(t + 1) * P],
                                            turned[t][:].rearrange("p (c n) -> p c n", c=C),
                                            xt[b][0][:, :, t * P:(t + 1) * P].bitcast(F32),
                                            ALU.subtract).then_inc(s_split[t], 1)

            def normalise(s, b, half):
                dve.wait_ge(s_turned[SUP - 1], s + 1)
                dve.wait_ge(s_rstd, s + 1)
                for t in range(SUP):
                    nc.vector.tensor_scalar(xn[b][:, t, :], x[b][:, t, :], mv[:, t, 0:1], rstd[:, t:t + 1],
                                            ALU.subtract, ALU.mult).then_inc(s_xn, 1)

            def split_weight():
                src, hi, low = (w32, w[0], w[1]) if q else (rw32, rw[0], rw[1])
                dve.wait_ge(s_w_hi, 1)
                nc.vector.tensor_tensor(low[:], src[:], hi[:].bitcast(F32), ALU.subtract).then_inc(s_w_split, 1)
                if q:
                    nc.vector.tensor_scalar(bias_s[:], bias[:], CROSS_SCALE, None, ALU.mult).then_inc(s_w_split, 1)

            def weight_first(s, b, half):
                if isinstance(s, int) and s == 0 and (q or router):
                    split_weight()

            pipeline(dve, statistics, (lo, 1), normalise, weight_first)

        @block.tensor
        def _(pe):
            pe.wait_ge(s_ident, 3)

            def turn(s, b, half):
                for t in range(SUP):
                    pe.wait_ge(s_xn, s * SUP + t + 2 + SUP)
                    pe.wait_ge(s_split[t], s + 1)
                    for c in range(C):
                        last = nc.tensor.transpose(turned[t][:, c * P:(c + 1) * P], xn[b][:, t, c * P:(c + 1) * P],
                                                   ident[:])
                    last.then_inc(s_turned[t], 1)

            def products(s, b, half):
                if not q and not router:
                    return
                pe.wait_ge(s_w_split, 1)
                for t in range(SUP):
                    pe.wait_ge(s_split[t], s + 2)
                if q:
                    for g in range(C):
                        pe.wait_ge(s_taken, s * C + g + 1)
                        for c in range(C):
                            for n, (a, d) in enumerate(PASSES):
                                last = nc.tensor.matmul(prod[g][:], w[a][:, c, g * P:(g + 1) * P], xt[b][d][:, c, :],
                                                        start=(c == 0 and n == 0), stop=(c == C - 1 and n == 2))
                        last.then_inc(s_prod, 1)
                if router:
                    pe.wait_ge(s_taken, s + 1)
                    for c in range(C):
                        for n, (a, d) in enumerate(PASSES):
                            last = nc.tensor.matmul(prod[0][0:EXPERTS, :], rw[a][:, c, :], xt[b][d][:, c, :],
                                                    start=(c == 0 and n == 0), stop=(c == C - 1 and n == 2))
                    last.then_inc(s_prod, 1)

            pipeline(pe, turn, (products, 1))

        @block.scalar
        def _(act):
            if q or router:
                act.wait_ge(s_w_in, 32 if q else 16)
                src, dst = (w32, w[0]) if q else (rw32, rw[0])
                nc.scalar.activation(dst[:], src[:], ACT.Copy).then_inc(s_w_hi, 1)
            act.sem_inc(s_taken, C if q else 1)
            act.sem_inc(s_out, 16)
            for b in range(2):
                act.sem_inc(s_xt_out[b], 32)

            def hi(s, b, half):
                if not q:
                    act.wait_ge(s_xt_out[b], half * 32 + 32)
                for t in range(SUP):
                    act.wait_ge(s_turned[t], s + 3)
                    nc.scalar.activation(xt[b][0][:, :, t * P:(t + 1) * P],
                                         turned[t][:].rearrange("p (c n) -> p c n", c=C),
                                         ACT.Copy).then_inc(s_hi, 1)

            def store(s, b, half):
                if not q:
                    for t in range(SUP):
                        wait(act, s_seen, (s_split[t], s + 2))
                    for k in range(2):
                        act.dma_start(xn_d[s, k], xt[b][k][:].bitcast(F32)).then_inc(s_xt_out[b], 16)

            def take(s, b, half):
                if q:
                    act.wait_ge(s_out, s * 16 + 16)
                    for g in range(C):
                        act.wait_ge(s_prod, s * C + g + 1)
                        nc.scalar.activation(qt[:, g, :], prod[g][:], ACT.Identity, bias=bias_s[:, g:g + 1],
                                             scale=CROSS_SCALE).then_inc(s_taken, 1)
                    act.wait_ge(s_taken, s * C + 2 * C)
                    act.dma_start(q_d[:, :, bass.ds(s * N, N)], qt[:]).then_inc(s_out, 16)
                if router:
                    act.wait_ge(s_out, s * 16 + 16)
                    act.wait_ge(s_prod, s + 1)
                    nc.scalar.activation(logit[:], prod[0][0:EXPERTS, :], ACT.Copy).then_inc(s_taken, 1)
                    act.wait_ge(s_taken, s + 2)
                    act.dma_start(logit_d[:, bass.ds(s * N, N)], logit[:]).then_inc(s_out, 16)

            def scaled_bias(s, b, half):
                if q and isinstance(s, int) and s == 0:
                    act.wait_ge(s_w_split, 2)

            pipeline(act, hi, scaled_bias, (take, 1), store)
            for b in range(2):
                if not q:
                    act.wait_ge(s_xt_out[b], 32 * (SUPERS // 2) + 32)
            if q or router:
                act.wait_ge(s_out, SUPERS * 16 + 16)


def cross_phase(nc, x_d, q_d, ctx_d, ctx_t_d, wk_d, wv_d, wo_d, bias_d, bo_d, x1_d):
    B = TILE_SEQ
    with ExitStack() as ctx:
        sb, ps, sem = alloc(nc, ctx)
        wk32 = sb("c_wk32", [P, CC, D])
        wk = [sb(f"c_wk{k}", [P, CC, D], F32R) for k in range(2)]
        wv = sb("c_wv", [P, CC, D])
        wo32 = sb("c_wo32", [P, C, D])
        wo = [sb(f"c_wo{k}", [P, C, D], F32R) for k in range(2)]
        bias = sb("c_bias", [P, 3, C])
        bo = sb("c_bo", [P, D])
        ident = sb("c_ident", [P, P])
        ct = [sb(f"c_ct{j}", [P, CC, LK]) for j in range(B)]
        cn = [sb(f"c_cn{j}", [P, 2, DC]) for j in range(B)]
        c1 = [sb(f"c_cl{j}", [P, DC]) for j in range(B)]
        cth = [[sb(f"c_cth{b}_{k}", [P, CC, LKE], F32R) for k in range(2)] for b in range(2)]
        cnh = [[sb(f"c_cnh{b}_{k}", [P, 2, DC], F32R) for k in range(2)] for b in range(2)]
        c1h = [sb(f"c_clh{b}", [P, DC], F32R) for b in range(2)]
        c1s = sb("c_cls", [P, DC])
        is_lo = sb("c_is_lo", [P, 1])
        sign = sb("c_sign", [P, 1])
        qt = sb("c_qt", [P, C, P])
        qs = [sb(f"c_qs{k}", [P, C, P], F32R) for k in range(2)]
        own = sb("c_own", [P, HG])
        qh = [[sb(f"c_qh{b}_{k}", [P, C, HG, LQ], F32R) for k in range(2)] for b in range(2)]
        kt = [sb(f"c_kt{k}", [P, C, LKE], F32R) for k in range(2)]
        negmax = sb("c_negmax", [P, C])
        total = sb("c_total", [P, C])
        inv = sb("c_inv", [P, C])
        probs = sb("c_probs", [P, C, LK])
        last_p = sb("c_last_p", [P, C, P // C], F32R)
        pt = [sb(f"c_pt{k}", [P, 2, C * P], F32R) for k in range(2)]
        p1 = sb("c_p1", [P, C, P], F32R)
        mix = sb("c_mix", [P, CC, H, B, LQ])
        ot = sb("c_ot", [P, C, P])
        oth = [sb(f"c_oth{k}", [P, C, P], F32R) for k in range(2)]
        xt = [sb(f"c_xt{b}", [P, D]) for b in range(2)]
        xb = sb("c_xb", [P, D])
        x1 = sb("c_x1", [P, D])

        bank_k = [ps(f"c_bank_k{b}") for b in range(2)]
        bank_s = [ps(f"c_bank_s{b}") for b in range(2)]
        bank_t = [ps(f"c_bank_t{b}") for b in range(2)]
        bank_v = [ps(f"c_bank_v{b}") for b in range(2)]

        s_seen = sem("c_s_seen")
        s_wk_in = sem("c_s_wk_in")
        s_w_in = sem("c_s_w_in")
        s_w_hi = sem("c_s_w_hi")
        s_w_split = sem("c_s_w_split")
        s_const = sem("c_s_const")
        s_ctx_in = [sem(f"c_s_ctx_in{j}") for j in range(B)]
        s_q_in = sem("c_s_q_in")
        s_x_in = sem("c_s_x_in")
        s_ct_hi = sem("c_s_ct_hi")
        s_ct_split = sem("c_s_ct_split")
        s_cn_hi = sem("c_s_cn_hi")
        s_cn_split = sem("c_s_cn_split")
        s_sign = sem("c_s_sign")
        s_c1_hi = sem("c_s_c1_hi")
        s_c1_split = sem("c_s_c1_split")
        s_q_hi = sem("c_s_q_hi")
        s_q_split = sem("c_s_q_split")
        s_k = [sem(f"c_s_k{b}") for b in range(2)]
        s_k_hi = sem("c_s_k_hi")
        s_k_split = [sem(f"c_s_k_split{b}") for b in range(2)]
        s_s = [sem(f"c_s_s{b}") for b in range(2)]
        s_max = sem("c_s_max")
        s_exp = [sem(f"c_s_exp{b}") for b in range(2)]
        s_inv = sem("c_s_inv")
        s_norm = sem("c_s_norm")
        s_last = sem("c_s_last")
        s_probs = sem("c_s_probs")
        s_t = [sem(f"c_s_t{b}") for b in range(2)]
        s_t_hi = sem("c_s_t_hi")
        s_t_split = [sem(f"c_s_t_split{b}") for b in range(2)]
        s_v = [sem(f"c_s_v{b}") for b in range(2)]
        s_v_taken = [sem(f"c_s_v_taken{b}") for b in range(2)]
        s_o_hi = sem("c_s_o_hi")
        s_o_split = sem("c_s_o_split")
        s_xb = sem("c_s_xb")
        s_x1 = sem("c_s_x1")
        s_out = sem("c_s_out")

        def v0_output(i):
            return i * (B + 1) - 1

        def v1_project(i):
            if isinstance(i, int) and i == TILES:
                return i * (B + 1) - 1
            return i * (B + 1)

        def v_before(i, j, bank):
            ahead = 1 if bank == 0 or j >= 1 else 0
            if isinstance(i, int) and i == 0:
                return j
            return i * (B + 1) - 1 + j + ahead

        block = ctx.enter_context(nc.Block())

        @block.sync
        def _(sp):
            sp.dma_start(wk32[:], wk_d).then_inc(s_wk_in, 16)
            sp.dma_start(bias[:], bias_d).then_inc(s_wk_in, 16)
            sp.sem_inc(s_out, 16)

            def load(i, j, first=False):
                m = i * B + j
                if not first:
                    wait(sp, s_seen, (s_ct_split, m - 3), (s_cn_split, m - 3), (s_c1_split, m - 3))
                sp.dma_start(ct[j][:], ctx_t_d[m]).then_inc(s_ctx_in[j], 16)
                sp.dma_start(cn[j][:], ctx_d[m, 0:LK - 1].rearrange("(c p) d -> p c d", p=P)).then_inc(s_ctx_in[j], 16)
                sp.dma_start(c1[j][:], ctx_d[m, LK - 1:LK].broadcast_to([P, DC])).then_inc(s_ctx_in[j], 16)

            def load_queries(i):
                sp.dma_start(qt[:], q_d[:, :, bass.ds(i * P, P)]).then_inc(s_q_in, 16)

            def load_x(i):
                sp.dma_start(xt[0][:], x_d[i]).then_inc(s_x_in, 16)

            def store(i):
                wait(sp, s_seen, (s_x1, i + 2))
                sp.dma_start(x1_d[i], x1[:]).then_inc(s_out, 16)

            def tile(i, first=False, last=False):
                if not last:
                    wait(sp, s_seen, (s_q_hi, 2 * i + 2))
                    load_queries(i + 1)
                load(i, 2, first)
                load(i, 3, first)
                if not last:
                    load(i + 1, 0)
                    load(i + 1, 1)
                if not first:
                    store(i - 1)
                    wait(sp, s_seen, (s_xb, i))
                load_x(i)

            load_queries(0)
            load(0, 0, first=True)
            load(0, 1, first=True)
            sp.dma_start(wo32[:], wo_d).then_inc(s_w_in, 16)
            sp.dma_start(wv[:], wv_d).then_inc(s_w_in, 16)
            sp.dma_start(bo[:], bo_d.broadcast_to([P, D])).then_inc(s_w_in, 16)
            tile(0, first=True)
            with sp.Fori(1, TILES - 1) as i:
                tile(i)
            tile(TILES - 1, last=True)
            store(TILES - 1)
            sp.wait_ge(s_out, 16 * TILES + 16)

        @block.gpsimd
        def _(pool):
            nc.gpsimd.memset(ident[:], 0.0).then_inc(s_const, 1)
            pool.wait_ge(s_const, 1)
            nc.gpsimd.affine_select(out=ident[:], in_=ident[:], compare_op=ALU.not_equal, fill=1.0, base=0,
                                    pattern=[[-1, P]], channel_multiplier=1).then_inc(s_const, 1)
            nc.gpsimd.memset(own[:], 1.0).then_inc(s_const, 1)
            pool.wait_ge(s_const, 3)
            nc.gpsimd.affine_select(out=own[:], in_=own[:], compare_op=ALU.is_ge, fill=0.0, base=0,
                                    pattern=[[-DH, HG]], channel_multiplier=1).then_inc(s_const, 1)
            pool.wait_ge(s_const, 4)
            nc.gpsimd.affine_select(out=own[:], in_=own[:], compare_op=ALU.is_ge, fill=0.0, base=DH - 1,
                                    pattern=[[DH, HG]], channel_multiplier=-1).then_inc(s_const, 1)
            for b in range(2):
                for k in range(2):
                    nc.gpsimd.memset(cth[b][k][:, :, LK:LKE].bitcast(F32), 0.0).then_inc(s_const, 1)
            nc.gpsimd.memset(last_p[:].bitcast(F32), 0.0).then_inc(s_const, 1)

            def split_queries(i, first=True):
                wait(pool, s_seen, (s_q_in, (i + 1) * 16))
                if not first:
                    wait(pool, s_seen, (s_q_split, i * 2 * B))
                nc.gpsimd.tensor_copy(qs[0][:], qt[:]).then_inc(s_q_hi, 1)
                pool.wait_ge(s_q_hi, 2 * i + 1)
                nc.gpsimd.tensor_tensor(qs[1][:], qt[:], qs[0][:].bitcast(F32), ALU.subtract).then_inc(s_q_hi, 1)
                wait(pool, s_seen, (s_q_hi, 2 * i + 2))

            def halves_t(i, j):
                b = j % 2
                m = i * B + j
                wait(pool, s_seen, (s_ct_hi, m + 1))
                nc.gpsimd.tensor_tensor(cth[b][1][:, :, 0:LK], ct[j][:], cth[b][0][:, :, 0:LK].bitcast(F32),
                                        ALU.subtract).then_inc(s_ct_split, 1)

            def queries(i, j):
                b = j % 2
                for k in range(2):
                    nc.gpsimd.tensor_tensor(
                        qh[b][k][:],
                        qs[k][:, :, j * LQ:(j + 1) * LQ].bitcast(F32).unsqueeze(2).broadcast_to([P, C, HG, LQ]),
                        own[:].unsqueeze(1).unsqueeze(3).broadcast_to([P, C, HG, LQ]),
                        ALU.mult).then_inc(s_q_split, 1)

            def halves_n(i, j):
                b = j % 2
                m = i * B + j
                pool.wait_ge(s_cn_hi, m + 1)
                nc.gpsimd.tensor_tensor(cnh[b][1][:], cn[j][:], cnh[b][0][:].bitcast(F32),
                                        ALU.subtract).then_inc(s_cn_split, 1)

            def add_bias(i):
                pool.wait_ge(s_w_in, 48)
                pool.wait_ge(s_x_in, (i + 1) * 16)
                pool.wait_ge(s_x1, i + 1)
                nc.gpsimd.tensor_tensor(xb[:], xt[0][:], bo[:], ALU.add).then_inc(s_xb, 1)

            def output(i):
                pool.wait_ge(s_o_hi, i * 2 + 2)
                nc.gpsimd.tensor_tensor(oth[1][:], ot[:], oth[0][:].bitcast(F32), ALU.subtract).then_inc(s_o_split, 1)

            pool.wait_ge(s_const, 10)
            split_queries(0)
            for j in range(2):
                halves_t(0, j)
                queries(0, j)
                halves_n(0, j)

            def tile(i, first=False, last=False):
                for j in range(B):
                    ahead = (i if j + 2 < B else i + 1, (j + 2) % B)
                    if (j > 0 or not first) and (j + 1 < B or not last):
                        halves_n(i if j + 1 < B else i + 1, (j + 1) % B)
                    if j + 2 < B or not last:
                        halves_t(*ahead)
                    if j == 0 and not first:
                        output(i - 1)
                    if j + 2 < B or not last:
                        queries(*ahead)
                    if j == 0 and not first:
                        add_bias(i - 1)
                    if j == 1 and not last:
                        split_queries(i + 1, first=False)

            tile(0, first=True)
            with pool.Fori(1, TILES - 1) as i:
                tile(i)
            tile(TILES - 1, last=True)
            output(TILES - 1)
            add_bias(TILES - 1)

        @block.tensor
        def _(pe):
            pe.wait_ge(s_const, 10)
            pe.wait_ge(s_w_split, 1)

            def keys(i, j, groups):
                b = j % 2
                m = i * B + j
                pe.wait_ge(s_ct_split, m + 1)
                for g in groups:
                    k = g % 2
                    pe.wait_ge(s_k_split[k], 2 * m + g // 2 + 1)
                    for c in range(CC):
                        for n, (a, d) in enumerate(PASSES):
                            last = nc.tensor.matmul(bank_k[k][:, 0:LKE], wk[a][:, c, g * P:(g + 1) * P],
                                                    cth[b][d][:, c, :], start=(c == 0 and n == 0),
                                                    stop=(c == CC - 1 and n == 2))
                    last.then_inc(s_k[k], 1)

            def scores(i, j, groups):
                b = j % 2
                m = i * B + j
                pe.wait_ge(s_q_split, 2 * m + 2)
                for g in groups:
                    k = g % 2
                    pe.wait_ge(s_k_split[k], 2 * m + g // 2 + 2)
                    pe.wait_ge(s_exp[k], 2 * m + g // 2 + 1)
                    for n, (a, d) in enumerate(PASSES):
                        last = nc.tensor.matmul(bank_s[k][:, 0:LKE], qh[b][a][:, g, :, :], kt[d][:, g, :],
                                                start=(n == 0), stop=(n == 2))
                    last.then_inc(s_s[k], 1)

            def turn(i, j, parts):
                m = i * B + j
                pe.wait_ge(s_probs, m + 1)
                for u in parts:
                    n = 3 * j + u
                    k = n % 2
                    pe.wait_ge(s_t_split[k], i * (3 * B // 2) + n // 2 + 1)
                    if u < 2:
                        for g in range(C):
                            last = nc.tensor.transpose(bank_t[k][:, g * P:(g + 1) * P],
                                                       probs[:, g, u * P:(u + 1) * P], ident[:])
                    else:
                        last = nc.tensor.transpose(bank_t[k][:, 0:P], last_p[:].rearrange("p g k -> p (g k)").bitcast(F32),
                                                   ident[:])
                    last.then_inc(s_t[k], 1)

            def sums(i, j, c):
                b = j % 2
                m = i * B + j

                def turned(u):
                    n = 3 * j + u
                    pe.wait_ge(s_t_split[n % 2], i * (3 * B // 2) + n // 2 + 2)

                pe.wait_ge(s_cn_split, m + 1)
                pe.wait_ge(s_v_taken[c], v_before(i, j, c) + 1)
                cols = slice(c * P, (c + 1) * P)
                for u in range(2):
                    turned(u)
                    for n, (a, d) in enumerate(PASSES):
                        nc.tensor.matmul(bank_v[c][:], cnh[b][a][:, u, cols], pt[d][:, u, :],
                                         start=(u == 0 and n == 0), stop=False)

            def sums_last(i, j, c):
                b = j % 2
                m = i * B + j
                n = 3 * j + 2
                pe.wait_ge(s_t_split[n % 2], i * (3 * B // 2) + n // 2 + 2)
                pe.wait_ge(s_c1_split, m + 1)
                cols = slice(c * P, (c + 1) * P)
                nc.tensor.matmul(bank_v[c][:], c1h[b][:, cols], p1[:].rearrange("p g n -> p (g n)"), start=False, stop=True).then_inc(s_v[c], 1)

            def output(i):
                pe.wait_ge(s_w_in, 48)
                for c in range(CC):
                    pe.wait_ge(s_v_taken[c], v0_output(i + 1) + 1)
                for h in range(H):
                    r = DH * (h % HG)
                    for c in range(CC):
                        last = nc.tensor.matmul(bank_v[0][r:r + DH, (h // HG) * P:(h // HG + 1) * P],
                                                wv[:, c, h * DH:(h + 1) * DH], mix[:, c, h, :, :],
                                                start=(c == 0), stop=(c == CC - 1), skip_group_check=True)
                last.then_inc(s_v[0], 1)

            def project(i):
                pe.wait_ge(s_w_split, 2)
                pe.wait_ge(s_o_split, i + 1)
                pe.wait_ge(s_v_taken[1], v1_project(i + 1) + 1)
                for c in range(C):
                    for n, (a, d) in enumerate(PASSES):
                        last = nc.tensor.matmul(bank_v[1][:], oth[a][:, c, :], wo[d][:, c, :],
                                                start=(c == 0 and n == 0), stop=(c == C - 1 and n == 2))
                last.then_inc(s_v[1], 1)

            keys(0, 0, range(C))
            scores(0, 0, range(C))

            def tile(i, first=False, last=False):
                for j in range(B):
                    more = j + 1 < B or not last
                    ni, nj = (i, j + 1) if j + 1 < B else (i + 1, 0)
                    if more:
                        keys(ni, nj, (0, 1))
                    turn(i, j, (0, 1))
                    if more:
                        keys(ni, nj, (2, 3))
                    turn(i, j, (2,))
                    if j == 0 and not first:
                        output(i - 1)
                    if more:
                        scores(ni, nj, (0, 1))
                    if j == 1 and not first:
                        project(i - 1)
                    sums(i, j, 0)
                    if more:
                        scores(ni, nj, (2, 3))
                    sums_last(i, j, 0)
                    sums(i, j, 1)
                    sums_last(i, j, 1)

            tile(0, first=True)
            with pe.Fori(1, TILES - 1) as i:
                tile(i)
            tile(TILES - 1, last=True)
            output(TILES - 1)
            project(TILES - 1)

        @block.scalar
        def _(act):
            act.wait_ge(s_wk_in, 32)
            nc.scalar.activation(wk[0][:], wk32[:], ACT.Copy).then_inc(s_w_hi, 1)
            for k in range(2):
                act.sem_inc(s_exp[k], 1)
                act.sem_inc(s_v_taken[k], 1)

            def context_t(i, j):
                b = j % 2
                act.wait_ge(s_ctx_in[j], (i + 1) * 48)
                nc.scalar.activation(cth[b][0][:, :, 0:LK], ct[j][:], ACT.Copy).then_inc(s_ct_hi, 1)

            def context_n(j):
                b = j % 2
                nc.scalar.activation(cnh[b][0][:], cn[j][:], ACT.Copy).then_inc(s_cn_hi, 1)

            def keys(i, j, groups):
                m = i * B + j
                for g in groups:
                    act.wait_ge(s_k[g % 2], 2 * m + g // 2 + 1)
                    nc.scalar.activation(kt[0][:, g, :], bank_k[g % 2][:, 0:LKE], ACT.Identity,
                                         bias=bias[:, 1, g:g + 1]).then_inc(s_k_hi, 1)

            def exps(i, j, groups):
                m = i * B + j
                for g in groups:
                    act.wait_ge(s_max, 4 * m + g + 1)
                    nc.scalar.activation(probs[:, g, :], bank_s[g % 2][:, 0:LK], ACT.Exp, bias=negmax[:, g:g + 1],
                                         accum_out=total[:, g:g + 1]).then_inc(s_exp[g % 2], 1)

            def turned(i, j):
                for u in range(2):
                    n = 3 * j + u
                    act.wait_ge(s_t[n % 2], i * (3 * B // 2) + n // 2 + 1)
                    nc.scalar.activation(pt[0][:, u, :], bank_t[n % 2][:], ACT.Copy).then_inc(s_t_hi, 1)

            def sums(i, j, c):
                act.wait_ge(s_v[c], v_before(i, j, c) + 1)
                nc.scalar.activation(mix[:, c, :, j, :], bank_v[c][:].rearrange("p (h q) -> p h q", h=H),
                                     ACT.Copy).then_inc(s_v_taken[c], 1)

            def output(i):
                act.wait_ge(s_o_hi, i * 2 + 1)
                nc.scalar.activation(oth[0][:], ot[:], ACT.Copy).then_inc(s_o_hi, 1)

            for j in range(2):
                context_t(0, j)
                context_n(j)
            keys(0, 0, range(C))
            exps(0, 0, range(C))
            act.wait_ge(s_w_in, 48)
            nc.scalar.activation(wo[0][:], wo32[:], ACT.Copy).then_inc(s_w_hi, 1)

            def tile(i, first=False, last=False):
                for j in range(B):
                    more = j + 1 < B or not last
                    ni, nj = (i, j + 1) if j + 1 < B else (i + 1, 0)
                    ahead = (i if j + 2 < B else i + 1, (j + 2) % B)
                    if more:
                        keys(ni, nj, (0, 1))
                    turned(i, j)
                    if more:
                        keys(ni, nj, (2, 3))
                    if j == 0 and not first:
                        output(i - 1)
                    if more and (j > 0 or not first):
                        context_n(nj)
                    if more:
                        exps(ni, nj, (0, 1))
                    if j + 2 < B or not last:
                        context_t(*ahead)
                    if more:
                        exps(ni, nj, (2, 3))
                    sums(i, j, 0)
                    sums(i, j, 1)

            tile(0, first=True)
            with act.Fori(1, TILES - 1) as i:
                tile(i)
            tile(TILES - 1, last=True)
            output(TILES - 1)

        @block.vector
        def _(dve):
            def split_weights(n, w32, lo, hi):
                dve.wait_ge(s_w_hi, n + 1)
                nc.vector.tensor_tensor(lo[:], w32[:], hi[:].bitcast(F32), ALU.subtract).then_inc(s_w_split, 1)

            dve.sem_inc(s_x1, 1)
            split_weights(0, wk32, wk[1], wk[0])
            for k in range(2):
                dve.sem_inc(s_k_split[k], 1)
                dve.sem_inc(s_t_split[k], 1)
            dve.wait_ge(s_const, 10)

            def keys(i, j, groups):
                m = i * B + j
                for g in groups:
                    dve.wait_ge(s_k_hi, 4 * m + g + 1)
                    nc.vector.scalar_tensor_tensor(out=kt[1][:, g, :], in0=bank_k[g % 2][:, 0:LKE],
                                                   scalar=bias[:, 1, g:g + 1], in1=kt[0][:, g, :].bitcast(F32),
                                                   op0=ALU.add, op1=ALU.subtract).then_inc(s_k_split[g % 2], 1)

            def maxima(i, j, groups):
                m = i * B + j
                for g in groups:
                    dve.wait_ge(s_s[g % 2], 2 * m + g // 2 + 1)
                    nc.vector.tensor_reduce(negmax[:, g:g + 1], bank_s[g % 2][:, 0:LK], X, ALU.max,
                                            negate=True).then_inc(s_max, 1)

            def normalise(i, j, pair):
                m = i * B + j
                for k in range(2):
                    dve.wait_ge(s_exp[k], 2 * m + pair + 2)
                both = slice(2 * pair, 2 * pair + 2)
                nc.vector.reciprocal(inv[:, both], total[:, both]).then_inc(s_inv, 1)
                dve.wait_ge(s_inv, 2 * m + pair + 1)
                for g in (2 * pair, 2 * pair + 1):
                    last = nc.vector.tensor_scalar(probs[:, g, :], probs[:, g, :], inv[:, g:g + 1], None, ALU.mult)
                last.then_inc(s_norm, 1)

            def last_halves(i, j):
                m = i * B + j
                dve.wait_ge(s_norm, 2 * m + 2)
                nc.vector.tensor_copy(last_p[:, :, 0:2],
                                      bc_last(probs[:, :, LK - 1], 2)).then_inc(s_last, 1)
                dve.wait_ge(s_last, m + 1)
                nc.vector.tensor_tensor(last_p[:, :, 2], probs[:, :, LK - 1], last_p[:, :, 0].bitcast(F32),
                                        ALU.subtract).then_inc(s_probs, 1)

            def turned(i, j):
                m = i * B + j
                for u in range(2):
                    n = 3 * j + u
                    dve.wait_ge(s_t_hi, 2 * m + u + 1)
                    nc.vector.tensor_tensor(pt[1][:, u, :], bank_t[n % 2][:], pt[0][:, u, :].bitcast(F32),
                                            ALU.subtract).then_inc(s_t_split[n % 2], 1)

            def turned_last(i, j):
                n = 3 * j + 2
                dve.wait_ge(s_t[n % 2], i * (3 * B // 2) + n // 2 + 1)
                nc.vector.tensor_tensor(p1[:], bc_mid(bank_t[n % 2][:, 0:P], C), bc_last(own[:], P),
                                        ALU.mult).then_inc(s_t_split[n % 2], 1)

            def output(i):
                dve.wait_ge(s_v[0], v0_output(i + 1) + 1)
                nc.vector.tensor_tensor(ot[:], bank_v[0][:].rearrange("p (g n) -> p g n", g=C),
                                        bc_last(bias[:, 2, :], P), ALU.add).then_inc(s_o_hi, 1)
                dve.wait_ge(s_o_hi, i * 2 + 1)
                dve.sem_inc(s_v_taken[0], 1)

            def residual(i):
                dve.wait_ge(s_v[1], v1_project(i + 1) + 1)
                dve.wait_ge(s_xb, i + 1)
                dve.wait_ge(s_out, 16 * i + 16)
                nc.vector.tensor_tensor(x1[:], bank_v[1][:], xb[:], ALU.add).then_inc(s_x1, 1)
                dve.wait_ge(s_x1, i + 2)
                dve.sem_inc(s_v_taken[1], 1)

            def last_key_hi(i, j):
                b = j % 2
                m = i * B + j
                dve.wait_ge(s_ctx_in[j], (i + 1) * 48)
                nc.vector.tensor_copy(c1h[b][:], c1[j][:]).then_inc(s_c1_hi, 1)
                dve.wait_ge(s_c1_hi, 2 * m + 1)
                nc.vector.tensor_scalar(c1s[:], c1h[b][:].bitcast(F32), sign[:], None, ALU.mult).then_inc(s_c1_hi, 1)

            def last_key(i, j):
                b = j % 2
                m = i * B + j
                dve.wait_ge(s_c1_hi, 2 * m + 2)
                nc.vector.scalar_tensor_tensor(out=c1h[b][:], in0=c1[j][:], scalar=is_lo[:], in1=c1s[:],
                                               op0=ALU.mult, op1=ALU.add).then_inc(s_c1_split, 1)

            nc.vector.tensor_reduce(is_lo[:], ident[:, 1:P:P // C], X, ALU.add).then_inc(s_sign, 1)
            dve.wait_ge(s_sign, 1)
            nc.vector.tensor_scalar(sign[:], is_lo[:], -2.0, 1.0, ALU.mult, ALU.add).then_inc(s_sign, 1)
            dve.wait_ge(s_sign, 2)
            last_key_hi(0, 0)
            keys(0, 0, range(C))
            maxima(0, 0, range(C))
            normalise(0, 0, 0)
            normalise(0, 0, 1)
            last_halves(0, 0)
            split_weights(1, wo32, wo[1], wo[0])

            def tile(i, first=False, last=False):
                for j in range(B):
                    more = j + 1 < B or not last
                    ni, nj = (i, j + 1) if j + 1 < B else (i + 1, 0)
                    if more:
                        keys(ni, nj, (0, 1))
                    last_key(i, j)
                    turned(i, j)
                    if j == 0 and not first:
                        keys(ni, nj, (2, 3))
                        output(i - 1)
                        maxima(ni, nj, (0, 1))
                    elif more:
                        maxima(ni, nj, (0, 1))
                        keys(ni, nj, (2, 3))
                    turned_last(i, j)
                    if j == 1 and not first:
                        residual(i - 1)
                    if more:
                        maxima(ni, nj, (2, 3))
                        normalise(ni, nj, 0)
                        normalise(ni, nj, 1)
                        last_halves(ni, nj)
                        last_key_hi(ni, nj)

            tile(0, first=True)
            with dve.Fori(1, TILES - 1) as i:
                tile(i)
            tile(TILES - 1, last=True)
            output(TILES - 1)
            residual(TILES - 1)


def attention_phase(nc, tag, layers, scale, w_d, bias_d, bo_d, xn_d, x_d, y_d, routed=None):
    with ExitStack() as ctx:
        sb, ps, sem = alloc(nc, ctx)
        w32 = sb(f"{tag}_w32", [P, C, D])
        w = [[sb(f"{tag}_w{m}_{k}", [P, C, D], F32R) for k in range(2)] for m in range(4)]
        bias_qk = sb(f"{tag}_bias_qk", [P, 2, C])
        bias_v = sb(f"{tag}_bias_v", [P, C])
        bias_q = sb(f"{tag}_bias_q", [P, C])
        bo = sb(f"{tag}_bo", [P, D])
        xn = [[sb(f"{tag}_xn{b}_{k}", [P, C, N], F32R) for k in range(2)] for b in range(2)]
        qt = sb(f"{tag}_qt", [P, C, N])
        kb = sb(f"{tag}_kb", [P, C, SUP * TILE_SEQ, HG, LQ])
        v = sb(f"{tag}_v", [P, SUP, D])
        ex = [sb(f"{tag}_ex{b}", [P, H, LQ]) for b in range(2)]
        negmax = [sb(f"{tag}_negmax{b}", [P, H]) for b in range(2)]
        total = sb(f"{tag}_total", [P, H])
        inv = [sb(f"{tag}_inv{b}", [P, H]) for b in range(2)]
        pt = [sb(f"{tag}_pt{b}", [P, H, P]) for b in range(2)]
        ot = sb(f"{tag}_ot", [P, C, P])
        oth = [[sb(f"{tag}_oth{b}_{k}", [P, C, P], F32R) for k in range(2)] for b in range(2)]
        x = [sb(f"{tag}_x{b}", [P, D]) for b in range(2)]
        y = [sb(f"{tag}_y{b}", [P, D]) for b in range(2)]
        if routed:
            mask_d, wt_d = routed
            mask = sb(f"{tag}_mask", [P, SUP, LQ])
            wt = sb(f"{tag}_wt", [P, SUP])

        w_first = [w32[:], v[:]] + [pt[b][:].rearrange("p h n -> p (h n)").rearrange("p (c d) -> p c d", c=C)
                                    for b in range(2)]

        bank_p = [ps(f"{tag}_bank_p{k}") for k in range(4)]
        bank_s = [ps(f"{tag}_bank_s{k}") for k in range(2)]
        bank_o = [ps(f"{tag}_bank_o{k}") for k in range(2)]

        s_seen = sem(f"{tag}_s_seen")
        s_w_first = [sem(f"{tag}_s_w_first{m}") for m in range(4)]
        s_w_in = sem(f"{tag}_s_w_in")
        s_w_hi = sem(f"{tag}_s_w_hi")
        s_w_split = sem(f"{tag}_s_w_split")
        s_bqk_in = sem(f"{tag}_s_bqk_in")
        s_bvo_in = sem(f"{tag}_s_bvo_in")
        s_bias_q = sem(f"{tag}_s_bias_q")
        s_zero = sem(f"{tag}_s_zero")
        s_xn_in = [sem(f"{tag}_s_xn_in{b}") for b in range(2)]
        s_m_in = sem(f"{tag}_s_m_in")
        s_x_in = [sem(f"{tag}_s_x_in{b}") for b in range(2)]
        s_prod = [sem(f"{tag}_s_prod{k}") for k in range(4)]
        s_taken = [sem(f"{tag}_s_taken{k}") for k in range(4)]
        s_scores = [sem(f"{tag}_s_scores{b}") for b in range(2)]
        s_s_free = [sem(f"{tag}_s_s_free{b}") for b in range(2)]
        s_max = sem(f"{tag}_s_max")
        s_shift = sem(f"{tag}_s_shift")
        s_exp = sem(f"{tag}_s_exp")
        s_total = sem(f"{tag}_s_total")
        s_inv = sem(f"{tag}_s_inv")
        s_norm = sem(f"{tag}_s_norm")
        s_pt = sem(f"{tag}_s_pt")
        s_sums = [sem(f"{tag}_s_sums{b}") for b in range(2)]
        s_o_free = [sem(f"{tag}_s_o_free{b}") for b in range(2)]
        s_o_hi = sem(f"{tag}_s_o_hi")
        s_o_split = sem(f"{tag}_s_o_split")
        s_xb = sem(f"{tag}_s_xb")
        s_y = sem(f"{tag}_s_y")
        s_out = [sem(f"{tag}_s_out{b}") for b in range(2)]

        VALUES, QUERIES, PROJECT, KEYS = range(2, 6)

        def use(i, what, final=False):
            return 4 * i + (VALUES + 1 if final and what == PROJECT else what)

        block = ctx.enter_context(nc.Block())

        def supertiles(eng, layer, body):
            def supertile(e, r, b, role):
                body(e, 2 * r + b, e * SUPERS + 2 * r + b, b, e * (SUPERS // 2) + r, role)

            def run(e, role):
                layer(e)
                with eng.Fori(0, SUPERS // 2 - 1) as r:
                    for b in range(2):
                        supertile(e, r, b, "middle")
                supertile(e, SUPERS // 2 - 1, 0, "before_" + role)
                supertile(e, SUPERS // 2 - 1, 1, role)

            if layers > 1:
                with eng.Fori(0, layers - 1) as e:
                    run(e, "turn")
            run(layers - 1, "end")

        @block.sync
        def _(sp):
            sp.sem_inc(s_y, 2)
            for b in range(2):
                sp.sem_inc(s_out[b], 16)

            def load_w(e, m):
                wait(sp, s_seen, (s_w_split, 4 * e + m))
                sp.dma_start(w32[:], w_d[e, m]).then_inc(s_w_in, 16)

            def load_bias_qk(e):
                sp.dma_start(bias_qk[:], bias_d[e][:, 0:2, :]).then_inc(s_bqk_in, 16)

            def load_bias_vo(e):
                sp.dma_start(bias_v[:], bias_d[e][:, 2, :]).then_inc(s_bvo_in, 16)
                sp.dma_start(bo[:], bo_d[e].broadcast_to([P, D])).then_inc(s_bvo_in, 16)

            def body(e, s, i, b, half, role):
                def load_x(t):
                    wait(sp, s_seen, (s_y, SUP * i + t + 1))
                    sp.dma_start(x[t % 2][:], x_d[s * SUP + t]).then_inc(s_x_in[t % 2], 16)

                def store(t):
                    wait(sp, s_seen, (s_y, SUP * i + t + 3))
                    sp.dma_start(y_d[s * SUP + t], y[t % 2][:]).then_inc(s_out[t % 2], 16)

                if routed:
                    wait(sp, s_seen, (s_y, SUP * i + 2))
                    sp.dma_start(mask[:], mask_d[:, e, bass.ds(s * SUP, SUP), :]).then_inc(s_m_in, 16)
                    sp.dma_start(wt[:], wt_d[:, e, bass.ds(s * SUP, SUP)]).then_inc(s_m_in, 16)
                load_x(0)
                load_x(1)
                if role == "turn":
                    wait(sp, s_seen, (s_taken[3], use(i, VALUES) + 2))
                    load_bias_qk(e + 1)
                    load_w(e + 1, 1)
                    load_w(e + 1, 2)
                store(0)
                load_x(2)
                store(1)
                load_x(3)
                if role == "before_turn":
                    load_w(e + 1, 0)
                if role == "turn":
                    load_w(e + 1, 3)
                store(2)
                store(3)
                if role == "turn":
                    load_bias_vo(e + 1)

            for m in range(4):
                sp.dma_start(w_first[m], w_d[0, m]).then_inc(s_w_first[m], 16)
                if m == 0:
                    load_bias_qk(0)
            load_bias_vo(0)
            supertiles(sp, lambda e: None, body)
            for b in range(2):
                sp.wait_ge(s_out[b], 16 * (layers * SUPERS * SUP // 2) + 16)

        def w_raw(e, m):
            return w_first[m] if isinstance(e, int) and e == 0 else w32[:]

        def w_lo(engine, e, m):
            return engine.tensor_tensor(w[m][1][:], w_raw(e, m), w[m][0][:].bitcast(F32), ALU.subtract)

        @block.gpsimd
        def _(pool):
            nc.gpsimd.memset(kb[:], 0.0).then_inc(s_zero, 1)
            pool.sem_inc(s_o_split, 1)

            def split_o(e):
                wait(pool, s_seen, (s_w_hi, 4 * e + 4), (s_w_split, 4 * e + 3))
                w_lo(nc.gpsimd, e, 3).then_inc(s_w_split, 1)

            for b in range(2):
                wait(pool, s_seen, (s_w_split, 3 + b))
                nc.gpsimd.memset(pt[b][:], 0.0).then_inc(s_zero, 1)

            def body(e, s, i, b, half, role):
                def normalise(t):
                    pool.wait_ge(s_inv, SUP * i + t + 1)
                    nc.gpsimd.tensor_tensor(ex[t % 2][:], ex[t % 2][:], bc_last(inv[t % 2][:], LQ), ALU.mult)\
                        .then_inc(s_norm, 1)

                def output_lo(t):
                    pool.wait_ge(s_o_hi, SUP * i + t + 1)
                    nc.gpsimd.tensor_tensor(oth[t % 2][1][:], ot[:], oth[t % 2][0][:].bitcast(F32),
                                            ALU.subtract).then_inc(s_o_split, 1)

                normalise(0)
                normalise(1)
                normalise(2)
                output_lo(0)
                normalise(3)
                output_lo(1)
                output_lo(2)
                output_lo(3)
                if role == "turn":
                    split_o(e + 1)

            supertiles(pool, lambda e: None, body)

        @block.tensor
        def _(pe):
            def product(k, u, out, pairs):
                pe.wait_ge(s_taken[k], u + 2)
                for c in range(C):
                    for n, (a, d) in enumerate(PASSES):
                        lhs, rhs = pairs(c, a, d)
                        last = nc.tensor.matmul(out, lhs, rhs, start=(c == 0 and n == 0),
                                                stop=(c == C - 1 and n == 2))
                last.then_inc(s_prod[k], 1)

            def turned_product(m, g, b, u):
                product(g, u, bank_p[g][:], lambda c, a, d: (w[m][a][:, c, g * P:(g + 1) * P], xn[b][d][:, c, :]))

            def body(e, s, i, b, half, role):
                end = role == "end"

                def values(t):
                    product(t, use(i, VALUES), bank_p[t][:],
                            lambda c, a, d: (xn[b][a][:, c, t * P:(t + 1) * P], w[2][d][:, c, :]))

                def scores(t):
                    if t == 0:
                        for g in range(C):
                            pe.wait_ge(s_taken[g], use(i, VALUES) + 2)
                    pe.wait_ge(s_s_free[t % 2], (SUP // 2) * i + t // 2 + 1)
                    for q in range(TILE_SEQ):
                        for g in range(C):
                            last = nc.tensor.matmul(
                                bank_s[t % 2][LQ * q:LQ * q + LQ, g * P:(g + 1) * P],
                                qt[:, g, t * P + LQ * q:t * P + LQ * q + LQ], kb[:, g, t * TILE_SEQ + q, :, :],
                                start=True, stop=True, skip_group_check=True)
                    last.then_inc(s_scores[t % 2], 1)

                def sums(t):
                    pe.wait_ge(s_pt, SUP * i + t + 3)
                    pe.wait_ge(s_taken[t], use(i, VALUES) + 3)
                    pe.wait_ge(s_o_free[t % 2], (SUP // 2) * i + t // 2 + 1)
                    for h in range(H):
                        r = DH * (h % HG)
                        last = nc.tensor.matmul(bank_o[t % 2][r:r + DH, (h // HG) * P:(h // HG + 1) * P],
                                                v[:, t, h * DH:(h + 1) * DH], pt[t % 2][:, h, :],
                                                start=True, stop=True, skip_group_check=True)
                    last.then_inc(s_sums[t % 2], 1)

                def project(t):
                    if t == 0:
                        pe.wait_ge(s_w_split, 4 * e + 4)
                    pe.wait_ge(s_o_split, SUP * i + t + 2)
                    product(t, use(i, PROJECT, end), bank_p[t][:],
                            lambda c, a, d: (oth[t % 2][a][:, c, :], w[3][d][:, c, :]))

                def queries(g):
                    if end:
                        return
                    if g == 0:
                        pe.wait_ge(s_xn_in[1 - b], 32 * (half + b) + 32)
                        if role == "turn":
                            pe.wait_ge(s_w_split, 4 * e + 5)
                    turned_product(0, g, 1 - b, use(i, QUERIES))

                def keys(g):
                    if end:
                        return
                    if g == 0 and role == "turn":
                        pe.wait_ge(s_w_split, 4 * e + 6)
                    turned_product(1, g, 1 - b, use(i, KEYS))

                for t in range(SUP):
                    values(t)
                    scores(t)
                queries(0)
                sums(0)
                queries(1)
                sums(1)
                queries(2)
                project(0)
                sums(2)
                queries(3)
                project(1)
                sums(3)
                keys(0)
                project(2)
                keys(1)
                project(3)
                keys(2)
                keys(3)

            pe.wait_ge(s_xn_in[0], 32)
            for m in range(2):
                pe.wait_ge(s_w_split, m + 1)
                for g in range(C):
                    turned_product(m, g, 0, m)
            supertiles(pe, lambda e: wait(pe, s_seen, (s_w_split, 4 * e + 3)), body)

        @block.scalar
        def _(act):
            def load_xn(s, b):
                for k in range(2):
                    act.dma_start(xn[b][k][:].bitcast(F32), xn_d[s, k]).then_inc(s_xn_in[b], 16)

            def w_hi(e, m):
                if isinstance(e, int) and e == 0:
                    act.wait_ge(s_w_first[m], 16)
                else:
                    wait(act, s_seen, (s_w_in, 64 * (e - 1) + 16 * m + 16))
                nc.scalar.activation(w[m][0][:], w_raw(e, m), ACT.Copy).then_inc(s_w_hi, 1)

            def scale_bias(e):
                wait(act, s_seen, (s_bqk_in, 16 * e + 16))
                nc.scalar.activation(bias_q[:], bias_qk[:, 0, :], ACT.Copy, scale=scale).then_inc(s_bias_q, 1)
                wait(act, s_seen, (s_bias_q, e + 1))

            def queries(g, u):
                act.wait_ge(s_prod[g], u + 1)
                nc.scalar.activation(qt[:, g, :], bank_p[g][:], ACT.Identity, bias=bias_q[:, g:g + 1],
                                     scale=scale).then_inc(s_taken[g], 1)

            def keys(g, u):
                act.wait_ge(s_prod[g], u + 1)
                for h in range(HG):
                    r = slice(DH * h, DH * h + DH)
                    last = nc.scalar.activation(kb[r, g, :, h, :],
                                                bank_p[g][r, :].rearrange("p (b k) -> p b k", k=LQ),
                                                ACT.Identity, bias=bias_qk[r, 1, g:g + 1])
                last.then_inc(s_taken[g], 1)

            for k in range(4):
                act.sem_inc(s_taken[k], 2)
            if not routed:
                for b in range(2):
                    act.sem_inc(s_s_free[b], 1)
            load_xn(0, 0)
            w_hi(0, 0)
            scale_bias(0)
            w_hi(0, 1)
            for g in range(C):
                queries(g, 0)
            w_hi(0, 2)
            load_xn(1, 1)
            w_hi(0, 3)
            act.wait_ge(s_zero, 1)
            for g in range(C):
                keys(g, 1)

            def body(e, s, i, b, half, role):
                end = role == "end"

                def exp(t):
                    act.wait_ge(s_shift, SUP * i + t + 1)
                    if not routed:
                        act.sem_inc(s_s_free[t % 2], 1)
                    nc.scalar.activation(ex[t % 2][:], ex[t % 2][:], ACT.Exp).then_inc(s_exp, 1)

                def values(t):
                    act.wait_ge(s_prod[t], use(i, VALUES) + 1)
                    nc.scalar.activation(v[:, t, :], bank_p[t][:], ACT.Copy).then_inc(s_taken[t], 1)

                def output_hi(t):
                    act.wait_ge(s_o_free[t % 2], (SUP // 2) * i + t // 2 + 2)
                    nc.scalar.activation(oth[t % 2][0][:], ot[:], ACT.Copy).then_inc(s_o_hi, 1)

                def next_queries(g):
                    if not end:
                        queries(g, use(i, QUERIES))

                values(0)
                exp(0)
                if role == "turn":
                    w_hi(e + 1, 0)
                    scale_bias(e + 1)
                values(1)
                exp(1)
                values(2)
                values(3)
                if role in ("middle", "before_turn", "turn"):
                    load_xn(s + 2 if role == "middle" else b, b)
                exp(2)
                next_queries(0)
                exp(3)
                output_hi(0)
                next_queries(1)
                if role == "turn":
                    w_hi(e + 1, 1)
                output_hi(1)
                next_queries(2)
                output_hi(2)
                next_queries(3)
                output_hi(3)
                if role == "turn":
                    w_hi(e + 1, 2)
                if not end:
                    for g in range(C):
                        keys(g, use(i, KEYS))
                if role == "turn":
                    w_hi(e + 1, 3)

            supertiles(act, lambda e: None, body)

        @block.vector
        def _(dve):
            for b in range(2):
                dve.sem_inc(s_o_free[b], 1)
                if routed:
                    dve.sem_inc(s_s_free[b], 1)
            dve.sem_inc(s_pt, 2)

            def split(e, m):
                dve.wait_ge(s_w_hi, 4 * e + m + 1)
                w_lo(nc.vector, e, m).then_inc(s_w_split, 1)

            for m in range(4):
                split(0, m)
            dve.wait_ge(s_zero, 3)

            def layer(e):
                wait(dve, s_seen, (s_bvo_in, 32 * e + 32))

            def body(e, s, i, b, half, role):
                end = role == "end"

                def shift(t):
                    bank = bank_s[t % 2][:].rearrange("p (h k) -> p h k", h=H)
                    dve.wait_ge(s_scores[t % 2], (SUP // 2) * i + t // 2 + 1)
                    dve.wait_ge(s_pt, SUP * i + t + 1)
                    if routed:
                        if t == 0:
                            dve.wait_ge(s_m_in, 32 * i + 32)
                        nc.vector.tensor_tensor(ex[t % 2][:], bank, bc_mid(mask[:, t, :], H), ALU.add)\
                            .then_inc(s_s_free[t % 2], 1)
                        dve.wait_ge(s_s_free[t % 2], (SUP // 2) * i + t // 2 + 2)
                        bank = ex[t % 2][:]
                    nc.vector.tensor_reduce(negmax[t % 2][:], bank, X, ALU.max, negate=True).then_inc(s_max, 1)
                    dve.wait_ge(s_max, SUP * i + t + 1)
                    nc.vector.tensor_tensor(ex[t % 2][:], bank, bc_last(negmax[t % 2][:], LQ), ALU.add).then_inc(s_shift, 1)

                def total_of(t):
                    dve.wait_ge(s_exp, SUP * i + t + 1)
                    nc.vector.tensor_reduce(total[:], ex[t % 2][:], X, ALU.add).then_inc(s_total, 1)
                    dve.wait_ge(s_total, SUP * i + t + 1)
                    nc.vector.reciprocal(inv[t % 2][:], total[:]).then_inc(s_inv, 1)

                def turn(t):
                    dve.wait_ge(s_norm, SUP * i + t + 1)
                    for q in range(TILE_SEQ):
                        r = slice(LQ * q, LQ * q + LQ)
                        last = nc.vector.transpose(pt[t % 2][r, :, r], ex[t % 2][r, :, :])
                    last.then_inc(s_pt, 1)

                def output(t):
                    dve.wait_ge(s_sums[t % 2], (SUP // 2) * i + t // 2 + 1)
                    dve.wait_ge(s_o_split, SUP * i + t + 1)
                    nc.vector.tensor_tensor(ot[:], bank_o[t % 2][:].rearrange("p (g n) -> p g n", g=C),
                                            bc_last(bias_v[:], P), ALU.add).then_inc(s_o_free[t % 2], 1)

                def add_bias(t):
                    dve.wait_ge(s_x_in[t % 2], 16 * ((SUP // 2) * i + t // 2) + 16)
                    if routed:
                        nc.vector.scalar_tensor_tensor(out=x[t % 2][:], in0=bo[:], scalar=wt[:, t:t + 1],
                                                       in1=x[t % 2][:], op0=ALU.mult, op1=ALU.add).then_inc(s_xb, 1)
                    else:
                        nc.vector.tensor_tensor(x[t % 2][:], x[t % 2][:], bo[:], ALU.add).then_inc(s_xb, 1)

                def residual(t):
                    u = use(i, PROJECT, end)
                    dve.wait_ge(s_prod[t], u + 1)
                    dve.wait_ge(s_xb, SUP * i + t + 1)
                    dve.wait_ge(s_out[t % 2], 16 * ((SUP // 2) * i + t // 2) + 16)
                    if routed:
                        nc.vector.scalar_tensor_tensor(out=y[t % 2][:], in0=bank_p[t][:], scalar=wt[:, t:t + 1],
                                                       in1=x[t % 2][:], op0=ALU.mult, op1=ALU.add).then_inc(s_y, 1)
                    else:
                        nc.vector.tensor_tensor(y[t % 2][:], bank_p[t][:], x[t % 2][:], ALU.add).then_inc(s_y, 1)
                    dve.wait_ge(s_y, SUP * i + t + 3)
                    dve.sem_inc(s_taken[t], 1)

                shift(0)
                total_of(0)
                if role == "turn":
                    split(e + 1, 0)
                shift(1)
                turn(0)
                total_of(1)
                shift(2)
                turn(1)
                total_of(2)
                shift(3)
                output(0)
                turn(2)
                total_of(3)
                output(1)
                add_bias(0)
                add_bias(1)
                turn(3)
                if role == "turn":
                    split(e + 1, 1)
                residual(0)
                output(2)
                residual(1)
                output(3)
                if role == "turn":
                    split(e + 1, 2)
                add_bias(2)
                residual(2)
                add_bias(3)
                residual(3)

            supertiles(dve, layer, body)


def router_phase(nc, logit_d, rb_d, mask_d, wt_d):
    ALL = TILES * EXPERTS
    with ExitStack() as ctx:
        sb, ps, sem = alloc(nc, ctx)
        logit_t = sb("r_logit_t", [EXPERTS, TOK])
        logit = sb("r_logit", [P, TILES, EXPERTS])
        rb = sb("r_rb", [P, EXPERTS])
        top = sb("r_top", [P, TILES])
        total = sb("r_total", [P, TILES])
        inv = sb("r_inv", [P, TILES])
        prob = sb("r_prob", [P, TILES, EXPERTS])
        above = sb("r_above", [P, TILES, EXPERTS, EXPERTS])
        tied = sb("r_tied", [P, TILES, EXPERTS, EXPERTS])
        before = sb("r_before", [P, EXPERTS, EXPERTS])
        rank = sb("r_rank", [P, TILES, EXPERTS])
        member = sb("r_member", [P, TILES, EXPERTS])
        wt = sb("r_wt", [P, EXPERTS, TILES])
        mask = sb("r_mask", [P, EXPERTS, TILES, LQ])
        ident = sb("r_ident", [P, P])
        place = sb("r_place", [P, LQ])
        own = sb("r_own", [P, TILE_SEQ])
        same = sb("r_same", [P, P], F32R)
        spread = [sb(f"r_spread{b}", [P, SUP, EXPERTS, LQ], F32R) for b in range(2)]
        bank = [ps(f"r_bank{b}") for b in range(2)]

        s_in = sem("r_s_in")
        s_logit = sem("r_s_logit")
        s_const = sem("r_s_const")
        s_dve = sem("r_s_dve")
        s_exp = sem("r_s_exp")
        s_spread = sem("r_s_spread")
        s_mask = sem("r_s_mask")
        s_taken = sem("r_s_taken")
        s_out = sem("r_s_out")

        block = ctx.enter_context(nc.Block())
        steps = [0]

        @block.sync
        def _(sp):
            sp.dma_start(logit_t[:], logit_d).then_inc(s_in, 16)
            sp.dma_start(rb[:], rb_d).then_inc(s_in, 16)
            sp.wait_ge(s_taken, SUPERS)
            sp.dma_start(mask_d, mask[:]).then_inc(s_out, 16)
            sp.dma_start(wt_d, wt[:]).then_inc(s_out, 16)
            sp.wait_ge(s_out, 32)

        @block.gpsimd
        def _(pool):
            nc.gpsimd.memset(ident[:], 0.0).then_inc(s_const, 1)
            nc.gpsimd.memset(own[:], 1.0).then_inc(s_const, 1)
            nc.gpsimd.memset(before[:], 0.0).then_inc(s_const, 1)
            pool.wait_ge(s_const, 3)
            nc.gpsimd.affine_select(out=ident[:], in_=ident[:], compare_op=ALU.not_equal, fill=1.0, base=0,
                                    pattern=[[-1, P]], channel_multiplier=1).then_inc(s_const, 1)
            nc.gpsimd.affine_select(out=own[:], in_=own[:], compare_op=ALU.is_ge, fill=0.0, base=0,
                                    pattern=[[-LQ, TILE_SEQ]], channel_multiplier=1).then_inc(s_const, 1)
            for e in range(1, EXPERTS):
                nc.gpsimd.memset(before[:, e, 0:e], 1.0).then_inc(s_const, 1)
            pool.wait_ge(s_const, 5 + EXPERTS - 1)
            nc.gpsimd.affine_select(out=own[:], in_=own[:], compare_op=ALU.is_ge, fill=0.0, base=LQ - 1,
                                    pattern=[[LQ, TILE_SEQ]], channel_multiplier=-1).then_inc(s_const, 1)

        @block.scalar
        def _(act):
            act.wait_ge(s_dve, 3)
            nc.scalar.activation(prob[:], logit[:], ACT.Exp).then_inc(s_exp, 1)

        @block.vector
        def _(dve):
            def step(ins):
                steps[0] += 1
                ins.then_inc(s_dve, 1)
                dve.wait_ge(s_dve, steps[0])

            dve.wait_ge(s_in, 32)
            dve.wait_ge(s_logit, 1)
            step(nc.vector.tensor_tensor(logit[:], bank[0][:, 0:ALL].rearrange("p (t e) -> p t e", e=EXPERTS),
                                         bc_mid(rb[:], TILES), ALU.add))
            step(nc.vector.tensor_reduce(top[:], logit[:], X, ALU.max, negate=True))
            step(nc.vector.tensor_tensor(logit[:], logit[:], bc_last(top[:], EXPERTS), ALU.add))
            dve.wait_ge(s_exp, 1)
            step(nc.vector.tensor_reduce(total[:], prob[:], X, ALU.add))
            step(nc.vector.reciprocal(inv[:], total[:]))
            step(nc.vector.tensor_tensor(prob[:], prob[:], bc_last(inv[:], EXPERTS), ALU.mult))
            wide = [P, TILES, EXPERTS, EXPERTS]
            other = prob[:].unsqueeze(2).broadcast_to(wide)
            mine = prob[:].unsqueeze(3).broadcast_to(wide)
            step(nc.vector.tensor_tensor(above[:], other, mine, ALU.is_gt))
            step(nc.vector.tensor_tensor(tied[:], other, mine, ALU.is_equal))
            dve.wait_ge(s_const, 6 + EXPERTS - 1)
            step(nc.vector.tensor_tensor(tied[:], tied[:], before[:].unsqueeze(1).broadcast_to(wide), ALU.mult))
            step(nc.vector.tensor_tensor(above[:], above[:], tied[:], ALU.add))
            step(nc.vector.tensor_reduce(rank[:], above[:], X, ALU.add))
            step(nc.vector.tensor_scalar(member[:], rank[:], 1.5, None, ALU.is_lt))
            step(nc.vector.tensor_tensor(wt[:].rearrange("p e t -> p t e"), prob[:], member[:], ALU.mult))
            step(nc.vector.tensor_tensor(place[:], ident[:, 0:LQ], ident[:, LQ:2 * LQ], ALU.add))
            step(nc.vector.tensor_tensor(place[:], place[:], ident[:, 2 * LQ:3 * LQ], ALU.add))
            step(nc.vector.tensor_tensor(place[:], place[:], ident[:, 3 * LQ:4 * LQ], ALU.add))
            step(nc.vector.tensor_copy(same[:].rearrange("p (b q) -> p b q", b=TILE_SEQ), bc_last(own[:], LQ)))
            for s in range(SUPERS):
                if s >= 2:
                    dve.wait_ge(s_mask, s - 1)
                nc.vector.tensor_tensor(
                    spread[s % 2][:].rearrange("p t e q -> p (t e) q"),
                    bc_last(member[:, s * SUP:(s + 1) * SUP, :].rearrange("p t e -> p (t e)"), LQ),
                    bc_mid(place[:], SUP * EXPERTS), ALU.mult).then_inc(s_spread, 1)
                dve.wait_ge(s_mask, s + 1)
                nc.vector.tensor_scalar(mask[:, :, s * SUP:(s + 1) * SUP, :].rearrange("p e t q -> p t e q"),
                                        bank[s % 2][:].rearrange("p (t e q) -> p t e q", t=SUP, e=EXPERTS),
                                        -1.0, MASKED, ALU.add, ALU.mult).then_inc(s_taken, 1)

        @block.tensor
        def _(pe):
            pe.wait_ge(s_in, 32)
            pe.wait_ge(s_const, 6 + EXPERTS - 1)
            for t in range(TILES):
                last = nc.tensor.transpose(bank[0][:, t * EXPERTS:(t + 1) * EXPERTS], logit_t[:, t * P:(t + 1) * P],
                                           ident[0:EXPERTS, 0:EXPERTS])
            last.then_inc(s_logit, 1)
            for s in range(SUPERS):
                pe.wait_ge(s_spread, s + 1)
                if s >= 2:
                    pe.wait_ge(s_taken, s - 1)
                nc.tensor.matmul(bank[s % 2][:], same[:], spread[s % 2][:].rearrange("p t e q -> p (t e q)"),
                                 start=True, stop=True).then_inc(s_mask, 1)


def program(nc, x, ctx, ctx_t, w, w_k, w_v, bias_p, bias_o, r_w, r_b, out):
    x_t = x.rearrange("(t p) d -> t p d", p=P)
    out_t = out.rearrange("(t p) d -> t p d", p=P)
    q_d = nc.dram_tensor("q_scratch", (P, C, TOK), F32).ap()
    xn_d = nc.dram_tensor("xn_scratch", (SUPERS, 2, P, C, N), F32).ap()
    x1_d = nc.dram_tensor("x1_scratch", (TILES, P, D), F32).ap()
    xn2_d = nc.dram_tensor("xn2_scratch", (SUPERS, 2, P, C, N), F32).ap()
    logit_d = nc.dram_tensor("logit_scratch", (EXPERTS, TOK), F32).ap()
    mask_d = nc.dram_tensor("mask_scratch", (P, EXPERTS, TILES, LQ), F32).ap()
    wt_d = nc.dram_tensor("wt_scratch", (P, EXPERTS, TILES), F32).ap()
    norm_phase(nc, "n0", x_t, None, q=(w[0], bias_p[0, :, 0], q_d))
    cross_phase(nc, x_t, q_d, ctx, ctx_t, w_k, w_v, w[1], bias_p[0], bias_o[0:1], x1_d)
    norm_phase(nc, "n1", x1_d, xn_d)
    attention_phase(nc, "a", 1, SELF_SCALE, w[2:6].rearrange("(l m) p c n -> l m p c n", m=4), bias_p[1:2],
                    bias_o[1:2].unsqueeze(1), xn_d, x1_d, out_t)
    norm_phase(nc, "n2", out_t, xn2_d, router=(r_w, logit_d))
    router_phase(nc, logit_d, r_b.broadcast_to([P, EXPERTS]), mask_d, wt_d)
    attention_phase(nc, "e", EXPERTS, EXPERT_SCALE, w[6:6 + 4 * EXPERTS].rearrange("(l m) p c n -> l m p c n", m=4),
                    bias_p[2:2 + EXPERTS], bias_o[2:2 + EXPERTS].unsqueeze(1), xn2_d, out_t, out_t,
                    routed=(mask_d, wt_d))


def kernel(**inputs):
    import numpy as np
    import concourse.bacc as bacc
    from concourse.bass_utils import run_bass_kernel_spmd as run

    a = {k: np.ascontiguousarray(v) for k, v in inputs.items()}

    def rows(w):
        return np.ascontiguousarray(w.reshape(-1, P, w.shape[-1]).transpose(1, 0, 2))

    def cols(*biases):
        return np.ascontiguousarray(np.stack([b.reshape(C, P).T for b in biases], axis=1))

    qkv, bqkv = a["L0_attn_w_qkv"], a["L0_attn_b_qkv"]
    w = [a["L0_xattn_Wq"], a["L0_xattn_Wo"]]
    w += [qkv[:, k * D:(k + 1) * D] for k in range(3)] + [a["L0_attn_w_proj"]]
    bias_p = [cols(a["L0_xattn_bq"], a["L0_xattn_bk"], a["L0_xattn_bv"]),
              cols(*[bqkv[k * D:(k + 1) * D] for k in range(3)])]
    bias_o = [a["L0_xattn_bo"], a["L0_attn_b_proj"]]
    for e in range(EXPERTS):
        w += [a[f"L0_ffn_w{k}"][e] for k in "qkvo"]
        bias_p.append(cols(*[a[f"L0_ffn_b{k}"][e] for k in "qkv"]))
        bias_o.append(a["L0_ffn_bo"][e])
    arrays = {
        "x": a["x"].reshape(TOK, D),
        "ctx": a["ctx_512"],
        "ctx_t": np.ascontiguousarray(a["ctx_512"].reshape(BATCH, LK, CC, P).transpose(0, 3, 2, 1)),
        "w": np.stack([rows(m) for m in w]),
        "w_k": rows(a["L0_xattn_Wk"]),
        "w_v": rows(a["L0_xattn_Wv"]),
        "bias_p": np.stack(bias_p),
        "bias_o": np.stack(bias_o),
        "r_w": rows(a["L0_ffn_router_w"]),
        "r_b": a["L0_ffn_router_b"].reshape(1, EXPERTS),
    }
    nc = bacc.Bacc("TRN2", target_bir_lowering=False, num_devices=1)
    args = [nc.dram_tensor(k, v.shape, F32, kind="ExternalInput").ap() for k, v in arrays.items()]
    args.append(nc.dram_tensor("out", (TOK, D), F32, kind="ExternalOutput").ap())
    program(nc, *args)
    r = run(nc, [arrays], core_ids=[0])
    return r.results[0]["out"].reshape(BATCH, LQ, D)
```
